# Optimizing a Trainium2 kernel written in Bass

```python
import numpy as np
import jax
import jax.numpy as jnp

def _softmax(x, axis=-1):
    return jax.nn.softmax(x, axis=axis)

def _gelu(x):
    return jax.nn.gelu(x, approximate=True)

def _silu(x):
    return jax.nn.silu(x)

def _sigmoid(x):
    return jax.nn.sigmoid(x)

def _layernorm(x, axis=-1, eps=1e-05):
    m = jnp.mean(x, axis=axis, keepdims=True)
    v = jnp.var(x, axis=axis, keepdims=True)
    return (x - m) / jnp.sqrt(v + eps)

def _scatter_add(tgt, idx, src, axis=0):
    return tgt.at[idx].add(src)

def _segment_sum(src, seg, n):
    return jax.ops.segment_sum(src, seg, n)
kernel_name = 'mk_decoder_preln_d1_seqx_r8_98e28b'

def setup_inputs(seed: int=0):
    np.random.seed(seed)
    _w = jnp.asarray

    def _rec_inputs():
        import jax
        import jax.numpy as jnp
        _rk = jax.random.key(seed)
        x = -0.0005207 + 1.001 * jax.random.normal(jax.random.fold_in(_rk, 1), (64, 128, 128), jnp.float32)
        _lenS = 128 - jax.random.randint(jax.random.fold_in(_rk, 7), (64,), 0, max(1, 128 // 4) + 1, jnp.int32)
        _lenS2 = 77 - jax.random.randint(jax.random.fold_in(_rk, 8), (64,), 0, max(1, 77 // 4) + 1, jnp.int32)
        _ctx_1024P = jax.random.normal(jax.random.fold_in(_rk, 11), (64, 16, 128), jnp.float32)
        _ctx_1024c = jax.random.dirichlet(jax.random.fold_in(_rk, 511), 0.3 * jnp.ones((16,), jnp.float32), (64, 77))
        _ctx_1024t = jnp.einsum('bsk,bkd->bsd', _ctx_1024c, _ctx_1024P)
        _ctx_1024t = _ctx_1024t * jax.lax.rsqrt(jnp.mean(jnp.square(_ctx_1024t)) + 1e-12) * 0.953939
        ctx_1024 = -0.000514642 + 1.00011 * (_ctx_1024t + 0.3 * jax.random.normal(jax.random.fold_in(_rk, 611), (64, 77, 128), jnp.float32))
        return (x, ctx_1024)
    x, ctx_1024 = _rec_inputs()

    def _L0_attn_setup():
        import jax, jax.numpy as jnp
        import numpy as np
        N_HEAD = 16

        def _rope_cache(T, head_dim):
            half = head_dim // 2
            inv_freq = 1.0 / 10000.0 ** (jnp.arange(half, dtype=jnp.float32) / half)
            t = jnp.arange(T, dtype=jnp.float32)
            freqs = jnp.einsum('i,j->ij', t, inv_freq)
            cos = jnp.repeat(jnp.cos(freqs), 2, axis=-1)
            sin = jnp.repeat(jnp.sin(freqs), 2, axis=-1)
            return (cos, sin)

        def _apply_rope(x, cos, sin):
            x1 = x[..., ::2]
            x2 = x[..., 1::2]
            x_rot = jnp.stack([-x2, x1], axis=-1).reshape(x.shape)
            return x * cos[None, None] + x_rot * sin[None, None]
        key = jax.random.key(seed)
        k1, k2, k3 = jax.random.split(key, 3)
        B, T, C = (2, 256, 128)
        x = jax.random.normal(k1, (B, T, C), dtype=jnp.float32)
        Wqkv = jax.random.normal(k2, (C, 3 * C), dtype=jnp.float32) * 0.02
        Wo = jax.random.normal(k3, (C, C), dtype=jnp.float32) * 0.02
        bo = jnp.zeros((C,), dtype=jnp.float32)
        return {'x': x, 'Wqkv': Wqkv, 'Wo': Wo, 'bo': bo}
    _L0_attn_all = _L0_attn_setup()
    _L0_attn_in = {k: v for k, v in _L0_attn_all.items() if k in ('Wqkv', 'Wo', 'bo')}
    del _L0_attn_all

    def _L0_xattn_setup():
        import jax, jax.numpy as jnp
        import numpy as np
        import math
        B, S, D, H = (1, 256, 128, 16)
        DK = D // H
        DH = 64
        LOG_T_MIN = math.log(0.1)
        LOG_T_MAX = math.log(10.0)

        def _linear(x, W, b):
            return x @ W.T + b
        key = jax.random.key(seed)
        ks = jax.random.split(key, 20)
        p = 0.02
        return {'query': jax.random.normal(ks[0], (B, S, D), jnp.float32), 'key': jax.random.normal(ks[1], (B, S, D), jnp.float32), 'value': jax.random.normal(ks[2], (B, S, D), jnp.float32), 'Wq': jax.random.normal(ks[3], (D, D), jnp.float32) * p, 'bq': jax.random.normal(ks[4], (D,), jnp.float32) * p, 'Wk': jax.random.normal(ks[5], (D, D), jnp.float32) * p, 'bk': jax.random.normal(ks[6], (D,), jnp.float32) * p, 'Wv': jax.random.normal(ks[7], (D, D), jnp.float32) * p, 'bv': jax.random.normal(ks[8], (D,), jnp.float32) * p, 'Wo': jax.random.normal(ks[9], (D, D), jnp.float32) * p, 'bo': jax.random.normal(ks[10], (D,), jnp.float32) * p, 'w1': jax.random.normal(ks[11], (DH, 3), jnp.float32) * 0.3, 'b1': jax.random.normal(ks[12], (DH,), jnp.float32) * 0.1, 'w2': jax.random.normal(ks[13], (DH, DH), jnp.float32) * 0.1, 'b2': jax.random.normal(ks[14], (DH,), jnp.float32) * 0.1, 'w3': jax.random.normal(ks[15], (1, DH), jnp.float32) * 0.1, 'b3': jnp.full((1,), (LOG_T_MIN + LOG_T_MAX) / 2, jnp.float32)}
    _L0_xattn_all = _L0_xattn_setup()
    _L0_xattn_in = {k: v for k, v in _L0_xattn_all.items() if k in ('Wq', 'bq', 'Wk', 'bk', 'Wv', 'bv', 'Wo', 'bo', 'w1', 'b1', 'w2', 'b2', 'w3', 'b3')}
    del _L0_xattn_all

    def _L0_ffn_setup():
        import jax, jax.numpy as jnp
        import numpy as np
        E = 8
        TOPK = 2
        SCALE = 2.0
        key = jax.random.key(seed)
        ks = jax.random.split(key, 12)
        B, S, D, F, R = (2, 64, 128, 512, 16)
        w = lambda k, shp: jax.random.normal(k, shp, dtype=jnp.float32) * 0.02
        return {'hidden_states': jax.random.normal(ks[0], (B, S, D), dtype=jnp.float32), 'gate_w': w(ks[1], (E, D)), 'w_gate': w(ks[2], (F, D)), 'w_up': w(ks[3], (F, D)), 'w_down': w(ks[4], (D, F)), 'A1': w(ks[5], (E, R, D)), 'B1': w(ks[6], (E, F, R)), 'A3': w(ks[7], (E, R, D)), 'B3': w(ks[8], (E, F, R)), 'A2': w(ks[9], (E, R, F)), 'B2': w(ks[10], (E, D, R))}
    _L0_ffn_all = _L0_ffn_setup()
    _L0_ffn_in = {k: v for k, v in _L0_ffn_all.items() if k in ('gate_w', 'w_gate', 'w_up', 'w_down', 'A1', 'B1', 'A3', 'B3', 'A2', 'B2')}
    del _L0_ffn_all
    return {'x': x, 'ctx_1024': ctx_1024, 'L0_attn_Wqkv': _L0_attn_in['Wqkv'], 'L0_attn_Wo': _L0_attn_in['Wo'], 'L0_attn_bo': _L0_attn_in['bo'], 'L0_xattn_Wq': _L0_xattn_in['Wq'], 'L0_xattn_bq': _L0_xattn_in['bq'], 'L0_xattn_Wk': _L0_xattn_in['Wk'], 'L0_xattn_bk': _L0_xattn_in['bk'], 'L0_xattn_Wv': _L0_xattn_in['Wv'], 'L0_xattn_bv': _L0_xattn_in['bv'], 'L0_xattn_Wo': _L0_xattn_in['Wo'], 'L0_xattn_bo': _L0_xattn_in['bo'], 'L0_xattn_w1': _L0_xattn_in['w1'], 'L0_xattn_b1': _L0_xattn_in['b1'], 'L0_xattn_w2': _L0_xattn_in['w2'], 'L0_xattn_b2': _L0_xattn_in['b2'], 'L0_xattn_w3': _L0_xattn_in['w3'], 'L0_xattn_b3': _L0_xattn_in['b3'], 'L0_ffn_gate_w': _L0_ffn_in['gate_w'], 'L0_ffn_w_gate': _L0_ffn_in['w_gate'], 'L0_ffn_w_up': _L0_ffn_in['w_up'], 'L0_ffn_w_down': _L0_ffn_in['w_down'], 'L0_ffn_A1': _L0_ffn_in['A1'], 'L0_ffn_B1': _L0_ffn_in['B1'], 'L0_ffn_A3': _L0_ffn_in['A3'], 'L0_ffn_B3': _L0_ffn_in['B3'], 'L0_ffn_A2': _L0_ffn_in['A2'], 'L0_ffn_B2': _L0_ffn_in['B2']}

def reference(x, ctx_1024, L0_attn_Wqkv, L0_attn_Wo, L0_attn_bo, L0_xattn_Wq, L0_xattn_bq, L0_xattn_Wk, L0_xattn_bk, L0_xattn_Wv, L0_xattn_bv, L0_xattn_Wo, L0_xattn_bo, L0_xattn_w1, L0_xattn_b1, L0_xattn_w2, L0_xattn_b2, L0_xattn_w3, L0_xattn_b3, L0_ffn_gate_w, L0_ffn_w_gate, L0_ffn_w_up, L0_ffn_w_down, L0_ffn_A1, L0_ffn_B1, L0_ffn_A3, L0_ffn_B3, L0_ffn_A2, L0_ffn_B2):
    import jax
    import jax.numpy as jnp

    def _L0_attn_ref(x, Wqkv, Wo, bo):
        import jax, jax.numpy as jnp
        import numpy as np
        N_HEAD = 16

        def _rope_cache(T, head_dim):
            half = head_dim // 2
            inv_freq = 1.0 / 10000.0 ** (jnp.arange(half, dtype=jnp.float32) / half)
            t = jnp.arange(T, dtype=jnp.float32)
            freqs = jnp.einsum('i,j->ij', t, inv_freq)
            cos = jnp.repeat(jnp.cos(freqs), 2, axis=-1)
            sin = jnp.repeat(jnp.sin(freqs), 2, axis=-1)
            return (cos, sin)

        def _apply_rope(x, cos, sin):
            x1 = x[..., ::2]
            x2 = x[..., 1::2]
            x_rot = jnp.stack([-x2, x1], axis=-1).reshape(x.shape)
            return x * cos[None, None] + x_rot * sin[None, None]
        B, T, C = x.shape
        H = N_HEAD
        D = C // H
        scale = D ** (-0.5)
        qkv = x @ Wqkv
        qkv = qkv.reshape(B, T, 3, H, D).transpose(2, 0, 3, 1, 4)
        q, k, v = (qkv[0], qkv[1], qkv[2])
        cos, sin = _rope_cache(T, D)
        q = _apply_rope(q, cos, sin)
        k = _apply_rope(k, cos, sin)
        att = jnp.einsum('bhqd,bhkd->bhqk', q, k) * scale
        causal = jnp.tril(jnp.ones((T, T), dtype=bool))
        att = jnp.where(causal[None, None], att, -jnp.inf)
        att = jax.nn.softmax(att, axis=-1)
        out = jnp.einsum('bhqk,bhkd->bhqd', att, v)
        out = out.transpose(0, 2, 1, 3).reshape(B, T, C)
        return out @ Wo + bo

    def _L0_xattn_ref(query, key, value, Wq, bq, Wk, bk, Wv, bv, Wo, bo, w1, b1, w2, b2, w3, b3):
        import jax, jax.numpy as jnp
        import numpy as np
        import math
        B, S, D, H = (1, 256, 128, 16)
        DK = D // H
        DH = 64
        LOG_T_MIN = math.log(0.1)
        LOG_T_MAX = math.log(10.0)

        def _linear(x, W, b):
            return x @ W.T + b
        b, sq, d = query.shape
        sk = key.shape[1]
        h, dk = (H, DK)
        Q = _linear(query, Wq, bq).reshape(b, sq, h, dk).transpose(0, 2, 1, 3)
        K = _linear(key, Wk, bk).reshape(b, sk, h, dk).transpose(0, 2, 1, 3)
        V = _linear(value, Wv, bv).reshape(b, sk, h, dk).transpose(0, 2, 1, 3)
        qk = jnp.einsum('bhqd,bhkd->bhqk', Q, K)
        scores = qk / math.sqrt(dk)
        mean_sim = scores.mean(axis=(-2, -1))
        max_sim = scores.max(axis=-1).mean(axis=-1)
        probs = jax.nn.softmax(scores, axis=-1)
        entropy_proxy = jnp.var(probs, axis=-1, ddof=1).mean(axis=-1)
        feats = jnp.stack([mean_sim, max_sim, entropy_proxy], axis=-1)
        hidden = jax.nn.gelu(_linear(feats, w1, b1), approximate=False)
        hidden = jax.nn.gelu(_linear(hidden, w2, b2), approximate=False)
        log_t = jnp.clip(_linear(hidden, w3, b3), LOG_T_MIN, LOG_T_MAX)
        t = jnp.exp(log_t)[..., None]
        attn_scores = qk / (2.0 * t)
        attn = jax.nn.softmax(attn_scores, axis=-1)
        attn = jnp.nan_to_num(attn, nan=0.0)
        out = jnp.einsum('bhqk,bhkd->bhqd', attn, V)
        out = out.transpose(0, 2, 1, 3).reshape(b, sq, d)
        return _linear(out, Wo, bo)

    def _L0_ffn_ref(hidden_states, gate_w, w_gate, w_up, w_down, A1, B1, A3, B3, A2, B2):
        import jax, jax.numpy as jnp
        import numpy as np
        E = 8
        TOPK = 2
        SCALE = 2.0
        B, S, D = hidden_states.shape
        x = hidden_states.reshape(-1, D)
        N = x.shape[0]
        probs = jax.nn.softmax(x @ gate_w.T, axis=-1)
        vals, idx = jax.lax.top_k(probs, TOPK)
        rw = vals / jnp.sum(vals, axis=-1, keepdims=True)
        weight = jnp.zeros((N, E), x.dtype).at[jnp.arange(N)[:, None], idx].add(rw)
        common_w1 = x @ w_gate.T
        common_w3 = x @ w_up.T
        d1 = jnp.einsum('enr,efr->enf', jnp.einsum('nd,erd->enr', x, A1), B1) * SCALE
        d3 = jnp.einsum('enr,efr->enf', jnp.einsum('nd,erd->enr', x, A3), B3) * SCALE
        act = jax.nn.silu(common_w1[None] + d1) * (common_w3[None] + d3)
        out = jnp.einsum('ne,enf->nf', weight, act) @ w_down.T
        z = jnp.einsum('enf,erf->enr', act, A2)
        out = out + jnp.einsum('ne,enr,edr->nd', weight, z, B2) * SCALE
        return out.reshape(B, S, D)
    x = x + _L0_attn_ref(_layernorm(x, axis=-1), L0_attn_Wqkv, L0_attn_Wo, L0_attn_bo)
    x = x + _L0_xattn_ref(_layernorm(x, axis=-1), ctx_1024, ctx_1024, L0_xattn_Wq, L0_xattn_bq, L0_xattn_Wk, L0_xattn_bk, L0_xattn_Wv, L0_xattn_bv, L0_xattn_Wo, L0_xattn_bo, L0_xattn_w1, L0_xattn_b1, L0_xattn_w2, L0_xattn_b2, L0_xattn_w3, L0_xattn_b3)
    x = x + _L0_ffn_ref(_layernorm(x, axis=-1), L0_ffn_gate_w, L0_ffn_w_gate, L0_ffn_w_up, L0_ffn_w_down, L0_ffn_A1, L0_ffn_B1, L0_ffn_A3, L0_ffn_B3, L0_ffn_A2, L0_ffn_B2)
    return x

_drawn_inputs = setup_inputs


def setup_inputs(seed=0):
    import zlib

    import numpy as np

    out = dict(_drawn_inputs(seed))
    spreads = {'L0_attn_bo': (0.0, 0.1)}
    factors = {'L0_attn_Wqkv': 5.402,
     'L0_attn_Wo': 5.362,
     'L0_xattn_Wq': 8.0,
     'L0_xattn_bq': 8.0,
     'L0_xattn_Wk': 8.0,
     'L0_xattn_bk': 200.0,
     'L0_xattn_bv': 8.0,
     'L0_xattn_w1': 24.034,
     'L0_xattn_b1': 54.432,
     'L0_xattn_w2': 42.99,
     'L0_xattn_b2': 8.0,
     'L0_xattn_w3': 42.99,
     'L0_ffn_gate_w': 8.0,
     'L0_ffn_w_gate': 4.777,
     'L0_ffn_w_up': 4.737,
     'L0_ffn_w_down': 4.747,
     'L0_ffn_A1': 8.0,
     'L0_ffn_B1': 8.0,
     'L0_ffn_A3': 8.0,
     'L0_ffn_B3': 8.0,
     'L0_ffn_A2': 8.0,
     'L0_ffn_B2': 8.0}
    for name, (base, spread) in spreads.items():
        noise = np.random.default_rng([zlib.crc32(name.encode()), seed]).standard_normal(out[name].shape)
        drawn = base * np.exp(spread * noise) if base else spread * noise
        out[name] = jnp.asarray(drawn.astype(out[name].dtype))
    for name, factor in factors.items():
        out[name] = (out[name] * factor).astype(out[name].dtype)
    return out
```

```python
import math

import concourse.bass as bass
from concourse import mybir
from contextlib import ExitStack

F32 = mybir.dt.float32
F32R = mybir.dt.float32r
BF16 = mybir.dt.bfloat16
F16 = mybir.dt.float16
ACT = mybir.ActivationFunctionType
ALU = mybir.AluOpType
AX = mybir.AxisListType

B, T, C, H, DK = 64, 128, 128, 16, 8
QUADS, JH = 4, 4
TC = 77
EPS = 1e-5
LOG_T_MIN, LOG_T_MAX = math.log(0.1), math.log(10.0)
LIFT = 15 * 0.6931471805599453


def need(eng, sem, value):
    if isinstance(value, int) and value <= 0:
        return
    eng.wait_ge(sem, value)


def row_stats(nc, X, ST, b):
    return nc.vector.bn_stats(ST[:, bass.ts(b, 6)], X[:, bass.ts(b, C)])


def inverse_std(nc, tag, X, ST, MEAN, RSTD, with_stats):
    ctx = ExitStack()
    with ctx:
        ve = ctx.enter_context(nc.sbuf_tensor(tag + "_ve", [128, B], F32))
        root = ctx.enter_context(nc.sbuf_tensor(tag + "_root", [128, B], F32))
        y = ctx.enter_context(nc.sbuf_tensor(tag + "_y", [128, B], F32))
        t = ctx.enter_context(nc.sbuf_tensor(tag + "_t", [128, B], F32))
        loaded = [ctx.enter_context(nc.semaphore(f"{tag}_loaded{g}")) for g in range(4)]
        gathered = ctx.enter_context(nc.semaphore(tag + "_gathered"))
        step = ctx.enter_context(nc.semaphore(tag + "_step"))
        rooted = ctx.enter_context(nc.semaphore(tag + "_rooted"))
        block = ctx.enter_context(nc.Block())
        if with_stats is not None:
            @block.sync
            def _(sp):
                for g in range(4):
                    sp.dma_start(X[:, g * 16 * C:(g + 1) * 16 * C].rearrange("t (b c) -> t b c", c=C),
                                 with_stats[g * 16:(g + 1) * 16].rearrange("b t c -> t b c")).then_inc(loaded[g], 16)

        @block.scalar
        def _(act):
            act.wait_ge(step, 3)
            nc.scalar.activation(root[:], ve[:], ACT.Sqrt).then_inc(rooted, 1)

        @block.vector
        def _(dve):
            if with_stats is not None:
                for g in range(4):
                    dve.wait_ge(loaded[g], 16)
                    with dve.Fori(16 * g, 16 * g + 16) as i:
                        row_stats(nc, X, ST, i).then_inc(gathered, 1)
                dve.wait_ge(gathered, B)
            s6 = ST[:].rearrange("t (b six) -> t b six", six=6)
            mean_even, m2_even, mean_odd, m2_odd = s6[:, :, 1], s6[:, :, 2], s6[:, :, 4], s6[:, :, 5]
            nc.vector.tensor_tensor(MEAN[:], mean_even, mean_odd, ALU.add)
            nc.vector.tensor_tensor(t[:], mean_even, mean_odd, ALU.subtract)
            nc.vector.tensor_tensor(ve[:], m2_even, m2_odd, ALU.add).then_inc(step, 1)
            dve.wait_ge(step, 1)
            nc.vector.tensor_scalar(MEAN[:], MEAN[:], 0.5, None, ALU.mult)
            nc.vector.tensor_tensor(t[:], t[:], t[:], ALU.mult)
            nc.vector.tensor_scalar(ve[:], ve[:], 1.0 / C, EPS, ALU.mult, ALU.add).then_inc(step, 1)
            dve.wait_ge(step, 2)
            nc.vector.scalar_tensor_tensor(ve[:], t[:], 0.25, ve[:], ALU.mult, ALU.add).then_inc(step, 1)
            dve.wait_ge(rooted, 1)
            nc.vector.reciprocal(y[:], root[:]).then_inc(step, 1)
            dve.wait_ge(step, 4)
            nc.vector.tensor_tensor(t[:], y[:], y[:], ALU.mult).then_inc(step, 1)
            dve.wait_ge(step, 5)
            nc.vector.tensor_tensor(t[:], t[:], ve[:], ALU.mult).then_inc(step, 1)
            dve.wait_ge(step, 6)
            nc.vector.tensor_scalar(t[:], t[:], -0.5, 1.5, ALU.mult, ALU.add).then_inc(step, 1)
            dve.wait_ge(step, 7)
            nc.vector.tensor_tensor(RSTD[:], t[:], y[:], ALU.mult).then_inc(step, 1)
            dve.wait_ge(step, 8)


def self_attention(nc, psum, X, ST, MEAN, RSTD, dram):
    ctx = ExitStack()
    with ctx:
        def sb(name, shape, dt=F32):
            return ctx.enter_context(nc.sbuf_tensor("sa_" + name, shape, dt))

        def sem(name):
            return ctx.enter_context(nc.semaphore("sa_" + name))

        S, TR, M, N = psum[0:4], psum[4:6], psum[6], psum[7]

        ident = sb("ident", [128, 128])
        identb = sb("identb", [128, 128], BF16)
        causal = sb("causal", [128, JH * T], BF16)
        headmask = sb("headmask", [128, JH])
        cos = sb("cos", [128, 2 * C])
        sin = sb("sin", [128, 2 * C])
        wqkv = sb("wqkv", [C, 3 * C])
        wo = sb("wo", [C, C])
        bo = sb("bo", [1, C])
        ones_row = sb("ones_row", [1, T])
        lift = sb("lift", [128, 1])
        ones_col = sb("ones_col", [128, H])
        ident16 = sb("ident16", [128, 128], F16)
        xn = sb("xn", [128, 2, C])
        xnT = sb("xnT", [C, T])
        rope_a = sb("rope_a", [128, 2 * C])
        rope_b = sb("rope_b", [128, 2 * C])
        qk = sb("qk", [128, 2 * C])
        vf = sb("vf", [128, C])
        vr = sb("vr", [128, C])
        VS = sb("VS", [128, 2, H, 3, DK + 1], BF16)
        QT = sb("QT", [C, T])
        KM = sb("KM", [C, JH, T])
        mx = sb("mx", [128, H])
        D = sb("D", [128, QUADS, JH * T])
        E = sb("E", [128, QUADS, JH * T])
        HI = sb("HI", [128, QUADS, JH * T], F16)
        LO = sb("LO", [128, QUADS, JH * T], F16)
        PT = sb("PT", [128, 2, 2 * JH * T], F16)
        o3 = sb("o3", [128, H, DK + 1])
        rinv = sb("rinv", [128, H])
        on = sb("on", [128, C])
        oT = sb("oT", [C, T])

        loaded = sem("loaded")
        const_set = sem("const_set")
        rows_done = sem("rows_done")
        xn_ready = sem("xn_ready")
        xnT_ps = sem("xnT_ps")
        xnT_sb = sem("xnT_sb")
        qkv_ps = sem("qkv_ps")
        rope_part = sem("rope_part")
        qk_roped = sem("qk_roped")
        v_sb = sem("v_sb")
        v_part = sem("v_part")
        qkT_ps = sem("qkT_ps")
        qT_sb = sem("qT_sb")
        km_ready = sem("km_ready")
        s_ps = sem("s_ps")
        max_ready = sem("max_ready")
        d_ready = sem("d_ready")
        e_ready = sem("e_ready")
        hi_ready = sem("hi_ready")
        lo_ready = sem("lo_ready")
        tr_ps = sem("tr_ps")
        pt_act = sem("pt_act")
        pt_dve = sem("pt_dve")
        pv_ps = sem("pv_ps")
        o_sum = sem("o_sum")
        o_rinv = sem("o_rinv")
        o_norm = sem("o_norm")
        oT_ps = sem("oT_ps")
        oT_sb = sem("oT_sb")
        proj_ps = sem("proj_ps")
        x_done = sem("x_done")

        def iterations(eng, first, step, last):
            first()
            step(0, 0, False, True, True)
            step(1, 1, True, True, True)
            with eng.Fori(0, (B - 4) // 2) as i:
                step(2 * i + 2, 0, True, True, True)
                step(2 * i + 3, 1, True, True, True)
            step(B - 2, 0, True, True, False)
            step(B - 1, 1, True, False, False)
            last()

        block = ctx.enter_context(nc.Block())

        @block.sync
        def _(sp):
            loads = [(ident, "ident"), (wqkv, "L0_attn_Wqkv"), (cos, "cos"), (sin, "sin"), (identb, "identb"),
                     (causal, "causal"), (headmask, "headmask"), (wo, "L0_attn_Wo"), (bo, "L0_attn_bo"),
                     (ident16, "ident16")]
            for tile, name in loads:
                sp.dma_start(tile[:], dram[name]).then_inc(loaded, 16)
            sp.wait_ge(loaded, 16 * 10)

        ALL_LOADED = 16 * 10

        @block.gpsimd
        def _(pool):
            nc.gpsimd.memset(VS[:], 0.0).then_inc(const_set, 1)
            pool.wait_ge(const_set, 1)
            nc.gpsimd.memset(VS[:, :, :, 0, DK:DK + 1], 1.0).then_inc(const_set, 1)
            nc.gpsimd.memset(ones_row[:], 1.0).then_inc(const_set, 1)
            nc.gpsimd.memset(lift[:], LIFT).then_inc(const_set, 1)
            nc.gpsimd.memset(ones_col[:], 1.0).then_inc(const_set, 1)
            pool.wait_ge(const_set, 5)

            def v_parts(b, p):
                v3 = vf[:].rearrange("k (h d) -> k h d", d=DK)
                r3 = vr[:].rearrange("k (h d) -> k h d", d=DK)
                one = ones_col[:].unsqueeze(2).to_broadcast([128, H, DK])
                need(pool, v_sb, b + 1)
                need(pool, pv_ps, QUADS * (b - 1))
                nc.gpsimd.tensor_tensor(VS[:, p, :, 0, 0:DK], v3, one, ALU.mult).then_inc(v_part, 1)
                pool.wait_ge(v_part, 5 * b + 1)
                nc.gpsimd.tensor_tensor(r3, v3, VS[:, p, :, 0, 0:DK], ALU.subtract).then_inc(v_part, 1)
                pool.wait_ge(v_part, 5 * b + 2)
                nc.gpsimd.tensor_tensor(VS[:, p, :, 1, 0:DK], r3, one, ALU.mult).then_inc(v_part, 1)
                pool.wait_ge(v_part, 5 * b + 3)
                nc.gpsimd.tensor_tensor(r3, r3, VS[:, p, :, 1, 0:DK], ALU.subtract).then_inc(v_part, 1)
                pool.wait_ge(v_part, 5 * b + 4)
                nc.gpsimd.tensor_tensor(VS[:, p, :, 2, 0:DK], r3, one, ALU.mult).then_inc(v_part, 1)

            def lo(b, g):
                pool.wait_ge(hi_ready, QUADS * b + g + 1)
                need(pool, tr_ps, QUADS * (b - 1) + g + 1)
                nc.gpsimd.tensor_tensor(LO[:, g, :], E[:, g, :], HI[:, g, :], ALU.subtract).then_inc(lo_ready, 1)

            def step(b, p, prev, nxt, nxt2):
                lo(b, 0)
                lo(b, 1)
                if nxt:
                    v_parts(b + 1, 1 - p)
                lo(b, 2)
                lo(b, 3)

            iterations(pool, lambda: v_parts(0, 0), step, lambda: None)

        @block.scalar
        def _(act):
            def xnT_copy(b):
                act.wait_ge(xnT_ps, b + 1)
                need(act, qkv_ps, b)
                nc.scalar.copy(xnT[:], M[:, 3 * C:4 * C]).then_inc(xnT_sb, 1)

            def v_copy(b):
                act.wait_ge(rope_part, 3 * (b + 1))
                need(act, v_part, 5 * b)
                nc.scalar.copy(vf[:], M[:, 2 * C:3 * C]).then_inc(v_sb, 1)

            def qT_copy(b):
                act.wait_ge(qkT_ps, b + 1)
                nc.scalar.copy(QT[:], M[:, 0:T]).then_inc(qT_sb, 1)

            def exps(b, g):
                act.wait_ge(d_ready, QUADS * b + g + 1)
                need(act, lo_ready, QUADS * (b - 1) + g + 1)
                nc.scalar.activation(E[:, g, :], D[:, g, :], ACT.Exp, bias=lift[:]).then_inc(e_ready, 1)
                need(act, tr_ps, QUADS * (b - 1) + g + 1)
                nc.scalar.activation(HI[:, g, :], D[:, g, :], ACT.Exp, bias=lift[:]).then_inc(hi_ready, 1)

            def pt_copy(b, g):
                act.wait_ge(tr_ps, QUADS * b + g + 1)
                need(act, pv_ps, QUADS * b + g - 1)
                nc.scalar.copy(PT[:, 0, :], TR[0][:].bitcast(F16)).then_inc(pt_act, 1)

            def oT_copy(b):
                act.wait_ge(oT_ps, b + 1)
                need(act, proj_ps, b)
                nc.scalar.copy(oT[:], N[:, 0:T]).then_inc(oT_sb, 1)

            def first():
                act.wait_ge(const_set, 5)
                xnT_copy(0)
                v_copy(0)
                qT_copy(0)

            def step(b, p, prev, nxt, nxt2):
                if prev:
                    oT_copy(b - 1)
                if nxt:
                    xnT_copy(b + 1)
                exps(b, 0)
                exps(b, 1)
                if nxt:
                    v_copy(b + 1)
                exps(b, 2)
                pt_copy(b, 0)
                exps(b, 3)
                if nxt:
                    qT_copy(b + 1)
                pt_copy(b, 2)

            iterations(act, first, step, lambda: oT_copy(B - 1))

        @block.vector
        def _(dve):
            def layernorm(b, p):
                xb = X[:, bass.ts(b, C)]
                need(dve, xnT_ps, b - 1)
                nc.vector.tensor_scalar(xn[:, p, :], xb, MEAN[:, bass.ds(b, 1)], RSTD[:, bass.ds(b, 1)],
                                        ALU.subtract, ALU.mult).then_inc(xn_ready, 1)

            def rope(b, x_written=0):
                dve.wait_ge(qkv_ps, b + 1)
                ps = M[:, 0:2 * C].rearrange("t (i two) -> t i two", two=2)
                rb = rope_b[:].rearrange("t (i two) -> t i two", two=2)
                sn = sin[:].rearrange("t (i two) -> t i two", two=2)
                nc.vector.tensor_tensor(rope_a[:], M[:, 0:2 * C], cos[:], ALU.mult).then_inc(rope_part, 1)
                nc.vector.tensor_tensor(rb[:, :, 0], ps[:, :, 1], sn[:, :, 0], ALU.mult).then_inc(rope_part, 1)
                nc.vector.tensor_tensor(rb[:, :, 1], ps[:, :, 0], sn[:, :, 1], ALU.mult).then_inc(rope_part, 1)
                dve.wait_ge(rope_part, 3 * b + 3)
                need(dve, x_done, x_written)
                need(dve, qkT_ps, b)
                nc.vector.tensor_tensor(qk[:], rope_a[:], rope_b[:], ALU.add).then_inc(qk_roped, 1)

            def km(b):
                dve.wait_ge(qT_sb, b + 1)
                nc.vector.tensor_tensor(KM[:], M[:, T:2 * T].unsqueeze(1).to_broadcast([C, JH, T]),
                                        headmask[:].unsqueeze(2).to_broadcast([C, JH, T]),
                                        ALU.mult).then_inc(km_ready, 1)

            def sub(b, g):
                dve.wait_ge(s_ps, QUADS * b + g + 1)
                s3 = S[g][:].rearrange("q (j k) -> q j k", j=JH)
                m4 = mx[:, JH * g:JH * g + JH]
                nc.vector.tensor_reduce(m4, s3, AX.X, ALU.max).then_inc(max_ready, 1)
                dve.wait_ge(max_ready, QUADS * b + g + 1)
                need(dve, hi_ready, QUADS * (b - 1) + g + 1)
                nc.vector.tensor_tensor(D[:, g, :].rearrange("q (j k) -> q j k", j=JH), s3,
                                        m4.unsqueeze(2).to_broadcast([128, JH, T]),
                                        ALU.subtract).then_inc(d_ready, 1)

            def pt_copy(b, g):
                dve.wait_ge(tr_ps, QUADS * b + g + 1)
                need(dve, pv_ps, QUADS * b + g - 1)
                nc.vector.tensor_copy(PT[:, 1, :], TR[1][:].bitcast(F16)).then_inc(pt_dve, 1)

            def norm(b):
                dve.wait_ge(pv_ps, QUADS * (b + 1))
                nc.vector.tensor_reduce(o3[:], N[:, 0:H * 27].rearrange("q (h s e) -> q h e s", h=H, s=3), AX.X,
                                        ALU.add).then_inc(o_sum, 1)
                dve.wait_ge(o_sum, b + 1)
                nc.vector.reciprocal(rinv[:], o3[:, :, DK]).then_inc(o_rinv, 1)
                dve.wait_ge(o_rinv, b + 1)
                need(dve, oT_ps, b)
                nc.vector.tensor_tensor(on[:].rearrange("q (h d) -> q h d", d=DK), o3[:, :, 0:DK],
                                        rinv[:].unsqueeze(2).to_broadcast([128, H, DK]),
                                        ALU.mult).then_inc(o_norm, 1)

            def residual(b):
                dve.wait_ge(proj_ps, b + 1)
                xb = X[:, bass.ts(b, C)]
                nc.vector.tensor_tensor(xb, xb, N[:, T:T + C], ALU.add).then_inc(x_done, 1)

            def stats(b):
                row_stats(nc, X, ST, b).then_inc(rows_done, 1)

            def first():
                dve.wait_ge(loaded, ALL_LOADED)
                layernorm(0, 0)
                rope(0)
                km(0)
                layernorm(1, 1)

            def step(b, p, prev, nxt, nxt2):
                sub(b, 0)
                sub(b, 1)
                if prev:
                    residual(b - 1)
                if nxt:
                    rope(b + 1, b)
                else:
                    dve.wait_ge(x_done, b)
                if prev:
                    stats(b - 1)
                sub(b, 2)
                sub(b, 3)
                if nxt:
                    km(b + 1)
                pt_copy(b, 1)
                pt_copy(b, 3)
                norm(b)
                if nxt2:
                    layernorm(b + 2, p)

            def last():
                residual(B - 1)
                dve.wait_ge(x_done, B)
                stats(B - 1)
                dve.wait_ge(rows_done, B)

            iterations(dve, first, step, last)

        @block.tensor
        def _(pe):
            mm, tr = nc.tensor.matmul, nc.tensor.transpose

            def xn_transpose(b, p):
                pe.wait_ge(xn_ready, b + 1)
                need(pe, qT_sb, b)
                need(pe, km_ready, b)
                tr(M[:, 3 * C:4 * C], xn[:, p, :], ident[:]).then_inc(xnT_ps, 1)

            def qkv(b):
                pe.wait_ge(xnT_sb, b + 1)
                mm(M[:, 0:3 * C], xnT[:], wqkv[:], start=True, stop=True).then_inc(qkv_ps, 1)

            def qk_transpose(b):
                pe.wait_ge(qk_roped, b + 1)
                pe.wait_ge(v_sb, b + 1)
                tr(M[:, 0:T], qk[:, 0:C], ident[:])
                tr(M[:, T:2 * T], qk[:, C:2 * C], ident[:]).then_inc(qkT_ps, 1)

            def scores(b):
                for g in range(QUADS):
                    need(pe, d_ready, QUADS * (b - 1) + g + 1)
                    mm(S[g][:], identb[:], causal[:], start=True, stop=False)
                pe.wait_ge(qT_sb, b + 1)
                pe.wait_ge(km_ready, b + 1)
                for g in range(QUADS):
                    rows = slice(32 * g, 32 * g + 32)
                    mm(S[g][:], QT[rows, :], KM[rows, :, :].rearrange("c j k -> c (j k)"),
                       start=False, stop=True).then_inc(s_ps, 1)

            def p_transpose(b, g):
                pe.wait_ge(lo_ready, QUADS * b + g + 1)
                free = pt_act if g % 2 == 0 else pt_dve
                need(pe, free, 2 * b + g // 2)
                t = TR[g % 2][:].bitcast(F16)
                for part, src in enumerate((HI, LO)):
                    for j in range(JH):
                        n = part * JH + j
                        last = tr(t[:, n * T:(n + 1) * T], src[:, g, j * T:(j + 1) * T], ident16[:])
                last.then_inc(tr_ps, 1)

            def pv(b, g, p):
                if g == 0:
                    pe.wait_ge(v_part, 5 * b + 5)
                    need(pe, x_done, b)
                pe.wait_ge(pt_act if g % 2 == 0 else pt_dve, 2 * b + g // 2 + 1)
                for j in range(JH):
                    h = JH * g + j
                    vs = VS[:, p, h, :, :].rearrange("k s e -> k (s e)")
                    mm(N[:, h * 27:h * 27 + 27], PT[:, g % 2, j * T:(j + 1) * T], vs, start=(h == 0), stop=False,
                       skip_group_check=True)
                    last = mm(N[:, h * 27:h * 27 + 18], PT[:, g % 2, (JH + j) * T:(JH + j + 1) * T], vs[:, 0:18],
                              start=False, stop=(h == H - 1), skip_group_check=True)
                last.then_inc(pv_ps, 1)

            def o_transpose(b):
                pe.wait_ge(o_norm, b + 1)
                tr(N[:, 0:T], on[:], ident[:]).then_inc(oT_ps, 1)

            def project(b):
                pe.wait_ge(oT_sb, b + 1)
                mm(N[:, T:T + C], ones_row[:], bo[:], start=True, stop=False)
                mm(N[:, T:T + C], oT[:], wo[:], start=False, stop=True).then_inc(proj_ps, 1)

            def first():
                pe.wait_ge(loaded, ALL_LOADED)
                pe.wait_ge(const_set, 5)
                xn_transpose(0, 0)
                qkv(0)
                qk_transpose(0)

            def step(b, p, prev, nxt, nxt2):
                scores(b)
                if prev:
                    o_transpose(b - 1)
                if nxt:
                    xn_transpose(b + 1, 1 - p)
                if prev:
                    project(b - 1)
                if nxt:
                    qkv(b + 1)
                p_transpose(b, 0)
                p_transpose(b, 1)
                if nxt:
                    qk_transpose(b + 1)
                pv(b, 0, p)
                p_transpose(b, 2)
                pv(b, 1, p)
                p_transpose(b, 3)
                pv(b, 2, p)
                pv(b, 3, p)

            def last():
                o_transpose(B - 1)
                project(B - 1)

            iterations(pe, first, step, last)

def cross_attention(nc, psum, X, ST, MEAN, RSTD, dram):
    GROUP = 8
    ROUNDS = B // GROUP
    W = JH * TC
    R8 = float(DK) ** 0.5
    ctx = ExitStack()
    with ctx:
        def sb(name, shape, dt=F32):
            return ctx.enter_context(nc.sbuf_tensor("xa_" + name, shape, dt))

        def sem(name):
            return ctx.enter_context(nc.semaphore("xa_" + name))

        S, BT, BQ, TR, BO, BP = psum[0:2], psum[2], psum[3], psum[4:6], psum[6], psum[7]

        ident = sb("ident", [128, 128])
        ident16 = sb("ident16", [128, 128], F16)
        headmask = sb("headmask", [128, JH])
        headsel = sb("headsel", [128, H])
        wq, wk, wv, wo = (sb(n, [C, C]) for n in ("wq", "wk", "wv", "wo"))
        bq, bk = sb("bq", [C, 1]), sb("bk", [C, 1])
        bv, bo = sb("bv", [1, C]), sb("bo", [1, C])
        w1b = sb("w1b", [128, 3, 64])
        w1s = sb("w1s", [128, 3, 64])
        b1, b2 = sb("b1", [64, 1]), sb("b2", [64, 1])
        w2 = sb("w2", [64, 64])
        w2p = sb("w2p", [64, 128])
        w3 = sb("w3", [64, 1])
        w3r = sb("w3r", [64, 128])
        b3 = sb("b3", [128, 1])
        ones_row = sb("ones_row", [1, T])
        ones_col = sb("ones_col", [128, H])
        lift = sb("lift", [128, 1])
        cx = sb("cx", [TC, 2, C])
        xn = sb("xn", [128, C])
        xcT = sb("xcT", [C, T + TC])
        QT = sb("QT", [C, T])
        KT = sb("KT", [C, TC])
        KM = sb("KM", [C, JH, TC])
        vf = sb("vf", [TC, C])
        vr = sb("vr", [TC, C])
        VT = sb("VT", [TC, H * 27], BF16)
        VS = sb("VS", [TC, 2 * GROUP * H * 27], BF16)
        qsum = sb("qsum", [C, 1])
        ksum = sb("ksum", [C, 1])
        mx = sb("mx", [128, H])
        D = sb("D", [128, 2 * GROUP * QUADS * W])
        E1 = sb("E1", [128, QUADS * W])
        E2 = sb("E2", [128, QUADS * W])
        zsum = sb("zsum", [128, 3, H])
        FEAT = sb("FEAT", [128, 3, GROUP * H])
        featq = sb("featq", [128, H])
        h1 = sb("h1", [64, GROUP * H])
        h2 = sb("h2", [64, GROUP * H])
        lt = sb("lt", [128, GROUP * H])
        CF = sb("CF", [128, GROUP * H])
        DC = sb("DC", [128, QUADS, W])
        E = sb("E", [128, QUADS, W])
        HI = sb("HI", [128, QUADS, W], F16)
        LO = sb("LO", [128, QUADS, W], F16)
        PT = sb("PT", [TC, 2, 2 * JH * T], F16)
        o3 = sb("o3", [128, H, DK + 1])
        rinv = sb("rinv", [128, H])
        on = sb("on", [128, C])
        oT = sb("oT", [C, T])

        loaded = sem("loaded")
        const_set = sem("const_set")
        prepared = sem("prepared")
        cx_loaded = [sem("cx_loaded0"), sem("cx_loaded1")]
        xn_ready = sem("xn_ready")
        xcT_ps = sem("xcT_ps")
        xcT_sb = sem("xcT_sb")
        qkv_ps = sem("qkv_ps")
        q_sb = sem("q_sb")
        k_sb = sem("k_sb")
        v_sb = sem("v_sb")
        km_ready = sem("km_ready")
        v_part = sem("v_part")
        v_kept = sem("v_kept")
        feat_q = sem("feat_q")
        s_ps = sem("s_ps")
        max_ready = sem("max_ready")
        d_ready = sem("d_ready")
        e1_ready = sem("e1_ready")
        e2_ready = sem("e2_ready")
        z_step = sem("z_step")
        feat_ready = sem("feat_ready")
        mlp_ps = sem("mlp_ps")
        mlp_act = sem("mlp_act")
        clip_step = sem("clip_step")
        cf_ready = sem("cf_ready")
        dc_ready = sem("dc_ready")
        hi_ready = sem("hi_ready")
        lo_ready = sem("lo_ready")
        tr_ps = sem("tr_ps")
        pt_act = sem("pt_act")
        pt_dve = sem("pt_dve")
        pv_ps = sem("pv_ps")
        o_sum = sem("o_sum")
        o_rinv = sem("o_rinv")
        o_norm = sem("o_norm")
        oT_ps = sem("oT_ps")
        oT_sb = sem("oT_sb")
        proj_ps = sem("proj_ps")
        x_done = sem("x_done")
        rows_done = sem("rows_done")

        loads = [(ident[:], "ident"), (ident16[:], "ident16"), (headmask[:], "headmask"), (headsel[:], "headsel"),
                 (wq[:], "L0_xattn_Wq"), (wk[:], "L0_xattn_Wk"), (wv[:], "L0_xattn_Wv"), (wo[:], "L0_xattn_Wo"),
                 (bq[:], "L0_xattn_bq"), (bk[:], "L0_xattn_bk"), (bv[:], "L0_xattn_bv"), (bo[:], "L0_xattn_bo"),
                 (b1[:], "L0_xattn_b1"), (b2[:], "L0_xattn_b2"), (w2[:], "L0_xattn_w2"), (w3[:], "L0_xattn_w3")]
        ALL_LOADED = 16 * (len(loads) + 2)

        def rounds(eng, step, mlp):
            def pair(r, odd, j, first_half, second_half):
                for k in range(2):
                    s = 2 * j + k
                    step(r, GROUP * r + s, odd * GROUP + s, s, k, first_half,
                         GROUP * (r - 1) + s, (1 - odd) * GROUP + s, second_half)

            def one(r, odd, first_half, second_half):
                peeled = isinstance(r, int) and r < 2
                if peeled:
                    pair(r, odd, 0, first_half, second_half)
                with eng.Fori(int(peeled), GROUP // 2) as j:
                    pair(r, odd, j, first_half, second_half)
                if first_half:
                    mlp(r)

            one(0, 0, True, False)
            one(1, 1, True, True)
            with eng.Fori(1, ROUNDS // 2) as i:
                one(2 * i, 0, True, True)
                one(2 * i + 1, 1, True, True)
            one(ROUNDS, 0, False, True)

        block = ctx.enter_context(nc.Block())

        @block.sync
        def _(sp):
            for tile, name in loads:
                sp.dma_start(tile, dram[name]).then_inc(loaded, 16)
            sp.dma_start(w1b[:], dram["L0_xattn_w1"].unsqueeze(0).to_broadcast([128, 3, 64])).then_inc(loaded, 16)
            sp.dma_start(b3[:], dram["L0_xattn_b3"].to_broadcast([128, 1])).then_inc(loaded, 16)
            ctx_d = dram["ctx_1024"]

            def load(b, k):
                sp.dma_start(cx[:, k, :], ctx_d[bass.ds(b, 1)].rearrange("b t c -> (b t) c")).then_inc(cx_loaded[k], 16)

            load(0, 0)
            load(1, 1)
            with sp.Fori(1, B // 2) as i:
                for k in range(2):
                    sp.wait_ge(xcT_ps, 2 * i + k - 1)
                    load(2 * i + k, k)

        @block.gpsimd
        def _(pool):
            nc.gpsimd.memset(VT[:], 0.0).then_inc(const_set, 1)
            pool.wait_ge(const_set, 1)
            nc.gpsimd.memset(VT[:].rearrange("k (h s e) -> k h s e", h=H, s=3)[:, :, 0, DK:DK + 1], 1.0).then_inc(const_set, 1)
            nc.gpsimd.memset(ones_row[:], 1.0).then_inc(const_set, 1)
            nc.gpsimd.memset(lift[:], LIFT).then_inc(const_set, 1)
            nc.gpsimd.memset(ones_col[:], 1.0).then_inc(const_set, 1)
            pool.wait_ge(const_set, 5)
            pool.wait_ge(loaded, ALL_LOADED)

            def km(b):
                need(pool, k_sb, b + 1)
                nc.gpsimd.tensor_tensor(KM[:], KT[:].unsqueeze(1).to_broadcast([C, JH, TC]),
                                        headmask[:].unsqueeze(2).to_broadcast([C, JH, TC]),
                                        ALU.mult).then_inc(km_ready, 1)

            def feature_qk(b, s, r):
                need(pool, feat_ready, 3 * b)
                nc.gpsimd.tensor_tensor(featq[:], headsel[:], qsum[:].to_broadcast([128, H]), ALU.mult).then_inc(feat_q, 1)
                pool.wait_ge(feat_q, 2 * b + 1)
                nc.gpsimd.tensor_tensor(featq[:], featq[:], ksum[:].to_broadcast([128, H]), ALU.mult).then_inc(feat_q, 1)

            def v_parts(b, slot):
                vs = VT[:].rearrange("k (h s e) -> k h s e", h=H, s=3)
                v3 = vf[:].rearrange("k (h d) -> k h d", d=DK)
                r3 = vr[:].rearrange("k (h d) -> k h d", d=DK)
                one = ones_col[0:TC].unsqueeze(2).to_broadcast([TC, H, DK])
                need(pool, v_sb, b + 1)
                need(pool, v_kept, b)
                nc.gpsimd.tensor_tensor(vs[:, :, 0, 0:DK], v3, one, ALU.mult).then_inc(v_part, 1)
                pool.wait_ge(v_part, 5 * b + 1)
                nc.gpsimd.tensor_tensor(r3, v3, vs[:, :, 0, 0:DK], ALU.subtract).then_inc(v_part, 1)
                pool.wait_ge(v_part, 5 * b + 2)
                nc.gpsimd.tensor_tensor(vs[:, :, 1, 0:DK], r3, one, ALU.mult).then_inc(v_part, 1)
                pool.wait_ge(v_part, 5 * b + 3)
                nc.gpsimd.tensor_tensor(r3, r3, vs[:, :, 1, 0:DK], ALU.subtract).then_inc(v_part, 1)
                pool.wait_ge(v_part, 5 * b + 4)
                nc.gpsimd.tensor_tensor(vs[:, :, 2, 0:DK], r3, one, ALU.mult).then_inc(v_part, 1)

            def lo(b, g):
                pool.wait_ge(hi_ready, QUADS * b + g + 1)
                nc.gpsimd.tensor_tensor(LO[:, g, :], E[:, g, :], HI[:, g, :], ALU.subtract).then_inc(lo_ready, 1)

            def step(r, b1_, slot1, s, k, first_half, b2_, slot2, second_half):
                if second_half:
                    lo(b2_, 0)
                    lo(b2_, 1)
                if first_half:
                    km(b1_)
                    feature_qk(b1_, s, r)
                    v_parts(b1_, slot1)
                if second_half:
                    lo(b2_, 2)
                    lo(b2_, 3)

            rounds(pool, step, lambda r: None)

        @block.scalar
        def _(act):
            act.wait_ge(const_set, 5)
            act.wait_ge(loaded, ALL_LOADED)

            def exps(b, g):
                act.wait_ge(dc_ready, QUADS * b + g + 1)
                nc.scalar.activation(E[:, g, :], DC[:, g, :], ACT.Exp, bias=lift[:])
                nc.scalar.activation(HI[:, g, :], DC[:, g, :], ACT.Exp, bias=lift[:]).then_inc(hi_ready, 1)

            def step(r, b1_, slot1, s, k, first_half, b2_, slot2, second_half):
                if first_half:
                    act.wait_ge(xcT_ps, b1_ + 1)
                    nc.scalar.copy(xcT[:], BT[:, 0:T + TC]).then_inc(xcT_sb, 1)
                if second_half:
                    exps(b2_, 0)
                    exps(b2_, 1)
                if first_half:
                    act.wait_ge(qkv_ps, b1_ + 1)
                    need(act, feat_ready, 3 * b1_)
                    nc.scalar.activation(QT[:], BQ[:, 0:T], ACT.Identity, bias=bq[:],
                                         accum_out=qsum[:]).then_inc(q_sb, 1)
                    nc.scalar.activation(KT[:], BQ[:, T:T + TC], ACT.Identity, bias=bk[:],
                                         accum_out=ksum[:]).then_inc(k_sb, 1)
                    need(act, v_part, 5 * b1_)
                    nc.scalar.copy(vf[:], BQ[0:TC, 2 * T:2 * T + C]).then_inc(v_sb, 1)
                if second_half:
                    exps(b2_, 2)
                    act.wait_ge(tr_ps, QUADS * b2_ + 1)
                    nc.scalar.copy(PT[:, 0, :], TR[0][0:TC].bitcast(F16)).then_inc(pt_act, 1)
                    exps(b2_, 3)
                    act.wait_ge(tr_ps, QUADS * b2_ + 3)
                    act.wait_ge(pv_ps, QUADS * b2_ + 1)
                    nc.scalar.copy(PT[:, 0, :], TR[0][0:TC].bitcast(F16)).then_inc(pt_act, 1)
                if first_half:
                    act.wait_ge(d_ready, QUADS * b1_ + QUADS)
                    d = D[:, bass.ds(slot1 * (QUADS * W), QUADS * W)]
                    nc.scalar.activation(E1[:], d, ACT.Exp, scale=1.0 / R8).then_inc(e1_ready, 1)
                    act.wait_ge(e1_ready, b1_ + 1)
                    nc.scalar.activation(E2[:], E1[:], ACT.Square).then_inc(e2_ready, 1)
                if second_half:
                    act.wait_ge(oT_ps, b2_ + 1)
                    nc.scalar.copy(oT[:], BP[:, 0:T]).then_inc(oT_sb, 1)

            def mlp(r):
                act.wait_ge(mlp_ps, 3 * r + 1)
                nc.scalar.activation(h1[:], BT[0:64, 0:128], ACT.Gelu, bias=b1[:]).then_inc(mlp_act, 1)
                act.wait_ge(mlp_ps, 3 * r + 2)
                nc.scalar.activation(h2[:], BT[0:64, 128:256], ACT.Gelu, bias=b2[:]).then_inc(mlp_act, 1)
                act.wait_ge(clip_step, 2 * r + 2)
                nc.scalar.activation(CF[:], lt[:], ACT.Exp, scale=-1.0).then_inc(mlp_act, 1)

            rounds(act, step, mlp)

        @block.vector
        def _(dve):
            dve.wait_ge(loaded, ALL_LOADED)
            for f, scale in enumerate((1.0 / (T * TC * R8), 1.0 / (T * R8), 1.0 / T)):
                nc.vector.tensor_scalar(w1s[:, f, :], w1b[:, f, :], scale, None, ALU.mult).then_inc(prepared, 1)
            nc.vector.memset(w2p[:, 64:128], 0.0).then_inc(prepared, 1)
            nc.vector.tensor_copy(w2p[:, 0:64], w2[:]).then_inc(prepared, 1)
            nc.vector.tensor_copy(w3r[:], w3[:].to_broadcast([64, 128])).then_inc(prepared, 1)

            def sub(b, slot, s, g):
                dve.wait_ge(s_ps, QUADS * b + g + 1)
                s3 = S[g % 2][:, 0:W].rearrange("q (j k) -> q j k", j=JH)
                m4 = mx[:, JH * g:JH * g + JH]
                nc.vector.tensor_reduce(m4, s3, AX.X, ALU.max).then_inc(max_ready, 1)
                dve.wait_ge(max_ready, QUADS * b + g + 1)
                nc.vector.tensor_tensor(D[:, bass.ds(slot * (QUADS * W) + g * W, W)].rearrange("q (j k) -> q j k", j=JH),
                                        s3, m4.unsqueeze(2).to_broadcast([128, JH, TC]),
                                        ALU.subtract).then_inc(d_ready, 1)

            def scaled(r, b, slot, s, g):
                dve.wait_ge(cf_ready, r)
                cf = CF[:, bass.ds(s * H + JH * g, JH)].unsqueeze(2).to_broadcast([128, JH, TC])
                nc.vector.tensor_tensor(DC[:, g, :].rearrange("q (j k) -> q j k", j=JH),
                                        D[:, bass.ds(slot * (QUADS * W) + g * W, W)].rearrange("q (j k) -> q j k", j=JH),
                                        cf, ALU.mult).then_inc(dc_ready, 1)

            def pt_copy(b, g):
                dve.wait_ge(tr_ps, QUADS * b + g + 1)
                need(dve, pv_ps, QUADS * b + g - 1)
                nc.vector.tensor_copy(PT[:, 1, :], TR[1][0:TC].bitcast(F16)).then_inc(pt_dve, 1)

            def step(r, b1_, slot1, s, k, first_half, b2_, slot2, second_half):
                if first_half:
                    nc.vector.tensor_scalar(xn[:], X[:, bass.ts(b1_, C)], MEAN[:, bass.ds(b1_, 1)],
                                            RSTD[:, bass.ds(b1_, 1)], ALU.subtract, ALU.mult).then_inc(xn_ready, 1)
                if second_half:
                    for g in range(QUADS):
                        scaled(r, b2_, slot2, s, g)
                if first_half:
                    sub(b1_, slot1, s, 0)
                    sub(b1_, slot1, s, 1)
                if second_half:
                    pt_copy(b2_, 1)
                if first_half:
                    sub(b1_, slot1, s, 2)
                    sub(b1_, slot1, s, 3)
                if second_half:
                    pt_copy(b2_, 3)
                    dve.wait_ge(pv_ps, QUADS * (b2_ + 1))
                    nc.vector.tensor_reduce(o3[:], BO[:, 0:H * 27].rearrange("q (h s e) -> q h e s", h=H, s=3), AX.X,
                                            ALU.add).then_inc(o_sum, 1)
                    dve.wait_ge(o_sum, b2_ + 1)
                    nc.vector.reciprocal(rinv[:], o3[:, :, DK]).then_inc(o_rinv, 1)
                    dve.wait_ge(o_rinv, b2_ + 1)
                    nc.vector.tensor_tensor(on[:].rearrange("q (h d) -> q h d", d=DK), o3[:, :, 0:DK],
                                            rinv[:].unsqueeze(2).to_broadcast([128, H, DK]),
                                            ALU.mult).then_inc(o_norm, 1)
                if first_half:
                    e4 = lambda t: t[:].rearrange("q (h k) -> q h k", k=TC)
                    dve.wait_ge(e1_ready, b1_ + 1)
                    nc.vector.tensor_reduce(zsum[:, 0, :], e4(E1), AX.X, ALU.add).then_inc(z_step, 1)
                    dve.wait_ge(z_step, 5 * b1_ + 1)
                    nc.vector.reciprocal(zsum[:, 1, :], zsum[:, 0, :]).then_inc(z_step, 1)
                    dve.wait_ge(e2_ready, b1_ + 1)
                    nc.vector.tensor_reduce(zsum[:, 2, :], e4(E2), AX.X, ALU.add).then_inc(z_step, 1)
                    dve.wait_ge(z_step, 5 * b1_ + 3)
                    nc.vector.tensor_tensor(zsum[:, 2, :], zsum[:, 2, :], zsum[:, 1, :], ALU.mult).then_inc(z_step, 1)
                    dve.wait_ge(z_step, 5 * b1_ + 4)
                    nc.vector.tensor_tensor(zsum[:, 2, :], zsum[:, 2, :], zsum[:, 1, :], ALU.mult).then_inc(z_step, 1)
                    dve.wait_ge(z_step, 5 * b1_ + 5)
                    need(dve, mlp_ps, 3 * r - 2)
                    nc.vector.tensor_scalar(FEAT[:, 2, bass.ts(s, H)], zsum[:, 2, :], -1.0 / TC, 1.0 / (TC - 1),
                                            ALU.add, ALU.mult).then_inc(feat_ready, 1)
                    dve.wait_ge(feat_q, 2 * b1_ + 2)
                    nc.vector.tensor_scalar(FEAT[:, 0, bass.ts(s, H)], featq[:], 1.0, None, ALU.mult).then_inc(feat_ready, 1)
                    dve.wait_ge(v_part, 5 * b1_ + 5)
                    nc.vector.tensor_scalar(VS[:, bass.ds(slot1 * (H * 27), H * 27)], VT[:], 1.0, None,
                                            ALU.mult).then_inc(v_kept, 1)
                    nc.vector.tensor_scalar(FEAT[:, 1, bass.ts(s, H)], mx[:], 1.0, None, ALU.mult).then_inc(feat_ready, 1)
                if second_half:
                    dve.wait_ge(proj_ps, b2_ + 1)
                    xb = X[:, bass.ts(b2_, C)]
                    nc.vector.tensor_tensor(xb, xb, BP[:, T:T + C], ALU.add).then_inc(x_done, 1)
                    dve.wait_ge(x_done, b2_ + 1)
                    nc.vector.tensor_scalar(zsum[:, 0, 0:1], rinv[:, 0:1], 1.0, None, ALU.mult)
                    row_stats(nc, X, ST, b2_).then_inc(rows_done, 1)

            def mlp(r):
                dve.wait_ge(mlp_ps, 3 * r + 3)
                nc.vector.tensor_scalar(lt[:], BT[:, 256:384], b3[:], LOG_T_MIN, ALU.add, ALU.max).then_inc(clip_step, 1)
                dve.wait_ge(clip_step, 2 * r + 1)
                nc.vector.tensor_scalar(lt[:], lt[:], LOG_T_MAX, None, ALU.min).then_inc(clip_step, 1)
                dve.wait_ge(mlp_act, 3 * r + 3)
                nc.vector.tensor_scalar(CF[:], CF[:], 0.5, None, ALU.mult).then_inc(cf_ready, 1)

            rounds(dve, step, mlp)
            dve.wait_ge(rows_done, B)

        @block.tensor
        def _(pe):
            mm, tr = nc.tensor.matmul, nc.tensor.transpose
            pe.wait_ge(const_set, 5)
            pe.wait_ge(loaded, ALL_LOADED)
            pe.wait_ge(prepared, 6)

            def scores(b, g):
                need(pe, d_ready, QUADS * b + max(g - 1, 0))
                rows = slice(32 * g, 32 * g + 32)
                mm(S[g % 2][:, 0:W], QT[rows, :], KM[rows, :, :].rearrange("c j k -> c (j k)"),
                   start=True, stop=True).then_inc(s_ps, 1)

            def p_transpose(b, g):
                pe.wait_ge(lo_ready, QUADS * b + g + 1)
                need(pe, pt_act if g % 2 == 0 else pt_dve, 2 * b + g // 2)
                t = TR[g % 2][0:TC].bitcast(F16)
                for part, src in enumerate((HI, LO)):
                    for j in range(JH):
                        n = part * JH + j
                        last = tr(t[:, n * T:(n + 1) * T], src[:, g, j * TC:(j + 1) * TC], ident16[:])
                last.then_inc(tr_ps, 1)

            def pv(b, slot, g):
                pe.wait_ge(pt_act if g % 2 == 0 else pt_dve, 2 * b + g // 2 + 1)
                if g == 0:
                    pe.wait_ge(v_kept, b + 1)
                    need(pe, o_norm, b)
                for j in range(JH):
                    h = JH * g + j
                    vs = VS[:, bass.ds(slot * (H * 27) + h * 27, 27)]
                    mm(BO[:, h * 27:h * 27 + 27], PT[:, g % 2, j * T:(j + 1) * T], vs, start=(h == 0), stop=False,
                       skip_group_check=True)
                    last = mm(BO[:, h * 27:h * 27 + 18], PT[:, g % 2, (JH + j) * T:(JH + j + 1) * T], VS[:, bass.ds(slot * (H * 27) + h * 27, 18)],
                              start=False, stop=(h == H - 1), skip_group_check=True)
                last.then_inc(pv_ps, 1)

            def step(r, b1_, slot1, s, k, first_half, b2_, slot2, second_half):
                if first_half:
                    pe.wait_ge(xn_ready, b1_ + 1)
                    need(pe, clip_step, 2 * r - 1)
                    tr(BT[:, 0:T], xn[:], ident[:])
                    pe.wait_ge(cx_loaded[k], 8 * (b1_ - k) + 16)
                    tr(BT[:, T:T + TC], cx[:, k, :], ident[0:TC, 0:TC]).then_inc(xcT_ps, 1)
                    pe.wait_ge(xcT_sb, b1_ + 1)
                    need(pe, v_sb, b1_)
                    mm(BQ[:, 0:T], wq[:], xcT[:, 0:T], start=True, stop=True)
                    mm(BQ[:, T:T + TC], wk[:], xcT[:, T:T + TC], start=True, stop=True)
                    mm(BQ[0:TC, 2 * T:2 * T + C], ones_row[:, 0:TC], bv[:], start=True, stop=False)
                    mm(BQ[0:TC, 2 * T:2 * T + C], xcT[:, T:T + TC], wv[:], start=False, stop=True).then_inc(qkv_ps, 1)
                if second_half:
                    p_transpose(b2_, 0)
                    p_transpose(b2_, 1)
                if first_half:
                    pe.wait_ge(q_sb, b1_ + 1)
                    pe.wait_ge(km_ready, b1_ + 1)
                    scores(b1_, 0)
                    scores(b1_, 1)
                if second_half:
                    pv(b2_, slot2, 0)
                    p_transpose(b2_, 2)
                if first_half:
                    scores(b1_, 2)
                    scores(b1_, 3)
                if second_half:
                    pv(b2_, slot2, 1)
                    p_transpose(b2_, 3)
                    pv(b2_, slot2, 2)
                    pv(b2_, slot2, 3)
                    pe.wait_ge(o_norm, b2_ + 1)
                    need(pe, x_done, b2_)
                    tr(BP[:, 0:T], on[:], ident[:]).then_inc(oT_ps, 1)
                    pe.wait_ge(oT_sb, b2_ + 1)
                    mm(BP[:, T:T + C], ones_row[:], bo[:], start=True, stop=False)
                    mm(BP[:, T:T + C], oT[:], wo[:], start=False, stop=True).then_inc(proj_ps, 1)

            def mlp(r):
                pe.wait_ge(feat_ready, 3 * GROUP * r + 3 * GROUP)
                for f in range(3):
                    last = mm(BT[0:64, 0:128], w1s[:, f, :], FEAT[:, f, :], start=(f == 0), stop=(f == 2))
                last.then_inc(mlp_ps, 1)
                pe.wait_ge(mlp_act, 3 * r + 1)
                mm(BT[:, 128:256], w2p[:], h1[:], start=True, stop=True).then_inc(mlp_ps, 1)
                pe.wait_ge(mlp_act, 3 * r + 2)
                mm(BT[:, 256:384], w3r[:], h2[:], start=True, stop=True).then_inc(mlp_ps, 1)

            rounds(pe, step, mlp)

def expert_ffn(nc, psum, X, ST, MEAN, RSTD, dram):
    E8, F, R = 8, 512, 16
    FC = F // 128
    NB = 4
    G = B // NB
    NT = NB * T
    STEPS = E8 * FC
    ctx = ExitStack()
    with ctx:
        def sb(name, shape, dt=F32):
            return ctx.enter_context(nc.sbuf_tensor("ff_" + name, shape, dt))

        def sem(name):
            return ctx.enter_context(nc.semaphore("ff_" + name))

        W1 = [sb("w1hi", [C, E8, F], F32R), sb("w1lo", [C, E8, F], F32R)]
        W3 = [sb("w3hi", [C, E8, F], F32R), sb("w3lo", [C, E8, F], F32R)]
        W2 = sb("w2", [128, E8, FC, C])
        ident = sb("ident", [128, 128])
        loaded = sem("loaded")

        prep = ExitStack()
        with prep:
            def psb(name, shape, dt=F32):
                return prep.enter_context(nc.sbuf_tensor("fp_" + name, shape, dt))

            def psem(name):
                return prep.enter_context(nc.semaphore("fp_" + name))

            wg, wu = psb("wg", [C, F]), psb("wu", [C, F])
            wd = psb("wd", [128, FC, C])
            A1, A3 = psb("A1", [R, E8, C]), psb("A3", [R, E8, C])
            B1, B3 = psb("B1", [R, E8, F]), psb("B3", [R, E8, F])
            A2, B2 = psb("A2", [R, E8, F]), psb("B2", [R, E8, C])
            full = psb("full", [C, 2, F])
            product = psem("product")
            summed = psem("summed")
            hi_done = psem("hi_done")
            lo_done = psem("lo_done")
            block = prep.enter_context(nc.Block())

            @block.sync
            def _(sp):
                loads = [(A1, "L0_ffn_A1"), (B1, "L0_ffn_B1"), (wg, "L0_ffn_w_gate"), (A3, "L0_ffn_A3"),
                         (B3, "L0_ffn_B3"), (wu, "L0_ffn_w_up"), (A2, "L0_ffn_A2"), (B2, "L0_ffn_B2"),
                         (ident, "ident")]
                for tile, name in loads:
                    sp.dma_start(tile[:], dram[name]).then_inc(loaded, 16)
                sp.dma_start(wd[:], dram["L0_ffn_w_down"].rearrange("(c f) d -> f c d", f=128)).then_inc(loaded, 16)

            @block.tensor
            def _(pe):
                pe.wait_ge(loaded, 160)
                for e in range(E8):
                    need(pe, summed, 3 * e)
                    nc.tensor.matmul(psum[0][:], A1[:, e, :], B1[:, e, :], start=True, stop=True).then_inc(product, 1)
                    nc.tensor.matmul(psum[1][:], A3[:, e, :], B3[:, e, :], start=True, stop=True).then_inc(product, 1)
                    for c in range(FC):
                        last = nc.tensor.matmul(psum[2][:, c * C:(c + 1) * C], A2[:, e, c * 128:(c + 1) * 128],
                                                B2[:, e, :], start=True, stop=True)
                    last.then_inc(product, 1)

            @block.vector
            def _(dve):
                dve.wait_ge(loaded, 160)
                for e in range(E8):
                    for n, (w, W) in enumerate(((wg, W1), (wu, W3))):
                        dve.wait_ge(product, 3 * e + n + 1)
                        nc.vector.scalar_tensor_tensor(full[:, n, :], psum[n][:], 2.0, w[:], ALU.mult,
                                                       ALU.add).then_inc(summed, 1)
                        dve.wait_ge(hi_done, 2 * e + n + 1)
                        nc.vector.tensor_tensor(W[1][:, e, :], full[:, n, :], W[0][:, e, :].bitcast(F32),
                                                ALU.subtract).then_inc(lo_done, 1)
                    dve.wait_ge(product, 3 * e + 3)
                    nc.vector.scalar_tensor_tensor(W2[:, e, :, :].rearrange("f c d -> f (c d)"), psum[2][:], 2.0,
                                                   wd[:].rearrange("f c d -> f (c d)"), ALU.mult,
                                                   ALU.add).then_inc(summed, 1)

            @block.scalar
            def _(act):
                for e in range(E8):
                    for n, W in enumerate((W1, W3)):
                        act.wait_ge(summed, 3 * e + n + 1)
                        nc.scalar.copy(W[0][:, e, :], full[:, n, :]).then_inc(hi_done, 1)

        gw = sb("gw", [C, E8])
        tri = sb("tri", [128, E8, E8])
        select = sb("select", [2 * E8, E8, 128], F32R)
        select32 = sb("select32", [2 * E8, E8, 128])
        xn = sb("xn", [128, NB, C])
        xT = sb("xT", [C, NT])
        XH = sb("XH", [C, 2, NT], F32R)
        XL = sb("XL", [C, 2, NT], F32R)
        mx = sb("mx", [128, NB])
        lg = sb("lg", [128, NB, E8])
        ex = sb("ex", [128, NB, E8])
        above = sb("above", [128, NB, E8, E8])
        equal = sb("equal", [128, NB, E8, E8])
        rank = sb("rank", [128, NB, E8])
        z = sb("z", [128, NB])
        zi = sb("zi", [128, NB])
        wt = sb("wt", [128, NB, E8])
        whl = sb("whl", [128, NB, 2 * E8], F32R)
        WT = sb("WT", [2 * E8, 2, NT], F32R)
        WB = sb("WB", [128, 2, NT])
        SG = sb("SG", [128, 2, NT])
        GU = sb("GU", [128, 2, NT])
        YW = sb("YW", [C, 2, NT])
        ACC = sb("ACC", [C, NT])

        zero = sb("zero", [C, 1])
        zero_set = sem("zero_set")
        const_loaded = sem("const_loaded")
        xn_ready = sem("xn_ready")
        xT_ps = sem("xT_ps")
        xT_sb = sem("xT_sb")
        xh_ready = sem("xh_ready")
        xl_ready = sem("xl_ready")
        logits_ps = sem("logits_ps")
        route = sem("route")
        ex_ready = sem("ex_ready")
        wT_ps = sem("wT_ps")
        wT_ready = sem("wT_ready")
        wb_ps = sem("wb_ps")
        wb_ready = sem("wb_ready")
        up_ps = sem("up_ps")
        silu_done = sem("silu_done")
        gu_done = sem("gu_done")
        y_ps = sem("y_ps")
        yw_done = sem("yw_done")
        acc_done = sem("acc_done")
        back_ps = sem("back_ps")
        x_done = sem("x_done")
        ROUTE = 12

        H1, H3, Y, BF, BW = psum[0:2], psum[2:4], psum[4:6], psum[6], psum[7]

        def groups(eng, first, step):
            first()
            step(0, 0, True)
            step(1, 1, True)
            with eng.Fori(1, G // 2 - 1) as i:
                step(2 * i, 0, True)
                step(2 * i + 1, 1, True)
            step(G - 2, 0, True)
            step(G - 1, 1, False)

        block = ctx.enter_context(nc.Block())

        @block.sync
        def _(sp):
            sp.dma_start(gw[:], dram["L0_ffn_gate_w"]).then_inc(const_loaded, 16)
            sp.dma_start(tri[:], dram["tri"]).then_inc(const_loaded, 16)
            sp.dma_start(select32[:], dram["select"]).then_inc(const_loaded, 16)

        @block.gpsimd
        def _(pool):
            def step(g, p, nxt):
                for e in range(E8):
                    pool.wait_ge(yw_done, E8 * g + e + 1)
                    if e == 0:
                        need(pool, back_ps, g)
                    if e == 1:
                        pool.wait_ge(acc_done, E8 * g + 1)
                    elif e > 1:
                        pool.wait_ge(acc_done, E8 * g + e)
                    if e == 0:
                        nc.gpsimd.tensor_tensor(ACC[:], YW[:, 0, :], zero[:].to_broadcast([C, NT]), ALU.add).then_inc(acc_done, 1)
                    else:
                        nc.gpsimd.tensor_tensor(ACC[:], ACC[:], YW[:, e % 2, :], ALU.add).then_inc(acc_done, 1)

            pool.wait_ge(zero_set, 1)
            groups(pool, lambda: None, step)

        @block.scalar
        def _(act):
            def front_a(g, p):
                act.wait_ge(xT_ps, g + 1)
                need(act, logits_ps, g)
                nc.scalar.copy(xT[:], BF[:]).then_inc(xT_sb, 1)
                act.wait_ge(xT_sb, g + 1)
                need(act, y_ps, STEPS * (g - 1))
                nc.scalar.copy(XH[:, p, :], xT[:]).then_inc(xh_ready, 1)

            def front_b(g, p):
                act.wait_ge(route, ROUTE * g + 2)
                nc.scalar.activation(ex[:], lg[:], ACT.Exp).then_inc(ex_ready, 1)

            def front_c(g, p):
                act.wait_ge(wT_ps, g + 1)
                nc.scalar.copy(WT[:, p, :], BF[0:2 * E8, :]).then_inc(wT_ready, 1)

            def weight(g, e):
                act.wait_ge(wb_ps, E8 * g + e + 1)
                need(act, yw_done, E8 * g + e - 1)
                nc.scalar.copy(WB[:, e % 2, :], BW[:]).then_inc(wb_ready, 1)

            def step(g, p, nxt):
                for e in range(E8):
                    if nxt and e == 1:
                        front_a(g + 1, 1 - p)
                    if nxt and e == 3:
                        front_b(g + 1, 1 - p)
                    if nxt and e == 5:
                        front_c(g + 1, 1 - p)
                    for c in range(FC):
                        k = FC * e + c
                        act.wait_ge(up_ps, STEPS * g + k + 1)
                        need(act, gu_done, STEPS * g + k - 1)
                        nc.scalar.activation(SG[:, k % 2, :], H1[k % 2][:], ACT.Silu).then_inc(silu_done, 1)
                        if c == 0:
                            weight(g, e)

            def first():
                front_a(0, 0)
                front_b(0, 0)
                front_c(0, 0)

            groups(act, first, step)

        @block.vector
        def _(dve):
            nc.vector.memset(zero[:], 0.0).then_inc(zero_set, 1)
            dve.wait_ge(const_loaded, 48)
            nc.vector.tensor_copy(select[:], select32[:]).then_inc(zero_set, 1)

            def front_a(g, p):
                need(dve, xT_ps, g)
                for n in range(NB):
                    b = g * NB + n
                    last = nc.vector.tensor_scalar(xn[:, n, :], X[:, bass.ds(b * C, C)], MEAN[:, bass.ds(b, 1)],
                                                   RSTD[:, bass.ds(b, 1)], ALU.subtract, ALU.mult)
                last.then_inc(xn_ready, 1)

            def front_b(g, p):
                dve.wait_ge(xh_ready, g + 1)
                nc.vector.tensor_tensor(XL[:, p, :], xT[:], XH[:, p, :].bitcast(F32), ALU.subtract).then_inc(xl_ready, 1)
                dve.wait_ge(logits_ps, g + 1)
                l3 = BF[:, 0:NB * E8].rearrange("n (b e) -> n b e", e=E8)
                nc.vector.tensor_reduce(mx[:], l3, AX.X, ALU.max).then_inc(route, 1)
                dve.wait_ge(route, ROUTE * g + 1)
                nc.vector.tensor_tensor(lg[:], l3, mx[:].unsqueeze(2).to_broadcast([128, NB, E8]),
                                        ALU.subtract).then_inc(route, 1)

            def front_c(g, p):
                dve.wait_ge(route, ROUTE * g + 2)
                for n in range(NB):
                    own = lg[:, n, :].unsqueeze(2).to_broadcast([128, E8, E8])
                    other = lg[:, n, :].unsqueeze(1).to_broadcast([128, E8, E8])
                    nc.vector.tensor_tensor(above[:, n], other, own, ALU.is_gt)
                    last = nc.vector.tensor_tensor(equal[:, n], other, own, ALU.is_equal)
                last.then_inc(route, 1)
                dve.wait_ge(route, ROUTE * g + 3)
                eq = equal[:].rearrange("n b e j -> n b (e j)")
                nc.vector.tensor_tensor(eq, eq, tri[:].rearrange("n e j -> n (e j)").unsqueeze(1)
                                        .to_broadcast([128, NB, E8 * E8]), ALU.mult).then_inc(route, 1)
                dve.wait_ge(route, ROUTE * g + 4)
                nc.vector.tensor_tensor(above[:], above[:], equal[:], ALU.add).then_inc(route, 1)
                dve.wait_ge(route, ROUTE * g + 5)
                nc.vector.tensor_reduce(rank[:], above[:], AX.X, ALU.add).then_inc(route, 1)
                dve.wait_ge(route, ROUTE * g + 6)
                dve.wait_ge(ex_ready, g + 1)
                nc.vector.scalar_tensor_tensor(wt[:], rank[:], 2.0, ex[:], ALU.is_lt, ALU.mult).then_inc(route, 1)
                dve.wait_ge(route, ROUTE * g + 7)
                nc.vector.tensor_reduce(z[:], wt[:], AX.X, ALU.add).then_inc(route, 1)
                dve.wait_ge(route, ROUTE * g + 8)
                nc.vector.reciprocal(zi[:], z[:]).then_inc(route, 1)
                dve.wait_ge(route, ROUTE * g + 9)
                nc.vector.tensor_tensor(wt[:], wt[:], zi[:].unsqueeze(2).to_broadcast([128, NB, E8]),
                                        ALU.mult).then_inc(route, 1)
                dve.wait_ge(route, ROUTE * g + 10)
                need(dve, wT_ps, g)
                nc.vector.tensor_scalar(whl[:, :, 0:E8], wt[:], 1.0, None, ALU.mult).then_inc(route, 1)
                dve.wait_ge(route, ROUTE * g + 11)
                nc.vector.tensor_tensor(whl[:, :, E8:2 * E8], wt[:], whl[:, :, 0:E8].bitcast(F32),
                                        ALU.subtract).then_inc(route, 1)

            def combine(g, e):
                dve.wait_ge(y_ps, STEPS * g + FC * e + FC)
                dve.wait_ge(wb_ready, E8 * g + e + 1)
                need(dve, acc_done, E8 * g + e - 1)
                nc.vector.tensor_tensor(YW[:, e % 2, :], Y[e % 2][:], WB[:, e % 2, :], ALU.mult).then_inc(yw_done, 1)

            def residual(g):
                dve.wait_ge(back_ps, g + 1)
                xg = X[:, bass.ds(g * (NB * C), NB * C)]
                nc.vector.tensor_tensor(xg, xg, BF[:], ALU.add).then_inc(x_done, 1)

            def step(g, p, nxt):
                for e in range(E8):
                    if nxt and e == 0:
                        front_a(g + 1, 1 - p)
                    if nxt and e == 2:
                        front_b(g + 1, 1 - p)
                    if nxt and e == 4:
                        front_c(g + 1, 1 - p)
                    for c in range(FC):
                        k = FC * e + c
                        dve.wait_ge(silu_done, STEPS * g + k + 1)
                        need(dve, y_ps, STEPS * g + k - 1)
                        nc.vector.tensor_tensor(GU[:, k % 2, :], SG[:, k % 2, :], H3[k % 2][:],
                                                ALU.mult).then_inc(gu_done, 1)
                        if c == 1 and e > 0:
                            combine(g, e - 1)
                combine(g, E8 - 1)
                residual(g)

            def first():
                front_a(0, 0)
                front_b(0, 0)
                front_c(0, 0)

            groups(dve, first, step)
            dve.wait_ge(x_done, G)

        @block.tensor
        def _(pe):
            mm, tr = nc.tensor.matmul, nc.tensor.transpose
            pe.wait_ge(const_loaded, 48)
            pe.wait_ge(zero_set, 2)

            def front_a(g, p):
                pe.wait_ge(xn_ready, g + 1)
                need(pe, x_done, g - 1)
                for n in range(NB):
                    last = tr(BF[:, n * T:(n + 1) * T], xn[:, n, :], ident[:])
                last.then_inc(xT_ps, 1)

            def front_b(g, p):
                pe.wait_ge(xT_sb, g + 1)
                for n in range(NB):
                    last = mm(BF[:, n * E8:(n + 1) * E8], xT[:, n * T:(n + 1) * T], gw[:], start=True, stop=True)
                last.then_inc(logits_ps, 1)

            def front_c(g, p):
                pe.wait_ge(route, ROUTE * g + ROUTE)
                for n in range(NB):
                    last = tr(BF[0:2 * E8, n * T:(n + 1) * T], whl[:, n, :].bitcast(F32), ident[:])
                last.then_inc(wT_ps, 1)

            def weight(g, e, p):
                pe.wait_ge(wT_ready, g + 1)
                need(pe, wb_ready, E8 * g + e)
                mm(BW[:], select[:, e, :], WT[:, p, :], start=True, stop=True).then_inc(wb_ps, 1)

            def up(g, k, p):
                e, c = divmod(k, FC)
                f = slice(c * 128, (c + 1) * 128)
                if k == 0:
                    pe.wait_ge(xh_ready, g + 1)
                    pe.wait_ge(xl_ready, g + 1)
                need(pe, silu_done, STEPS * g + k - 1)
                for w, xx, first in ((W1[0], XH, True), (W1[0], XL, False), (W1[1], XH, False)):
                    mm(H1[k % 2][:], w[:, e, f], xx[:, p, :], start=first, stop=(w is W1[1]))
                need(pe, gu_done, STEPS * g + k - 1)
                for w, xx, first in ((W3[0], XH, True), (W3[0], XL, False), (W3[1], XH, False)):
                    last = mm(H3[k % 2][:], w[:, e, f], xx[:, p, :], start=first, stop=(w is W3[1]))
                last.then_inc(up_ps, 1)

            def down(g, k):
                e, c = divmod(k, FC)
                pe.wait_ge(gu_done, STEPS * g + k + 1)
                if c == 0:
                    need(pe, yw_done, E8 * g + e - 1)
                mm(Y[e % 2][:], W2[:, e, c, :], GU[:, k % 2, :], start=(c == 0), stop=(c == FC - 1)).then_inc(y_ps, 1)

            def step(g, p, nxt):
                for k in range(STEPS):
                    e, c = divmod(k, FC)
                    up(g, k, p)
                    if k:
                        down(g, k - 1)
                    if c == 0:
                        weight(g, e, p)
                    if nxt and k == 3:
                        front_a(g + 1, 1 - p)
                    if nxt and k == 8:
                        front_b(g + 1, 1 - p)
                    if nxt and k == 20:
                        front_c(g + 1, 1 - p)
                down(g, STEPS - 1)
                pe.wait_ge(acc_done, E8 * g + E8)
                if nxt:
                    pe.wait_ge(wT_ready, g + 2)
                for n in range(NB):
                    last = tr(BF[:, n * T:(n + 1) * T], ACC[:, n * T:(n + 1) * T], ident[:])
                last.then_inc(back_ps, 1)

            def first():
                front_a(0, 0)
                front_b(0, 0)
                front_c(0, 0)

            groups(pe, first, step)


def program(nc, dram, out):
    ctx = ExitStack()
    with ctx:
        X = ctx.enter_context(nc.sbuf_tensor("X", [T, B * C], F32))
        psum = [ctx.enter_context(nc.psum_tensor(f"bank{n}", [128, 512], F32)) for n in range(8)]
        ST = ctx.enter_context(nc.sbuf_tensor("ST", [T, 6 * B], F32))
        MEAN = ctx.enter_context(nc.sbuf_tensor("MEAN", [T, B], F32))
        RSTD = ctx.enter_context(nc.sbuf_tensor("RSTD", [T, B], F32))
        inverse_std(nc, "ln1", X, ST, MEAN, RSTD, dram["x"])
        self_attention(nc, psum, X, ST, MEAN, RSTD, dram)
        inverse_std(nc, "ln2", X, ST, MEAN, RSTD, None)
        cross_attention(nc, psum, X, ST, MEAN, RSTD, dram)
        inverse_std(nc, "ln3", X, ST, MEAN, RSTD, None)
        expert_ffn(nc, psum, X, ST, MEAN, RSTD, dram)
        stored = ctx.enter_context(nc.semaphore("stored"))
        block = ctx.enter_context(nc.Block())

        @block.sync
        def _(sp):
            for g in range(4):
                sp.dma_start(out[g * 16:(g + 1) * 16].rearrange("b t c -> t b c"),
                             X[:, g * 16 * C:(g + 1) * 16 * C].rearrange("t (b c) -> t b c", c=C)).then_inc(stored, 16)
            sp.wait_ge(stored, 64)


def kernel(**inputs):
    import numpy as np
    import concourse.bacc as bacc
    from concourse import mybir as mb
    from concourse.bass_utils import run_bass_kernel_spmd

    nc = bacc.Bacc("TRN2", target_bir_lowering=False, num_devices=1)
    arrays = {k: np.ascontiguousarray(v) for k, v in inputs.items()}
    for name, order in (("L0_xattn_Wq", (1, 0)), ("L0_xattn_Wk", (1, 0)), ("L0_xattn_Wv", (1, 0)),
                        ("L0_xattn_Wo", (1, 0)), ("L0_xattn_w1", (1, 0)), ("L0_xattn_w2", (1, 0)),
                        ("L0_xattn_w3", (1, 0)), ("L0_ffn_gate_w", (1, 0)), ("L0_ffn_w_gate", (1, 0)),
                        ("L0_ffn_w_up", (1, 0)), ("L0_ffn_w_down", (1, 0)), ("L0_ffn_A1", (1, 0, 2)),
                        ("L0_ffn_A3", (1, 0, 2)), ("L0_ffn_A2", (1, 0, 2)), ("L0_ffn_B1", (2, 0, 1)),
                        ("L0_ffn_B3", (2, 0, 1)), ("L0_ffn_B2", (2, 0, 1))):
        arrays[name] = np.ascontiguousarray(arrays[name].transpose(order))
    for name in [n for n, a in arrays.items() if a.ndim == 1]:
        as_column = name in ("L0_xattn_bq", "L0_xattn_bk", "L0_xattn_b1", "L0_xattn_b2")
        arrays[name] = arrays[name].reshape(-1, 1) if as_column else arrays[name].reshape(1, -1)
    eye = np.eye(128, dtype=np.float32)
    bf16, f16 = mb.dt.np(mb.dt.bfloat16), np.float16
    inv_freq = 1.0 / 10000.0 ** (np.arange(DK // 2, dtype=np.float32) / (DK // 2))
    angle = np.arange(T, dtype=np.float32)[:, None] * inv_freq.astype(np.float32)[None]
    per_head = lambda a: np.tile(np.repeat(a, 2, axis=1), (1, H))
    sign = np.tile(np.array([-1.0, 1.0]), C // 2)
    scale = DK ** -0.5
    cos, sin = per_head(np.cos(angle)), per_head(np.sin(angle)) * sign
    arrays.update(
        ident=eye, identb=eye.astype(bf16), ident16=eye.astype(f16),
        causal=np.tile(np.where(np.tril(np.ones((T, T), bool)), 0.0, -1e30), (1, JH)).astype(bf16),
        tri=np.ascontiguousarray(np.broadcast_to(np.tril(np.ones((8, 8), np.float32), -1), (128, 8, 8))),
        select=np.repeat(np.tile(np.eye(8, dtype=np.float32), (2, 1))[:, :, None], 128, axis=2),
        headsel=(np.arange(128)[:, None] // DK == np.arange(H)[None]).astype(np.float32),
        headmask=(np.arange(128)[:, None] // DK % JH == np.arange(JH)[None]).astype(np.float32),
        cos=np.concatenate([cos * scale, cos], 1).astype(np.float32),
        sin=np.concatenate([sin * scale, sin], 1).astype(np.float32),
    )
    dram = {n: nc.dram_tensor(n, a.shape, mb.dt.from_np(a.dtype), kind="ExternalInput").ap() for n, a in arrays.items()}
    out = nc.dram_tensor("out", (B, T, C), mb.dt.float32, kind="ExternalOutput").ap()
    program(nc, dram, out)
    r = run_bass_kernel_spmd(nc, [arrays], core_ids=[0])
    return r.results[0]["out"]
```

```python
import math

import concourse.bass as bass
from concourse import mybir
from contextlib import ExitStack

F32 = mybir.dt.float32
F32R = mybir.dt.float32r
BF16 = mybir.dt.bfloat16
F16 = mybir.dt.float16
ACT = mybir.ActivationFunctionType
ALU = mybir.AluOpType
AX = mybir.AxisListType

B, T, C, H, DK = 64, 128, 128, 16, 8
QUADS, JH = 4, 4
TC = 77
EPS = 1e-5
LOG_T_MIN, LOG_T_MAX = math.log(0.1), math.log(10.0)
LIFT = 15 * 0.6931471805599453


def need(eng, sem, value):
    if isinstance(value, int) and value <= 0:
        return
    eng.wait_ge(sem, value)


def row_stats(nc, X, ST, b):
    return nc.vector.bn_stats(ST[:, bass.ts(b, 6)], X[:, bass.ts(b, C)])


def inverse_std(nc, tag, X, ST, MEAN, RSTD, with_stats):
    ctx = ExitStack()
    with ctx:
        ve = ctx.enter_context(nc.sbuf_tensor(tag + "_ve", [128, B], F32))
        root = ctx.enter_context(nc.sbuf_tensor(tag + "_root", [128, B], F32))
        y = ctx.enter_context(nc.sbuf_tensor(tag + "_y", [128, B], F32))
        t = ctx.enter_context(nc.sbuf_tensor(tag + "_t", [128, B], F32))
        loaded = [ctx.enter_context(nc.semaphore(f"{tag}_loaded{g}")) for g in range(4)]
        gathered = ctx.enter_context(nc.semaphore(tag + "_gathered"))
        step = ctx.enter_context(nc.semaphore(tag + "_step"))
        rooted = ctx.enter_context(nc.semaphore(tag + "_rooted"))
        block = ctx.enter_context(nc.Block())
        if with_stats is not None:
            @block.sync
            def _(sp):
                for g in range(4):
                    sp.dma_start(X[:, g * 16 * C:(g + 1) * 16 * C].rearrange("t (b c) -> t b c", c=C),
                                 with_stats[g * 16:(g + 1) * 16].rearrange("b t c -> t b c")).then_inc(loaded[g], 16)

        @block.scalar
        def _(act):
            act.wait_ge(step, 3)
            nc.scalar.activation(root[:], ve[:], ACT.Sqrt).then_inc(rooted, 1)

        @block.vector
        def _(dve):
            if with_stats is not None:
                for g in range(4):
                    dve.wait_ge(loaded[g], 16)
                    with dve.Fori(16 * g, 16 * g + 16) as i:
                        row_stats(nc, X, ST, i).then_inc(gathered, 1)
                dve.wait_ge(gathered, B)
            s6 = ST[:].rearrange("t (b six) -> t b six", six=6)
            mean_even, m2_even, mean_odd, m2_odd = s6[:, :, 1], s6[:, :, 2], s6[:, :, 4], s6[:, :, 5]
            nc.vector.tensor_tensor(MEAN[:], mean_even, mean_odd, ALU.add)
            nc.vector.tensor_tensor(t[:], mean_even, mean_odd, ALU.subtract)
            nc.vector.tensor_tensor(ve[:], m2_even, m2_odd, ALU.add).then_inc(step, 1)
            dve.wait_ge(step, 1)
            nc.vector.tensor_scalar(MEAN[:], MEAN[:], 0.5, None, ALU.mult)
            nc.vector.tensor_tensor(t[:], t[:], t[:], ALU.mult)
            nc.vector.tensor_scalar(ve[:], ve[:], 1.0 / C, EPS, ALU.mult, ALU.add).then_inc(step, 1)
            dve.wait_ge(step, 2)
            nc.vector.scalar_tensor_tensor(ve[:], t[:], 0.25, ve[:], ALU.mult, ALU.add).then_inc(step, 1)
            dve.wait_ge(rooted, 1)
            nc.vector.reciprocal(y[:], root[:]).then_inc(step, 1)
            dve.wait_ge(step, 4)
            nc.vector.tensor_tensor(t[:], y[:], y[:], ALU.mult).then_inc(step, 1)
            dve.wait_ge(step, 5)
            nc.vector.tensor_tensor(t[:], t[:], ve[:], ALU.mult).then_inc(step, 1)
            dve.wait_ge(step, 6)
            nc.vector.tensor_scalar(t[:], t[:], -0.5, 1.5, ALU.mult, ALU.add).then_inc(step, 1)
            dve.wait_ge(step, 7)
            nc.vector.tensor_tensor(RSTD[:], t[:], y[:], ALU.mult).then_inc(step, 1)
            dve.wait_ge(step, 8)


def self_attention(nc, psum, X, ST, MEAN, RSTD, dram):
    ctx = ExitStack()
    with ctx:
        def sb(name, shape, dt=F32):
            return ctx.enter_context(nc.sbuf_tensor("sa_" + name, shape, dt))

        def sem(name):
            return ctx.enter_context(nc.semaphore("sa_" + name))

        S, TR, M, N = psum[0:4], psum[4:6], psum[6], psum[7]

        ident = sb("ident", [128, 128])
        identb = sb("identb", [128, 128], BF16)
        causal = sb("causal", [128, JH * T], BF16)
        headmask = sb("headmask", [128, JH])
        cos = sb("cos", [128, 2 * C])
        sin = sb("sin", [128, 2 * C])
        wqkv = sb("wqkv", [C, 3 * C])
        wo = sb("wo", [C, C])
        bo = sb("bo", [1, C])
        ones_row = sb("ones_row", [1, T])
        lift = sb("lift", [128, 1])
        ones_col = sb("ones_col", [128, H])
        ident16 = sb("ident16", [128, 128], F16)
        xn = sb("xn", [128, 2, C])
        xnT = sb("xnT", [C, T])
        rope_a = sb("rope_a", [128, 2 * C])
        rope_b = sb("rope_b", [128, 2 * C])
        qk = sb("qk", [128, 2 * C])
        vf = sb("vf", [128, C])
        vr = sb("vr", [128, C])
        VS = sb("VS", [128, 2, H, 3, DK + 1], BF16)
        QT = sb("QT", [C, 2, T])
        KM = sb("KM", [C, 2, JH, T])
        mx = sb("mx", [128, H])
        D = sb("D", [128, QUADS, JH * T])
        E = sb("E", [128, QUADS, JH * T])
        HI = sb("HI", [128, 2, QUADS, JH * T], F16)
        LO = sb("LO", [128, 2, QUADS, JH * T], F16)
        PT = sb("PT", [128, 2, 2 * JH * T], F16)
        o3 = sb("o3", [128, H, DK + 1])
        rinv = sb("rinv", [128, H])
        on = sb("on", [128, C])
        oT = sb("oT", [C, T])

        loaded = sem("loaded")
        const_set = sem("const_set")
        rows_done = sem("rows_done")
        xn_ready = sem("xn_ready")
        xnT_ps = sem("xnT_ps")
        xnT_sb = sem("xnT_sb")
        qkv_ps = sem("qkv_ps")
        rope_part = sem("rope_part")
        qk_roped = sem("qk_roped")
        v_sb = sem("v_sb")
        v_part = sem("v_part")
        qkT_ps = sem("qkT_ps")
        qT_sb = sem("qT_sb")
        km_ready = sem("km_ready")
        s_ps = sem("s_ps")
        max_ready = sem("max_ready")
        d_ready = sem("d_ready")
        e_ready = sem("e_ready")
        hi_ready = sem("hi_ready")
        lo_ready = sem("lo_ready")
        tr_ps = sem("tr_ps")
        pt_act = sem("pt_act")
        pt_dve = sem("pt_dve")
        pv_ps = sem("pv_ps")
        o_sum = sem("o_sum")
        o_rinv = sem("o_rinv")
        o_norm = sem("o_norm")
        oT_ps = sem("oT_ps")
        oT_sb = sem("oT_sb")
        proj_ps = sem("proj_ps")
        x_done = sem("x_done")

        def steps(eng, step):
            for n in (-3, -2, -1, 0, 1):
                step(n, n % 2)
            with eng.Fori(1, B // 2 - 2) as i:
                step(2 * i, 0)
                step(2 * i + 1, 1)
            for n in (B - 4, B - 3, B - 2, B - 1, B):
                step(n, n % 2)

        def real(b):
            return not isinstance(b, int) or 0 <= b < B

        block = ctx.enter_context(nc.Block())

        @block.sync
        def _(sp):
            loads = [(ident, "ident"), (wqkv, "L0_attn_Wqkv"), (cos, "cos"), (sin, "sin"), (identb, "identb"),
                     (causal, "causal"), (headmask, "headmask"), (wo, "L0_attn_Wo"), (bo, "L0_attn_bo"),
                     (ident16, "ident16")]
            for tile, name in loads:
                sp.dma_start(tile[:], dram[name]).then_inc(loaded, 16)
            sp.wait_ge(loaded, 16 * 10)

        ALL_LOADED = 16 * 10

        @block.gpsimd
        def _(pool):
            nc.gpsimd.memset(VS[:], 0.0).then_inc(const_set, 1)
            pool.wait_ge(const_set, 1)
            nc.gpsimd.memset(VS[:, :, :, 0, DK:DK + 1], 1.0).then_inc(const_set, 1)
            nc.gpsimd.memset(ones_row[:], 1.0).then_inc(const_set, 1)
            nc.gpsimd.memset(lift[:], LIFT).then_inc(const_set, 1)
            nc.gpsimd.memset(ones_col[:], 1.0).then_inc(const_set, 1)
            pool.wait_ge(const_set, 5)

            def v_parts(b, p):
                v3 = vf[:].rearrange("k (h d) -> k h d", d=DK)
                r3 = vr[:].rearrange("k (h d) -> k h d", d=DK)
                one = ones_col[:].unsqueeze(2).to_broadcast([128, H, DK])
                need(pool, v_sb, b + 1)
                need(pool, pv_ps, QUADS * (b - 1))
                nc.gpsimd.tensor_tensor(VS[:, p, :, 0, 0:DK], v3, one, ALU.mult).then_inc(v_part, 1)
                pool.wait_ge(v_part, 5 * b + 1)
                nc.gpsimd.tensor_tensor(r3, v3, VS[:, p, :, 0, 0:DK], ALU.subtract).then_inc(v_part, 1)
                pool.wait_ge(v_part, 5 * b + 2)
                nc.gpsimd.tensor_tensor(VS[:, p, :, 1, 0:DK], r3, one, ALU.mult).then_inc(v_part, 1)
                pool.wait_ge(v_part, 5 * b + 3)
                nc.gpsimd.tensor_tensor(r3, r3, VS[:, p, :, 1, 0:DK], ALU.subtract).then_inc(v_part, 1)
                pool.wait_ge(v_part, 5 * b + 4)
                nc.gpsimd.tensor_tensor(VS[:, p, :, 2, 0:DK], r3, one, ALU.mult).then_inc(v_part, 1)

            def lo(b, g, p):
                pool.wait_ge(hi_ready, QUADS * b + g + 1)
                need(pool, tr_ps, QUADS * (b - 2) + g + 1)
                nc.gpsimd.tensor_tensor(LO[:, p, g, :], E[:, g, :], HI[:, p, g, :], ALU.subtract).then_inc(lo_ready, 1)

            def step(n, p):
                if real(n + 1):
                    v_parts(n + 1, 1 - p)
                    for g in range(QUADS):
                        lo(n + 1, g, 1 - p)

            steps(pool, step)

        @block.scalar
        def _(act):
            def xnT_copy(b):
                act.wait_ge(xnT_ps, b + 1)
                need(act, qkv_ps, b)
                nc.scalar.copy(xnT[:], M[:, 3 * C:4 * C]).then_inc(xnT_sb, 1)

            def v_copy(b):
                act.wait_ge(rope_part, 3 * (b + 1))
                need(act, v_part, 5 * b)
                nc.scalar.copy(vf[:], M[:, 2 * C:3 * C]).then_inc(v_sb, 1)

            def qT_copy(b, p):
                act.wait_ge(qkT_ps, b + 1)
                nc.scalar.copy(QT[:, p, :], M[:, 0:T]).then_inc(qT_sb, 1)

            def exps(b, g, p):
                act.wait_ge(d_ready, QUADS * b + g + 1)
                need(act, lo_ready, QUADS * (b - 1) + g + 1)
                nc.scalar.activation(E[:, g, :], D[:, g, :], ACT.Exp, bias=lift[:]).then_inc(e_ready, 1)
                need(act, tr_ps, QUADS * (b - 2) + g + 1)
                nc.scalar.activation(HI[:, p, g, :], D[:, g, :], ACT.Exp, bias=lift[:]).then_inc(hi_ready, 1)

            def pt_copy(b, g):
                act.wait_ge(tr_ps, QUADS * b + g + 1)
                need(act, pv_ps, QUADS * b + g - 1)
                nc.scalar.copy(PT[:, 0, :], TR[0][:].bitcast(F16)).then_inc(pt_act, 1)

            def oT_copy(b):
                act.wait_ge(oT_ps, b + 1)
                need(act, proj_ps, b)
                nc.scalar.copy(oT[:], N[:, 0:T]).then_inc(oT_sb, 1)

            act.wait_ge(const_set, 5)

            def step(n, p):
                q = 1 - p
                if real(n - 1):
                    oT_copy(n - 1)
                if real(n):
                    pt_copy(n, 0)
                if real(n + 1):
                    exps(n + 1, 0, q)
                if real(n + 2):
                    xnT_copy(n + 2)
                if real(n + 1):
                    exps(n + 1, 1, q)
                if real(n):
                    pt_copy(n, 2)
                if real(n + 1):
                    exps(n + 1, 2, q)
                    exps(n + 1, 3, q)
                if real(n + 2):
                    v_copy(n + 2)
                    qT_copy(n + 2, p)

            steps(act, step)

        @block.vector
        def _(dve):
            def layernorm(b, p):
                xb = X[:, bass.ts(b, C)]
                need(dve, xnT_ps, b - 1)
                nc.vector.tensor_scalar(xn[:, p, :], xb, MEAN[:, bass.ds(b, 1)], RSTD[:, bass.ds(b, 1)],
                                        ALU.subtract, ALU.mult).then_inc(xn_ready, 1)

            def rope(b):
                dve.wait_ge(qkv_ps, b + 1)
                ps = M[:, 0:2 * C].rearrange("t (i two) -> t i two", two=2)
                rb = rope_b[:].rearrange("t (i two) -> t i two", two=2)
                sn = sin[:].rearrange("t (i two) -> t i two", two=2)
                nc.vector.tensor_tensor(rope_a[:], M[:, 0:2 * C], cos[:], ALU.mult).then_inc(rope_part, 1)
                nc.vector.tensor_tensor(rb[:, :, 0], ps[:, :, 1], sn[:, :, 0], ALU.mult).then_inc(rope_part, 1)
                nc.vector.tensor_tensor(rb[:, :, 1], ps[:, :, 0], sn[:, :, 1], ALU.mult).then_inc(rope_part, 1)
                dve.wait_ge(rope_part, 3 * b + 3)
                need(dve, qkT_ps, b)
                nc.vector.tensor_tensor(qk[:], rope_a[:], rope_b[:], ALU.add).then_inc(qk_roped, 1)

            def km(b, p):
                dve.wait_ge(qT_sb, b + 1)
                nc.vector.tensor_tensor(KM[:, p], M[:, T:2 * T].unsqueeze(1).to_broadcast([C, JH, T]),
                                        headmask[:].unsqueeze(2).to_broadcast([C, JH, T]),
                                        ALU.mult).then_inc(km_ready, 1)

            def sub(b, g):
                dve.wait_ge(s_ps, QUADS * b + g + 1)
                s3 = S[g][:].rearrange("q (j k) -> q j k", j=JH)
                m4 = mx[:, JH * g:JH * g + JH]
                nc.vector.tensor_reduce(m4, s3, AX.X, ALU.max).then_inc(max_ready, 1)
                dve.wait_ge(max_ready, QUADS * b + g + 1)
                need(dve, hi_ready, QUADS * (b - 1) + g + 1)
                nc.vector.tensor_tensor(D[:, g, :].rearrange("q (j k) -> q j k", j=JH), s3,
                                        m4.unsqueeze(2).to_broadcast([128, JH, T]),
                                        ALU.subtract).then_inc(d_ready, 1)

            def pt_copy(b, g):
                dve.wait_ge(tr_ps, QUADS * b + g + 1)
                need(dve, pv_ps, QUADS * b + g - 1)
                nc.vector.tensor_copy(PT[:, 1, :], TR[1][:].bitcast(F16)).then_inc(pt_dve, 1)

            def norm(b):
                dve.wait_ge(pv_ps, QUADS * (b + 1))
                nc.vector.tensor_reduce(o3[:], N[:, 0:H * 27].rearrange("q (h s e) -> q h e s", h=H, s=3), AX.X,
                                        ALU.add).then_inc(o_sum, 1)
                dve.wait_ge(o_sum, b + 1)
                nc.vector.reciprocal(rinv[:], o3[:, :, DK]).then_inc(o_rinv, 1)
                dve.wait_ge(o_rinv, b + 1)
                need(dve, oT_ps, b)
                nc.vector.tensor_tensor(on[:].rearrange("q (h d) -> q h d", d=DK), o3[:, :, 0:DK],
                                        rinv[:].unsqueeze(2).to_broadcast([128, H, DK]),
                                        ALU.mult).then_inc(o_norm, 1)

            def residual(b):
                dve.wait_ge(proj_ps, b + 1)
                xb = X[:, bass.ts(b, C)]
                nc.vector.tensor_tensor(xb, xb, N[:, T:T + C], ALU.add).then_inc(x_done, 1)

            def stats(b):
                row_stats(nc, X, ST, b).then_inc(rows_done, 1)

            dve.wait_ge(loaded, ALL_LOADED)

            def step(n, p):
                if real(n + 1):
                    sub(n + 1, 0)
                if real(n - 1):
                    residual(n - 1)
                if real(n + 1):
                    need(dve, x_done, n)
                    sub(n + 1, 1)
                if real(n):
                    pt_copy(n, 1)
                if real(n - 1):
                    if isinstance(n, int):
                        dve.wait_ge(x_done, n)
                    stats(n - 1)
                if real(n + 1):
                    sub(n + 1, 2)
                    sub(n + 1, 3)
                if real(n + 2):
                    rope(n + 2)
                if real(n):
                    pt_copy(n, 3)
                    norm(n)
                if real(n + 2):
                    km(n + 2, p)
                if real(n + 3):
                    layernorm(n + 3, 1 - p)

            steps(dve, step)
            dve.wait_ge(rows_done, B)

        @block.tensor
        def _(pe):
            mm, tr = nc.tensor.matmul, nc.tensor.transpose

            def xn_transpose(b, p):
                pe.wait_ge(xn_ready, b + 1)
                need(pe, qT_sb, b)
                need(pe, km_ready, b)
                tr(M[:, 3 * C:4 * C], xn[:, p, :], ident[:]).then_inc(xnT_ps, 1)

            def qkv(b):
                pe.wait_ge(xnT_sb, b + 1)
                mm(M[:, 0:3 * C], xnT[:], wqkv[:], start=True, stop=True).then_inc(qkv_ps, 1)

            def qk_transpose(b):
                pe.wait_ge(qk_roped, b + 1)
                pe.wait_ge(v_sb, b + 1)
                tr(M[:, 0:T], qk[:, 0:C], ident[:])
                tr(M[:, T:2 * T], qk[:, C:2 * C], ident[:]).then_inc(qkT_ps, 1)

            def masks(b):
                for g in range(QUADS):
                    need(pe, d_ready, QUADS * (b - 1) + g + 1)
                    mm(S[g][:], identb[:], causal[:], start=True, stop=False)

            def scores(b, g, p):
                if g == 0:
                    pe.wait_ge(qT_sb, b + 1)
                    pe.wait_ge(km_ready, b + 1)
                rows = slice(32 * g, 32 * g + 32)
                mm(S[g][:], QT[rows, p, :], KM[rows, p, :, :].rearrange("c j k -> c (j k)"),
                   start=False, stop=True).then_inc(s_ps, 1)

            def p_transpose(b, g, p):
                pe.wait_ge(lo_ready, QUADS * b + g + 1)
                free = pt_act if g % 2 == 0 else pt_dve
                need(pe, free, 2 * b + g // 2)
                t = TR[g % 2][:].bitcast(F16)
                for part, src in enumerate((HI, LO)):
                    for j in range(JH):
                        n = part * JH + j
                        last = tr(t[:, n * T:(n + 1) * T], src[:, p, g, j * T:(j + 1) * T], ident16[:])
                last.then_inc(tr_ps, 1)

            def pv(b, g, p):
                if g == 0:
                    pe.wait_ge(v_part, 5 * b + 5)
                    need(pe, x_done, b)
                pe.wait_ge(pt_act if g % 2 == 0 else pt_dve, 2 * b + g // 2 + 1)
                for j in range(JH):
                    h = JH * g + j
                    vs = VS[:, p, h, :, :].rearrange("k s e -> k (s e)")
                    mm(N[:, h * 27:h * 27 + 27], PT[:, g % 2, j * T:(j + 1) * T], vs, start=(h == 0), stop=False,
                       skip_group_check=True)
                    last = mm(N[:, h * 27:h * 27 + 18], PT[:, g % 2, (JH + j) * T:(JH + j + 1) * T], vs[:, 0:18],
                              start=False, stop=(h == H - 1), skip_group_check=True)
                last.then_inc(pv_ps, 1)

            def o_transpose(b):
                pe.wait_ge(o_norm, b + 1)
                tr(N[:, 0:T], on[:], ident[:]).then_inc(oT_ps, 1)

            def project(b):
                pe.wait_ge(oT_sb, b + 1)
                mm(N[:, T:T + C], ones_row[:], bo[:], start=True, stop=False)
                mm(N[:, T:T + C], oT[:], wo[:], start=False, stop=True).then_inc(proj_ps, 1)

            pe.wait_ge(loaded, ALL_LOADED)
            pe.wait_ge(const_set, 5)

            def step(n, p):
                q = 1 - p
                now, after, then, prev = real(n), real(n + 1), real(n + 2), real(n - 1)
                if after:
                    masks(n + 1)
                    scores(n + 1, 0, q)
                    scores(n + 1, 1, q)
                if prev:
                    o_transpose(n - 1)
                if now:
                    p_transpose(n, 0, p)
                if prev:
                    project(n - 1)
                if now:
                    p_transpose(n, 1, p)
                if then:
                    xn_transpose(n + 2, p)
                if after:
                    scores(n + 1, 2, q)
                    scores(n + 1, 3, q)
                if now:
                    pv(n, 0, p)
                    p_transpose(n, 2, p)
                if then:
                    qkv(n + 2)
                if now:
                    pv(n, 1, p)
                    p_transpose(n, 3, p)
                    pv(n, 2, p)
                    pv(n, 3, p)
                if then:
                    qk_transpose(n + 2)

            steps(pe, step)


def cross_attention(nc, psum, X, ST, MEAN, RSTD, dram):
    GROUP = 8
    SLOTS = 2 * GROUP
    ROUNDS = B // GROUP
    W = JH * TC
    R8 = float(DK) ** 0.5
    ctx = ExitStack()
    with ctx:
        def sb(name, shape, dt=F32):
            return ctx.enter_context(nc.sbuf_tensor("xa_" + name, shape, dt))

        def sem(name):
            return ctx.enter_context(nc.semaphore("xa_" + name))

        S, BT, BQ, TR, BO, BP = psum[0:2], psum[2], psum[3], psum[4:6], psum[6], psum[7]

        ident = sb("ident", [128, 128])
        ident16 = sb("ident16", [128, 128], F16)
        headmask = sb("headmask", [128, JH])
        headsel = sb("headsel", [128, H])
        wq, wk, wv, wo = (sb(n, [C, C]) for n in ("wq", "wk", "wv", "wo"))
        bq, bk = sb("bq", [C, 1]), sb("bk", [C, 1])
        bv, bo = sb("bv", [1, C]), sb("bo", [1, C])
        w1b = sb("w1b", [128, 3, 64])
        w1s = sb("w1s", [128, 3, 64])
        b1, b2 = sb("b1", [64, 1]), sb("b2", [64, 1])
        w2 = sb("w2", [64, 64])
        w2p = sb("w2p", [64, 128])
        w3 = sb("w3", [64, 1])
        w3r = sb("w3r", [64, 128])
        b3 = sb("b3", [128, 1])
        ones_row = sb("ones_row", [1, T])
        ones_col = sb("ones_col", [128, H])
        lift = sb("lift", [128, 1])
        cx = sb("cx", [TC, 2, C])
        xn = sb("xn", [128, 2, C])
        xcT = sb("xcT", [C, T + TC])
        QT = sb("QT", [C, 2, T])
        KT = sb("KT", [C, TC])
        KM = sb("KM", [C, 2, JH, TC])
        vf = sb("vf", [TC, C])
        vr = sb("vr", [TC, C])
        VT = sb("VT", [TC, H * 27], BF16)
        VS = sb("VS", [TC, SLOTS * H * 27], BF16)
        qsum = sb("qsum", [C, 2])
        ksum = sb("ksum", [C, 2])
        mx = sb("mx", [128, 2, H])
        D = sb("D", [128, SLOTS * QUADS * W])
        E1 = sb("E1", [128, QUADS * W])
        E2 = sb("E2", [128, QUADS * W])
        zsum = sb("zsum", [128, 3, H])
        FEAT = sb("FEAT", [128, 3, GROUP * H])
        h1 = sb("h1", [64, GROUP * H])
        h2 = sb("h2", [64, GROUP * H])
        lt = sb("lt", [128, GROUP * H])
        CF = sb("CF", [128, GROUP * H])
        DC = sb("DC", [128, QUADS, W])
        E = sb("E", [128, QUADS, W])
        HI = sb("HI", [128, 2, QUADS, W], F16)
        LO = sb("LO", [128, 2, QUADS, W], F16)
        PT = sb("PT", [TC, 2, 2 * JH * T], F16)
        o3 = sb("o3", [128, H, DK + 1])
        rinv = sb("rinv", [128, H])
        on = sb("on", [128, C])
        oT = sb("oT", [C, T])

        loaded = sem("loaded")
        const_set = sem("const_set")
        prepared = sem("prepared")
        cx_loaded = [sem("cx_loaded0"), sem("cx_loaded1")]
        xn_ready = sem("xn_ready")
        xcT_ps = sem("xcT_ps")
        xcT_sb = sem("xcT_sb")
        qkv_ps = sem("qkv_ps")
        q_sb = sem("q_sb")
        k_sb = sem("k_sb")
        v_sb = sem("v_sb")
        km_ready = sem("km_ready")
        v_part = sem("v_part")
        v_kept = sem("v_kept")
        feat_qk = sem("feat_qk")
        s_ps = sem("s_ps")
        max_ready = sem("max_ready")
        d_ready = sem("d_ready")
        e1_ready = sem("e1_ready")
        e2_ready = sem("e2_ready")
        z_step = sem("z_step")
        feat_ready = sem("feat_ready")
        mlp_ps = sem("mlp_ps")
        mlp_act = sem("mlp_act")
        clip_step = sem("clip_step")
        cf_ready = sem("cf_ready")
        dc_ready = sem("dc_ready")
        hi_ready = sem("hi_ready")
        lo_ready = sem("lo_ready")
        tr_ps = sem("tr_ps")
        pt_act = sem("pt_act")
        pt_dve = sem("pt_dve")
        pv_ps = sem("pv_ps")
        o_sum = sem("o_sum")
        o_rinv = sem("o_rinv")
        o_norm = sem("o_norm")
        oT_ps = sem("oT_ps")
        oT_sb = sem("oT_sb")
        proj_ps = sem("proj_ps")
        x_done = sem("x_done")
        rows_done = sem("rows_done")

        loads = [(ident[:], "ident"), (ident16[:], "ident16"), (headmask[:], "headmask"), (headsel[:], "headsel"),
                 (wq[:], "L0_xattn_Wq"), (wk[:], "L0_xattn_Wk"), (wv[:], "L0_xattn_Wv"), (wo[:], "L0_xattn_Wo"),
                 (bq[:], "L0_xattn_bq"), (bk[:], "L0_xattn_bk"), (bv[:], "L0_xattn_bv"), (bo[:], "L0_xattn_bo"),
                 (b1[:], "L0_xattn_b1"), (b2[:], "L0_xattn_b2"), (w2[:], "L0_xattn_w2"), (w3[:], "L0_xattn_w3")]
        ALL_LOADED = 16 * (len(loads) + 2)

        def real(b, on=True):
            return 0 <= b < B if isinstance(b, int) else on

        def rounds(eng, step, mlp):
            def alone(r, steps):
                for n in steps:
                    step(r, n, n % 2, (n - 1) % GROUP, True, True)

            def pairs(r, first, last, early, late):
                with eng.Fori(first, last) as j:
                    for k in range(2):
                        step(r, GROUP * r + 1 + 2 * j + k, 1 - k, 2 * j + k, early, late)

            alone(0, (-2, -1, 0, 1, 2))
            pairs(0, 1, 4, True, False)
            mlp(0)
            alone(1, (9, 10, 11, 12, 13, 14))
            pairs(1, 3, 4, True, True)
            mlp(1)
            with eng.Fori(2, ROUNDS - 1) as r:
                pairs(r, 0, 4, True, True)
                mlp(r)
            pairs(ROUNDS - 1, 0, 2, True, True)
            alone(ROUNDS - 1, (B - 3, B - 2, B - 1, B))
            mlp(ROUNDS - 1)
            pairs(ROUNDS, 0, 4, False, True)
            alone(ROUNDS, range(B + 9, B + 12))

        block = ctx.enter_context(nc.Block())

        @block.sync
        def _(sp):
            for tile, name in loads:
                sp.dma_start(tile, dram[name]).then_inc(loaded, 16)
            sp.dma_start(w1b[:], dram["L0_xattn_w1"].unsqueeze(0).to_broadcast([128, 3, 64])).then_inc(loaded, 16)
            sp.dma_start(b3[:], dram["L0_xattn_b3"].to_broadcast([128, 1])).then_inc(loaded, 16)
            ctx_d = dram["ctx_1024"]

            def load(b, k):
                sp.dma_start(cx[:, k, :], ctx_d[bass.ds(b, 1)].rearrange("b t c -> (b t) c")).then_inc(cx_loaded[k], 16)

            load(0, 0)
            load(1, 1)
            with sp.Fori(1, B // 2) as i:
                for k in range(2):
                    sp.wait_ge(xcT_ps, 2 * i + k - 1)
                    load(2 * i + k, k)

        @block.gpsimd
        def _(pool):
            nc.gpsimd.memset(VT[:], 0.0).then_inc(const_set, 1)
            pool.wait_ge(const_set, 1)
            nc.gpsimd.memset(VT[:].rearrange("k (h s e) -> k h s e", h=H, s=3)[:, :, 0, DK:DK + 1], 1.0).then_inc(const_set, 1)
            nc.gpsimd.memset(ones_row[:], 1.0).then_inc(const_set, 1)
            nc.gpsimd.memset(lift[:], LIFT).then_inc(const_set, 1)
            nc.gpsimd.memset(ones_col[:], 1.0).then_inc(const_set, 1)
            pool.wait_ge(const_set, 5)
            pool.wait_ge(loaded, ALL_LOADED)

            def km(b, p):
                need(pool, k_sb, b + 1)
                need(pool, s_ps, QUADS * (b - 1))
                nc.gpsimd.tensor_tensor(KM[:, p], KT[:].unsqueeze(1).to_broadcast([C, JH, TC]),
                                        headmask[:].unsqueeze(2).to_broadcast([C, JH, TC]),
                                        ALU.mult).then_inc(km_ready, 1)

            def v_parts(b):
                vs = VT[:].rearrange("k (h s e) -> k h s e", h=H, s=3)
                v3 = vf[:].rearrange("k (h d) -> k h d", d=DK)
                r3 = vr[:].rearrange("k (h d) -> k h d", d=DK)
                one = ones_col[0:TC].unsqueeze(2).to_broadcast([TC, H, DK])
                need(pool, v_sb, b + 1)
                need(pool, v_kept, b)
                nc.gpsimd.tensor_tensor(vs[:, :, 0, 0:DK], v3, one, ALU.mult).then_inc(v_part, 1)
                pool.wait_ge(v_part, 5 * b + 1)
                nc.gpsimd.tensor_tensor(r3, v3, vs[:, :, 0, 0:DK], ALU.subtract).then_inc(v_part, 1)
                pool.wait_ge(v_part, 5 * b + 2)
                nc.gpsimd.tensor_tensor(vs[:, :, 1, 0:DK], r3, one, ALU.mult).then_inc(v_part, 1)
                pool.wait_ge(v_part, 5 * b + 3)
                nc.gpsimd.tensor_tensor(r3, r3, vs[:, :, 1, 0:DK], ALU.subtract).then_inc(v_part, 1)
                pool.wait_ge(v_part, 5 * b + 4)
                nc.gpsimd.tensor_tensor(vs[:, :, 2, 0:DK], r3, one, ALU.mult).then_inc(v_part, 1)

            def lo(r, b, g, p):
                pool.wait_ge(hi_ready, QUADS * b + g + 1)
                need(pool, tr_ps, QUADS * (b - 2) + g + 1)
                if g == 0:
                    need(pool, cf_ready, r)
                nc.gpsimd.tensor_tensor(LO[:, p, g, :], E[:, g, :], HI[:, p, g, :], ALU.subtract).then_inc(lo_ready, 1)

            def scaled(r, b, s, g):
                if isinstance(b, int):
                    pool.wait_ge(cf_ready, r)
                cf = CF[:, bass.ds(s * H + JH * g, JH)].unsqueeze(2).to_broadcast([128, JH, TC])
                d = D[:, bass.ds((b % SLOTS) * (QUADS * W) + g * W, W)].rearrange("q (j k) -> q j k", j=JH)
                nc.gpsimd.tensor_tensor(DC[:, g, :].rearrange("q (j k) -> q j k", j=JH), d, cf,
                                        ALU.mult).then_inc(dc_ready, 1)

            def step(r, n, p, s, early, late):
                for g in range(QUADS):
                    if real(n - 10, late):
                        lo(r, n - 10, g, p)
                    if real(n - 9, late):
                        scaled(r, n - 9, s, g)
                    if g == 1 and real(n + 1, early):
                        km(n + 1, 1 - p)
                        v_parts(n + 1)

            rounds(pool, step, lambda r: None)

        @block.scalar
        def _(act):
            act.wait_ge(const_set, 5)
            act.wait_ge(loaded, ALL_LOADED)

            def xcT_copy(b):
                act.wait_ge(xcT_ps, b + 1)
                need(act, qkv_ps, b)
                nc.scalar.copy(xcT[:], BT[:, 0:T + TC]).then_inc(xcT_sb, 1)

            def qkv_copy(b, p):
                act.wait_ge(qkv_ps, b + 1)
                need(act, feat_qk, b - 1)
                need(act, s_ps, QUADS * (b - 1))
                nc.scalar.activation(QT[:, p, :], BQ[:, 0:T], ACT.Identity, bias=bq[:],
                                     accum_out=qsum[:, p:p + 1]).then_inc(q_sb, 1)
                need(act, km_ready, b)
                nc.scalar.activation(KT[:], BQ[:, T:T + TC], ACT.Identity, bias=bk[:],
                                     accum_out=ksum[:, p:p + 1]).then_inc(k_sb, 1)
                need(act, v_part, 5 * b)
                nc.scalar.copy(vf[:], BQ[0:TC, 2 * T:2 * T + C]).then_inc(v_sb, 1)

            def exps(b, g, p):
                act.wait_ge(dc_ready, QUADS * b + g + 1)
                need(act, tr_ps, QUADS * (b - 2) + g + 1)
                nc.scalar.activation(E[:, g, :], DC[:, g, :], ACT.Exp, bias=lift[:])
                nc.scalar.activation(HI[:, p, g, :], DC[:, g, :], ACT.Exp, bias=lift[:]).then_inc(hi_ready, 1)

            def pt_copy(b, g):
                act.wait_ge(tr_ps, QUADS * b + g + 1)
                need(act, pv_ps, QUADS * b + g - 1)
                nc.scalar.copy(PT[:, 0, :], TR[0][0:TC].bitcast(F16)).then_inc(pt_act, 1)

            def squares(b):
                act.wait_ge(d_ready, QUADS * b + QUADS)
                need(act, z_step, 5 * b)
                d = D[:, bass.ds((b % SLOTS) * (QUADS * W), QUADS * W)]
                nc.scalar.activation(E1[:], d, ACT.Exp, scale=1.0 / R8).then_inc(e1_ready, 1)
                act.wait_ge(e1_ready, b + 1)
                nc.scalar.activation(E2[:], E1[:], ACT.Square).then_inc(e2_ready, 1)

            def oT_copy(b):
                act.wait_ge(oT_ps, b + 1)
                need(act, proj_ps, b)
                nc.scalar.copy(oT[:], BP[:, 0:T]).then_inc(oT_sb, 1)

            def step(r, n, p, s, early, late):
                if real(n - 12, late):
                    oT_copy(n - 12)
                if real(n - 10, late):
                    exps(n - 10, 0, p)
                if real(n - 11, late):
                    pt_copy(n - 11, 0)
                if real(n + 1, early):
                    xcT_copy(n + 1)
                if real(n - 10, late):
                    exps(n - 10, 1, p)
                    exps(n - 10, 2, p)
                if real(n - 11, late):
                    pt_copy(n - 11, 2)
                if real(n + 1, early):
                    qkv_copy(n + 1, 1 - p)
                if real(n - 10, late):
                    exps(n - 10, 3, p)
                if real(n, early):
                    squares(n)

            def mlp(r):
                act.wait_ge(mlp_ps, 3 * r + 1)
                nc.scalar.activation(h1[:], BT[0:64, 0:128], ACT.Gelu, bias=b1[:]).then_inc(mlp_act, 1)
                act.wait_ge(mlp_ps, 3 * r + 2)
                nc.scalar.activation(h2[:], BT[0:64, 128:256], ACT.Gelu, bias=b2[:]).then_inc(mlp_act, 1)
                act.wait_ge(clip_step, 2 * r + 2)
                need(act, dc_ready, QUADS * GROUP * r)
                nc.scalar.activation(CF[:], lt[:], ACT.Exp, scale=-1.0).then_inc(mlp_act, 1)

            rounds(act, step, mlp)

        @block.vector
        def _(dve):
            dve.wait_ge(loaded, ALL_LOADED)
            for f, scale in enumerate((1.0 / (T * TC * R8), 1.0 / (T * R8), 1.0 / T)):
                nc.vector.tensor_scalar(w1s[:, f, :], w1b[:, f, :], scale, None, ALU.mult).then_inc(prepared, 1)
            nc.vector.memset(w2p[:, 64:128], 0.0).then_inc(prepared, 1)
            nc.vector.tensor_copy(w2p[:, 0:64], w2[:]).then_inc(prepared, 1)
            nc.vector.tensor_copy(w3r[:], w3[:].to_broadcast([64, 128])).then_inc(prepared, 1)

            def layernorm(b, p):
                need(dve, xcT_ps, b - 1)
                nc.vector.tensor_scalar(xn[:, p, :], X[:, bass.ts(b, C)], MEAN[:, bass.ds(b, 1)],
                                        RSTD[:, bass.ds(b, 1)], ALU.subtract, ALU.mult).then_inc(xn_ready, 1)

            def sub(b, p, g):
                dve.wait_ge(s_ps, QUADS * b + g + 1)
                s3 = S[g % 2][:, 0:W].rearrange("q (j k) -> q j k", j=JH)
                m4 = mx[:, p, JH * g:JH * g + JH]
                nc.vector.tensor_reduce(m4, s3, AX.X, ALU.max).then_inc(max_ready, 1)
                dve.wait_ge(max_ready, QUADS * b + g + 1)
                nc.vector.tensor_tensor(D[:, bass.ds((b % SLOTS) * (QUADS * W) + g * W, W)]
                                        .rearrange("q (j k) -> q j k", j=JH),
                                        s3, m4.unsqueeze(2).to_broadcast([128, JH, TC]),
                                        ALU.subtract).then_inc(d_ready, 1)

            def keep_v(b):
                dve.wait_ge(v_part, 5 * b + 5)
                nc.vector.tensor_scalar(VS[:, bass.ds((b % SLOTS) * (H * 27), H * 27)], VT[:], 1.0, None,
                                        ALU.mult).then_inc(v_kept, 1)

            def pt_copy(b, g):
                dve.wait_ge(tr_ps, QUADS * b + g + 1)
                need(dve, pv_ps, QUADS * b + g - 1)
                nc.vector.tensor_copy(PT[:, 1, :], TR[1][0:TC].bitcast(F16)).then_inc(pt_dve, 1)

            def norm(b):
                dve.wait_ge(pv_ps, QUADS * (b + 1))
                nc.vector.tensor_reduce(o3[:], BO[:, 0:H * 27].rearrange("q (h s e) -> q h e s", h=H, s=3), AX.X,
                                        ALU.add).then_inc(o_sum, 1)
                dve.wait_ge(o_sum, b + 1)
                nc.vector.reciprocal(rinv[:], o3[:, :, DK]).then_inc(o_rinv, 1)
                dve.wait_ge(o_rinv, b + 1)
                need(dve, oT_ps, b)
                nc.vector.tensor_tensor(on[:].rearrange("q (h d) -> q h d", d=DK), o3[:, :, 0:DK],
                                        rinv[:].unsqueeze(2).to_broadcast([128, H, DK]),
                                        ALU.mult).then_inc(o_norm, 1)

            def residual(b):
                dve.wait_ge(proj_ps, b + 1)
                xb = X[:, bass.ts(b, C)]
                nc.vector.tensor_tensor(xb, xb, BP[:, T:T + C], ALU.add).then_inc(x_done, 1)

            e4 = lambda t: t[:].rearrange("q (h k) -> q h k", k=TC)

            def sum_e(b, p, s):
                dve.wait_ge(q_sb, b + 1)
                dve.wait_ge(k_sb, b + 1)
                nc.vector.scalar_tensor_tensor(FEAT[:, 0, bass.ds(s * H, H)], headsel[:], qsum[:, p:p + 1],
                                               ksum[:, p:p + 1].to_broadcast([128, H]), ALU.mult,
                                               ALU.mult).then_inc(feat_qk, 1)
                nc.vector.tensor_scalar(FEAT[:, 1, bass.ds(s * H, H)], mx[:, p, :], 1.0, None, ALU.mult).then_inc(feat_ready, 1)
                dve.wait_ge(e1_ready, b + 1)
                nc.vector.tensor_reduce(zsum[:, 0, :], e4(E1), AX.X, ALU.add).then_inc(z_step, 1)

            def sum_e2(b, s):
                dve.wait_ge(z_step, 5 * b + 1)
                nc.vector.reciprocal(zsum[:, 1, :], zsum[:, 0, :]).then_inc(z_step, 1)
                dve.wait_ge(e2_ready, b + 1)
                nc.vector.tensor_reduce(zsum[:, 2, :], e4(E2), AX.X, ALU.add).then_inc(z_step, 1)
                dve.wait_ge(z_step, 5 * b + 3)
                nc.vector.tensor_tensor(zsum[:, 2, :], zsum[:, 2, :], zsum[:, 1, :], ALU.mult).then_inc(z_step, 1)
                dve.wait_ge(z_step, 5 * b + 4)
                nc.vector.tensor_tensor(zsum[:, 2, :], zsum[:, 2, :], zsum[:, 1, :], ALU.mult).then_inc(z_step, 1)
                dve.wait_ge(z_step, 5 * b + 5)
                nc.vector.tensor_scalar(FEAT[:, 2, bass.ds(s * H, H)], zsum[:, 2, :], -1.0 / TC, 1.0 / (TC - 1),
                                        ALU.add, ALU.mult).then_inc(feat_ready, 1)

            def step(r, n, p, s, early, late):
                scores, features = real(n, early), real(n - 1, early)
                if scores:
                    sub(n, p, 0)
                if real(n - 12, late):
                    residual(n - 12)
                if scores:
                    sub(n, p, 1)
                    keep_v(n)
                if real(n - 12, late):
                    dve.wait_ge(x_done, n - 11)
                if real(n - 11, late):
                    pt_copy(n - 11, 1)
                if real(n - 12, late):
                    row_stats(nc, X, ST, n - 12).then_inc(rows_done, 1)
                if features:
                    sum_e(n - 1, 1 - p, s)
                if scores:
                    sub(n, p, 2)
                    sub(n, p, 3)
                if features:
                    sum_e2(n - 1, s)
                if real(n - 11, late):
                    pt_copy(n - 11, 3)
                    norm(n - 11)
                if real(n + 2, early):
                    layernorm(n + 2, p)

            def mlp(r):
                dve.wait_ge(mlp_ps, 3 * r + 3)
                nc.vector.tensor_scalar(lt[:], BT[:, 256:384], b3[:], LOG_T_MIN, ALU.add, ALU.max).then_inc(clip_step, 1)
                dve.wait_ge(clip_step, 2 * r + 1)
                nc.vector.tensor_scalar(lt[:], lt[:], LOG_T_MAX, None, ALU.min).then_inc(clip_step, 1)
                dve.wait_ge(mlp_act, 3 * r + 3)
                nc.vector.tensor_scalar(CF[:], CF[:], 0.5, None, ALU.mult).then_inc(cf_ready, 1)

            rounds(dve, step, mlp)
            dve.wait_ge(rows_done, B)

        @block.tensor
        def _(pe):
            mm, tr = nc.tensor.matmul, nc.tensor.transpose
            pe.wait_ge(const_set, 5)
            pe.wait_ge(loaded, ALL_LOADED)
            pe.wait_ge(prepared, 6)

            def scores(b, g, p):
                need(pe, d_ready, QUADS * b + g - 1)
                if g == 0:
                    pe.wait_ge(q_sb, b + 1)
                    pe.wait_ge(km_ready, b + 1)
                rows = slice(32 * g, 32 * g + 32)
                mm(S[g % 2][:, 0:W], QT[rows, p, :], KM[rows, p, :, :].rearrange("c j k -> c (j k)"),
                   start=True, stop=True).then_inc(s_ps, 1)

            def xc_transpose(r, b, p):
                pe.wait_ge(xn_ready, b + 1)
                need(pe, xcT_sb, b)
                need(pe, clip_step, 2 * r - 1)
                tr(BT[:, 0:T], xn[:, p, :], ident[:])
                pe.wait_ge(cx_loaded[p], 8 * (b - p) + 16)
                tr(BT[:, T:T + TC], cx[:, p, :], ident[0:TC, 0:TC]).then_inc(xcT_ps, 1)

            def qkv(b):
                pe.wait_ge(xcT_sb, b + 1)
                need(pe, v_sb, b)
                mm(BQ[:, 0:T], wq[:], xcT[:, 0:T], start=True, stop=True)
                mm(BQ[:, T:T + TC], wk[:], xcT[:, T:T + TC], start=True, stop=True)
                mm(BQ[0:TC, 2 * T:2 * T + C], ones_row[:, 0:TC], bv[:], start=True, stop=False)
                mm(BQ[0:TC, 2 * T:2 * T + C], xcT[:, T:T + TC], wv[:], start=False, stop=True).then_inc(qkv_ps, 1)

            def p_transpose(b, g, p):
                pe.wait_ge(lo_ready, QUADS * b + g + 1)
                need(pe, pt_act if g % 2 == 0 else pt_dve, 2 * b + g // 2)
                t = TR[g % 2][0:TC].bitcast(F16)
                for part, src in enumerate((HI, LO)):
                    for j in range(JH):
                        n = part * JH + j
                        last = tr(t[:, n * T:(n + 1) * T], src[:, p, g, j * TC:(j + 1) * TC], ident16[:])
                last.then_inc(tr_ps, 1)

            def pv(b, g):
                pe.wait_ge(pt_act if g % 2 == 0 else pt_dve, 2 * b + g // 2 + 1)
                if g == 0:
                    pe.wait_ge(v_kept, b + 1)
                    need(pe, o_sum, b)
                slot = (b % SLOTS) * (H * 27)
                for j in range(JH):
                    h = JH * g + j
                    mm(BO[:, h * 27:h * 27 + 27], PT[:, g % 2, j * T:(j + 1) * T], VS[:, bass.ds(slot + h * 27, 27)],
                       start=(h == 0), stop=False, skip_group_check=True)
                    last = mm(BO[:, h * 27:h * 27 + 18], PT[:, g % 2, (JH + j) * T:(JH + j + 1) * T],
                              VS[:, bass.ds(slot + h * 27, 18)], start=False, stop=(h == H - 1), skip_group_check=True)
                last.then_inc(pv_ps, 1)

            def o_transpose(b):
                pe.wait_ge(o_norm, b + 1)
                need(pe, x_done, b)
                tr(BP[:, 0:T], on[:], ident[:]).then_inc(oT_ps, 1)

            def project(b):
                pe.wait_ge(oT_sb, b + 1)
                mm(BP[:, T:T + C], ones_row[:], bo[:], start=True, stop=False)
                mm(BP[:, T:T + C], oT[:], wo[:], start=False, stop=True).then_inc(proj_ps, 1)

            def step(r, n, p, s, early, late):
                now, out, end, then = real(n, early), real(n - 11, late), real(n - 12, late), real(n + 1, early)
                if end:
                    o_transpose(n - 12)
                if now:
                    scores(n, 0, p)
                    scores(n, 1, p)
                if out:
                    p_transpose(n - 11, 0, 1 - p)
                if end:
                    project(n - 12)
                if out:
                    p_transpose(n - 11, 1, 1 - p)
                if then:
                    xc_transpose(r, n + 1, 1 - p)
                if out:
                    pv(n - 11, 0)
                if now:
                    scores(n, 2, p)
                if out:
                    p_transpose(n - 11, 2, 1 - p)
                if now:
                    scores(n, 3, p)
                if then:
                    qkv(n + 1)
                if out:
                    pv(n - 11, 1)
                    p_transpose(n - 11, 3, 1 - p)
                    pv(n - 11, 2)
                    pv(n - 11, 3)

            def mlp(r):
                pe.wait_ge(feat_ready, 2 * GROUP * r + 2 * GROUP)
                for f in range(3):
                    last = mm(BT[0:64, 0:128], w1s[:, f, :], FEAT[:, f, :], start=(f == 0), stop=(f == 2))
                last.then_inc(mlp_ps, 1)
                pe.wait_ge(mlp_act, 3 * r + 1)
                mm(BT[:, 128:256], w2p[:], h1[:], start=True, stop=True).then_inc(mlp_ps, 1)
                pe.wait_ge(mlp_act, 3 * r + 2)
                mm(BT[:, 256:384], w3r[:], h2[:], start=True, stop=True).then_inc(mlp_ps, 1)

            rounds(pe, step, mlp)


def expert_ffn(nc, psum, X, ST, MEAN, RSTD, dram):
    E8, F, R = 8, 512, 16
    FC = F // 128
    NB = 4
    G = B // NB
    NT = NB * T
    STEPS = E8 * FC
    ctx = ExitStack()
    with ctx:
        def sb(name, shape, dt=F32):
            return ctx.enter_context(nc.sbuf_tensor("ff_" + name, shape, dt))

        def sem(name):
            return ctx.enter_context(nc.semaphore("ff_" + name))

        W1 = [sb("w1hi", [C, E8, F], F32R), sb("w1lo", [C, E8, F], F32R)]
        W3 = [sb("w3hi", [C, E8, F], F32R), sb("w3lo", [C, E8, F], F32R)]
        W2 = sb("w2", [128, E8, FC, C])
        ident = sb("ident", [128, 128])
        loaded = sem("loaded")

        prep = ExitStack()
        with prep:
            def psb(name, shape, dt=F32):
                return prep.enter_context(nc.sbuf_tensor("fp_" + name, shape, dt))

            def psem(name):
                return prep.enter_context(nc.semaphore("fp_" + name))

            wg, wu = psb("wg", [C, F]), psb("wu", [C, F])
            wd = psb("wd", [128, FC, C])
            A1, A3 = psb("A1", [R, E8, C]), psb("A3", [R, E8, C])
            B1, B3 = psb("B1", [R, E8, F]), psb("B3", [R, E8, F])
            A2, B2 = psb("A2", [R, E8, F]), psb("B2", [R, E8, C])
            full = psb("full", [C, 2, F])
            product = psem("product")
            summed = psem("summed")
            hi_done = psem("hi_done")
            lo_done = psem("lo_done")
            block = prep.enter_context(nc.Block())

            @block.sync
            def _(sp):
                loads = [(A1, "L0_ffn_A1"), (B1, "L0_ffn_B1"), (wg, "L0_ffn_w_gate"), (A3, "L0_ffn_A3"),
                         (B3, "L0_ffn_B3"), (wu, "L0_ffn_w_up"), (A2, "L0_ffn_A2"), (B2, "L0_ffn_B2"),
                         (ident, "ident")]
                for tile, name in loads:
                    sp.dma_start(tile[:], dram[name]).then_inc(loaded, 16)
                sp.dma_start(wd[:], dram["L0_ffn_w_down"].rearrange("(c f) d -> f c d", f=128)).then_inc(loaded, 16)

            @block.tensor
            def _(pe):
                pe.wait_ge(loaded, 160)
                for e in range(E8):
                    need(pe, summed, 3 * e)
                    nc.tensor.matmul(psum[0][:], A1[:, e, :], B1[:, e, :], start=True, stop=True).then_inc(product, 1)
                    nc.tensor.matmul(psum[1][:], A3[:, e, :], B3[:, e, :], start=True, stop=True).then_inc(product, 1)
                    for c in range(FC):
                        last = nc.tensor.matmul(psum[2][:, c * C:(c + 1) * C], A2[:, e, c * 128:(c + 1) * 128],
                                                B2[:, e, :], start=True, stop=True)
                    last.then_inc(product, 1)

            @block.vector
            def _(dve):
                dve.wait_ge(loaded, 160)
                for e in range(E8):
                    for n, (w, W) in enumerate(((wg, W1), (wu, W3))):
                        dve.wait_ge(product, 3 * e + n + 1)
                        nc.vector.scalar_tensor_tensor(full[:, n, :], psum[n][:], 2.0, w[:], ALU.mult,
                                                       ALU.add).then_inc(summed, 1)
                        dve.wait_ge(hi_done, 2 * e + n + 1)
                        nc.vector.tensor_tensor(W[1][:, e, :], full[:, n, :], W[0][:, e, :].bitcast(F32),
                                                ALU.subtract).then_inc(lo_done, 1)
                    dve.wait_ge(product, 3 * e + 3)
                    nc.vector.scalar_tensor_tensor(W2[:, e, :, :].rearrange("f c d -> f (c d)"), psum[2][:], 2.0,
                                                   wd[:].rearrange("f c d -> f (c d)"), ALU.mult,
                                                   ALU.add).then_inc(summed, 1)

            @block.scalar
            def _(act):
                for e in range(E8):
                    for n, W in enumerate((W1, W3)):
                        act.wait_ge(summed, 3 * e + n + 1)
                        nc.scalar.copy(W[0][:, e, :], full[:, n, :]).then_inc(hi_done, 1)

        gw = sb("gw", [C, E8])
        tri = sb("tri", [128, E8, E8])
        select = sb("select", [2 * E8, E8, 128], F32R)
        select32 = sb("select32", [2 * E8, E8, 128])
        xn = sb("xn", [128, NB, C])
        xT = sb("xT", [C, NT])
        XH = sb("XH", [C, 2, NT], F32R)
        XL = sb("XL", [C, 2, NT], F32R)
        mx = sb("mx", [128, NB])
        lg = sb("lg", [128, NB, E8])
        ex = sb("ex", [128, NB, E8])
        above = sb("above", [128, NB, E8, E8])
        equal = sb("equal", [128, NB, E8, E8])
        rank = sb("rank", [128, NB, E8])
        z = sb("z", [128, NB])
        zi = sb("zi", [128, NB])
        wt = sb("wt", [128, NB, E8])
        whl = sb("whl", [128, NB, 2 * E8], F32R)
        WT = sb("WT", [2 * E8, 2, NT], F32R)
        WB = sb("WB", [128, 2, NT])
        SG = sb("SG", [128, 2, NT])
        GU = sb("GU", [128, 2, NT])
        YW = sb("YW", [C, 2, NT])
        ACC = sb("ACC", [C, NT])

        zero = sb("zero", [C, 1])
        zero_set = sem("zero_set")
        const_loaded = sem("const_loaded")
        xn_ready = sem("xn_ready")
        xT_ps = sem("xT_ps")
        xT_sb = sem("xT_sb")
        xh_ready = sem("xh_ready")
        xl_ready = sem("xl_ready")
        logits_ps = sem("logits_ps")
        route = sem("route")
        ex_ready = sem("ex_ready")
        wT_ps = sem("wT_ps")
        wT_ready = sem("wT_ready")
        wb_ps = sem("wb_ps")
        wb_ready = sem("wb_ready")
        up_ps = sem("up_ps")
        silu_done = sem("silu_done")
        gu_done = sem("gu_done")
        y_ps = sem("y_ps")
        yw_done = sem("yw_done")
        acc_done = sem("acc_done")
        back_ps = sem("back_ps")
        x_done = sem("x_done")
        ROUTE = 12

        H1, H3, Y, BF, BW = psum[0:2], psum[2:4], psum[4:6], psum[6], psum[7]

        def groups(eng, first, step):
            first()
            step(0, 0, True)
            step(1, 1, True)
            with eng.Fori(1, G // 2 - 1) as i:
                step(2 * i, 0, True)
                step(2 * i + 1, 1, True)
            step(G - 2, 0, True)
            step(G - 1, 1, False)

        block = ctx.enter_context(nc.Block())

        @block.sync
        def _(sp):
            sp.dma_start(gw[:], dram["L0_ffn_gate_w"]).then_inc(const_loaded, 16)
            sp.dma_start(tri[:], dram["tri"]).then_inc(const_loaded, 16)
            sp.dma_start(select32[:], dram["select"]).then_inc(const_loaded, 16)

        @block.gpsimd
        def _(pool):
            def step(g, p, nxt):
                for e in range(E8):
                    pool.wait_ge(yw_done, E8 * g + e + 1)
                    if e == 0:
                        need(pool, back_ps, g)
                    if e == 1:
                        pool.wait_ge(acc_done, E8 * g + 1)
                    elif e > 1:
                        pool.wait_ge(acc_done, E8 * g + e)
                    if e == 0:
                        nc.gpsimd.tensor_tensor(ACC[:], YW[:, 0, :], zero[:].to_broadcast([C, NT]), ALU.add).then_inc(acc_done, 1)
                    else:
                        nc.gpsimd.tensor_tensor(ACC[:], ACC[:], YW[:, e % 2, :], ALU.add).then_inc(acc_done, 1)

            pool.wait_ge(zero_set, 1)
            groups(pool, lambda: None, step)

        @block.scalar
        def _(act):
            def front_a(g, p):
                act.wait_ge(xT_ps, g + 1)
                need(act, logits_ps, g)
                nc.scalar.copy(xT[:], BF[:]).then_inc(xT_sb, 1)
                act.wait_ge(xT_sb, g + 1)
                need(act, y_ps, STEPS * (g - 1))
                nc.scalar.copy(XH[:, p, :], xT[:]).then_inc(xh_ready, 1)

            def front_b(g, p):
                act.wait_ge(route, ROUTE * g + 2)
                nc.scalar.activation(ex[:], lg[:], ACT.Exp).then_inc(ex_ready, 1)

            def front_c(g, p):
                act.wait_ge(wT_ps, g + 1)
                nc.scalar.copy(WT[:, p, :], BF[0:2 * E8, :]).then_inc(wT_ready, 1)

            def weight(g, e):
                act.wait_ge(wb_ps, E8 * g + e + 1)
                need(act, yw_done, E8 * g + e - 1)
                nc.scalar.copy(WB[:, e % 2, :], BW[:]).then_inc(wb_ready, 1)

            def step(g, p, nxt):
                for e in range(E8):
                    if nxt and e == 1:
                        front_a(g + 1, 1 - p)
                    if nxt and e == 3:
                        front_b(g + 1, 1 - p)
                    if nxt and e == 5:
                        front_c(g + 1, 1 - p)
                    for c in range(FC):
                        k = FC * e + c
                        act.wait_ge(up_ps, STEPS * g + k + 1)
                        need(act, gu_done, STEPS * g + k - 1)
                        nc.scalar.activation(SG[:, k % 2, :], H1[k % 2][:], ACT.Silu).then_inc(silu_done, 1)
                        if c == 0:
                            weight(g, e)

            def first():
                front_a(0, 0)
                front_b(0, 0)
                front_c(0, 0)

            groups(act, first, step)

        @block.vector
        def _(dve):
            nc.vector.memset(zero[:], 0.0).then_inc(zero_set, 1)
            dve.wait_ge(const_loaded, 48)
            nc.vector.tensor_copy(select[:], select32[:]).then_inc(zero_set, 1)

            def front_a(g, p):
                need(dve, xT_ps, g)
                for n in range(NB):
                    b = g * NB + n
                    last = nc.vector.tensor_scalar(xn[:, n, :], X[:, bass.ds(b * C, C)], MEAN[:, bass.ds(b, 1)],
                                                   RSTD[:, bass.ds(b, 1)], ALU.subtract, ALU.mult)
                last.then_inc(xn_ready, 1)

            def front_b(g, p):
                dve.wait_ge(xh_ready, g + 1)
                nc.vector.tensor_tensor(XL[:, p, :], xT[:], XH[:, p, :].bitcast(F32), ALU.subtract).then_inc(xl_ready, 1)
                dve.wait_ge(logits_ps, g + 1)
                l3 = BF[:, 0:NB * E8].rearrange("n (b e) -> n b e", e=E8)
                nc.vector.tensor_reduce(mx[:], l3, AX.X, ALU.max).then_inc(route, 1)
                dve.wait_ge(route, ROUTE * g + 1)
                nc.vector.tensor_tensor(lg[:], l3, mx[:].unsqueeze(2).to_broadcast([128, NB, E8]),
                                        ALU.subtract).then_inc(route, 1)

            def front_c(g, p):
                dve.wait_ge(route, ROUTE * g + 2)
                for n in range(NB):
                    own = lg[:, n, :].unsqueeze(2).to_broadcast([128, E8, E8])
                    other = lg[:, n, :].unsqueeze(1).to_broadcast([128, E8, E8])
                    nc.vector.tensor_tensor(above[:, n], other, own, ALU.is_gt)
                    last = nc.vector.tensor_tensor(equal[:, n], other, own, ALU.is_equal)
                last.then_inc(route, 1)
                dve.wait_ge(route, ROUTE * g + 3)
                eq = equal[:].rearrange("n b e j -> n b (e j)")
                nc.vector.tensor_tensor(eq, eq, tri[:].rearrange("n e j -> n (e j)").unsqueeze(1)
                                        .to_broadcast([128, NB, E8 * E8]), ALU.mult).then_inc(route, 1)
                dve.wait_ge(route, ROUTE * g + 4)
                nc.vector.tensor_tensor(above[:], above[:], equal[:], ALU.add).then_inc(route, 1)
                dve.wait_ge(route, ROUTE * g + 5)
                nc.vector.tensor_reduce(rank[:], above[:], AX.X, ALU.add).then_inc(route, 1)
                dve.wait_ge(route, ROUTE * g + 6)
                dve.wait_ge(ex_ready, g + 1)
                nc.vector.scalar_tensor_tensor(wt[:], rank[:], 2.0, ex[:], ALU.is_lt, ALU.mult).then_inc(route, 1)
                dve.wait_ge(route, ROUTE * g + 7)
                nc.vector.tensor_reduce(z[:], wt[:], AX.X, ALU.add).then_inc(route, 1)
                dve.wait_ge(route, ROUTE * g + 8)
                nc.vector.reciprocal(zi[:], z[:]).then_inc(route, 1)
                dve.wait_ge(route, ROUTE * g + 9)
                nc.vector.tensor_tensor(wt[:], wt[:], zi[:].unsqueeze(2).to_broadcast([128, NB, E8]),
                                        ALU.mult).then_inc(route, 1)
                dve.wait_ge(route, ROUTE * g + 10)
                need(dve, wT_ps, g)
                nc.vector.tensor_scalar(whl[:, :, 0:E8], wt[:], 1.0, None, ALU.mult).then_inc(route, 1)
                dve.wait_ge(route, ROUTE * g + 11)
                nc.vector.tensor_tensor(whl[:, :, E8:2 * E8], wt[:], whl[:, :, 0:E8].bitcast(F32),
                                        ALU.subtract).then_inc(route, 1)

            def combine(g, e):
                dve.wait_ge(y_ps, STEPS * g + FC * e + FC)
                dve.wait_ge(wb_ready, E8 * g + e + 1)
                need(dve, acc_done, E8 * g + e - 1)
                nc.vector.tensor_tensor(YW[:, e % 2, :], Y[e % 2][:], WB[:, e % 2, :], ALU.mult).then_inc(yw_done, 1)

            def residual(g):
                dve.wait_ge(back_ps, g + 1)
                xg = X[:, bass.ds(g * (NB * C), NB * C)]
                nc.vector.tensor_tensor(xg, xg, BF[:], ALU.add).then_inc(x_done, 1)

            def step(g, p, nxt):
                for e in range(E8):
                    if nxt and e == 0:
                        front_a(g + 1, 1 - p)
                    if nxt and e == 2:
                        front_b(g + 1, 1 - p)
                    if nxt and e == 4:
                        front_c(g + 1, 1 - p)
                    for c in range(FC):
                        k = FC * e + c
                        dve.wait_ge(silu_done, STEPS * g + k + 1)
                        need(dve, y_ps, STEPS * g + k - 1)
                        nc.vector.tensor_tensor(GU[:, k % 2, :], SG[:, k % 2, :], H3[k % 2][:],
                                                ALU.mult).then_inc(gu_done, 1)
                        if c == 1 and e > 0:
                            combine(g, e - 1)
                combine(g, E8 - 1)
                residual(g)

            def first():
                front_a(0, 0)
                front_b(0, 0)
                front_c(0, 0)

            groups(dve, first, step)
            dve.wait_ge(x_done, G)

        @block.tensor
        def _(pe):
            mm, tr = nc.tensor.matmul, nc.tensor.transpose
            pe.wait_ge(const_loaded, 48)
            pe.wait_ge(zero_set, 2)

            def front_a(g, p):
                pe.wait_ge(xn_ready, g + 1)
                need(pe, x_done, g - 1)
                for n in range(NB):
                    last = tr(BF[:, n * T:(n + 1) * T], xn[:, n, :], ident[:])
                last.then_inc(xT_ps, 1)

            def front_b(g, p):
                pe.wait_ge(xT_sb, g + 1)
                for n in range(NB):
                    last = mm(BF[:, n * E8:(n + 1) * E8], xT[:, n * T:(n + 1) * T], gw[:], start=True, stop=True)
                last.then_inc(logits_ps, 1)

            def front_c(g, p):
                pe.wait_ge(route, ROUTE * g + ROUTE)
                for n in range(NB):
                    last = tr(BF[0:2 * E8, n * T:(n + 1) * T], whl[:, n, :].bitcast(F32), ident[:])
                last.then_inc(wT_ps, 1)

            def weight(g, e, p):
                pe.wait_ge(wT_ready, g + 1)
                need(pe, wb_ready, E8 * g + e)
                mm(BW[:], select[:, e, :], WT[:, p, :], start=True, stop=True).then_inc(wb_ps, 1)

            def up(g, k, p):
                e, c = divmod(k, FC)
                f = slice(c * 128, (c + 1) * 128)
                if k == 0:
                    pe.wait_ge(xh_ready, g + 1)
                    pe.wait_ge(xl_ready, g + 1)
                need(pe, silu_done, STEPS * g + k - 1)
                for w, xx, first in ((W1[0], XH, True), (W1[0], XL, False), (W1[1], XH, False)):
                    mm(H1[k % 2][:], w[:, e, f], xx[:, p, :], start=first, stop=(w is W1[1]))
                need(pe, gu_done, STEPS * g + k - 1)
                for w, xx, first in ((W3[0], XH, True), (W3[0], XL, False), (W3[1], XH, False)):
                    last = mm(H3[k % 2][:], w[:, e, f], xx[:, p, :], start=first, stop=(w is W3[1]))
                last.then_inc(up_ps, 1)

            def down(g, k):
                e, c = divmod(k, FC)
                pe.wait_ge(gu_done, STEPS * g + k + 1)
                if c == 0:
                    need(pe, yw_done, E8 * g + e - 1)
                mm(Y[e % 2][:], W2[:, e, c, :], GU[:, k % 2, :], start=(c == 0), stop=(c == FC - 1)).then_inc(y_ps, 1)

            def step(g, p, nxt):
                for k in range(STEPS):
                    e, c = divmod(k, FC)
                    up(g, k, p)
                    if k:
                        down(g, k - 1)
                    if c == 0:
                        weight(g, e, p)
                    if nxt and k == 3:
                        front_a(g + 1, 1 - p)
                    if nxt and k == 8:
                        front_b(g + 1, 1 - p)
                    if nxt and k == 20:
                        front_c(g + 1, 1 - p)
                down(g, STEPS - 1)
                pe.wait_ge(acc_done, E8 * g + E8)
                if nxt:
                    pe.wait_ge(wT_ready, g + 2)
                for n in range(NB):
                    last = tr(BF[:, n * T:(n + 1) * T], ACC[:, n * T:(n + 1) * T], ident[:])
                last.then_inc(back_ps, 1)

            def first():
                front_a(0, 0)
                front_b(0, 0)
                front_c(0, 0)

            groups(pe, first, step)


def program(nc, dram, out):
    ctx = ExitStack()
    with ctx:
        X = ctx.enter_context(nc.sbuf_tensor("X", [T, B * C], F32))
        psum = [ctx.enter_context(nc.psum_tensor(f"bank{n}", [128, 512], F32)) for n in range(8)]
        ST = ctx.enter_context(nc.sbuf_tensor("ST", [T, 6 * B], F32))
        MEAN = ctx.enter_context(nc.sbuf_tensor("MEAN", [T, B], F32))
        RSTD = ctx.enter_context(nc.sbuf_tensor("RSTD", [T, B], F32))
        inverse_std(nc, "ln1", X, ST, MEAN, RSTD, dram["x"])
        self_attention(nc, psum, X, ST, MEAN, RSTD, dram)
        inverse_std(nc, "ln2", X, ST, MEAN, RSTD, None)
        cross_attention(nc, psum, X, ST, MEAN, RSTD, dram)
        inverse_std(nc, "ln3", X, ST, MEAN, RSTD, None)
        expert_ffn(nc, psum, X, ST, MEAN, RSTD, dram)
        stored = ctx.enter_context(nc.semaphore("stored"))
        block = ctx.enter_context(nc.Block())

        @block.sync
        def _(sp):
            for g in range(4):
                sp.dma_start(out[g * 16:(g + 1) * 16].rearrange("b t c -> t b c"),
                             X[:, g * 16 * C:(g + 1) * 16 * C].rearrange("t (b c) -> t b c", c=C)).then_inc(stored, 16)
            sp.wait_ge(stored, 64)


def kernel(**inputs):
    import numpy as np
    import concourse.bacc as bacc
    from concourse import mybir as mb
    from concourse.bass_utils import run_bass_kernel_spmd

    nc = bacc.Bacc("TRN2", target_bir_lowering=False, num_devices=1)
    arrays = {k: np.ascontiguousarray(v) for k, v in inputs.items()}
    for name, order in (("L0_xattn_Wq", (1, 0)), ("L0_xattn_Wk", (1, 0)), ("L0_xattn_Wv", (1, 0)),
                        ("L0_xattn_Wo", (1, 0)), ("L0_xattn_w1", (1, 0)), ("L0_xattn_w2", (1, 0)),
                        ("L0_xattn_w3", (1, 0)), ("L0_ffn_gate_w", (1, 0)), ("L0_ffn_w_gate", (1, 0)),
                        ("L0_ffn_w_up", (1, 0)), ("L0_ffn_w_down", (1, 0)), ("L0_ffn_A1", (1, 0, 2)),
                        ("L0_ffn_A3", (1, 0, 2)), ("L0_ffn_A2", (1, 0, 2)), ("L0_ffn_B1", (2, 0, 1)),
                        ("L0_ffn_B3", (2, 0, 1)), ("L0_ffn_B2", (2, 0, 1))):
        arrays[name] = np.ascontiguousarray(arrays[name].transpose(order))
    for name in [n for n, a in arrays.items() if a.ndim == 1]:
        as_column = name in ("L0_xattn_bq", "L0_xattn_bk", "L0_xattn_b1", "L0_xattn_b2")
        arrays[name] = arrays[name].reshape(-1, 1) if as_column else arrays[name].reshape(1, -1)
    eye = np.eye(128, dtype=np.float32)
    bf16, f16 = mb.dt.np(mb.dt.bfloat16), np.float16
    inv_freq = 1.0 / 10000.0 ** (np.arange(DK // 2, dtype=np.float32) / (DK // 2))
    angle = np.arange(T, dtype=np.float32)[:, None] * inv_freq.astype(np.float32)[None]
    per_head = lambda a: np.tile(np.repeat(a, 2, axis=1), (1, H))
    sign = np.tile(np.array([-1.0, 1.0]), C // 2)
    scale = DK ** -0.5
    cos, sin = per_head(np.cos(angle)), per_head(np.sin(angle)) * sign
    arrays.update(
        ident=eye, identb=eye.astype(bf16), ident16=eye.astype(f16),
        causal=np.tile(np.where(np.tril(np.ones((T, T), bool)), 0.0, -1e30), (1, JH)).astype(bf16),
        tri=np.ascontiguousarray(np.broadcast_to(np.tril(np.ones((8, 8), np.float32), -1), (128, 8, 8))),
        select=np.repeat(np.tile(np.eye(8, dtype=np.float32), (2, 1))[:, :, None], 128, axis=2),
        headsel=(np.arange(128)[:, None] // DK == np.arange(H)[None]).astype(np.float32),
        headmask=(np.arange(128)[:, None] // DK % JH == np.arange(JH)[None]).astype(np.float32),
        cos=np.concatenate([cos * scale, cos], 1).astype(np.float32),
        sin=np.concatenate([sin * scale, sin], 1).astype(np.float32),
    )
    dram = {n: nc.dram_tensor(n, a.shape, mb.dt.from_np(a.dtype), kind="ExternalInput").ap() for n, a in arrays.items()}
    out = nc.dram_tensor("out", (B, T, C), mb.dt.float32, kind="ExternalOutput").ap()
    program(nc, dram, out)
    r = run_bass_kernel_spmd(nc, [arrays], core_ids=[0])
    return r.results[0]["out"]
```

```python
import math

import concourse.bass as bass
from concourse import mybir
from contextlib import ExitStack

F32 = mybir.dt.float32
F32R = mybir.dt.float32r
BF16 = mybir.dt.bfloat16
F16 = mybir.dt.float16
ACT = mybir.ActivationFunctionType
ALU = mybir.AluOpType
AX = mybir.AxisListType

B, T, C, H, DK = 64, 128, 128, 16, 8
QUADS, JH = 4, 4
TC = 77
EPS = 1e-5
LOG_T_MIN, LOG_T_MAX = math.log(0.1), math.log(10.0)
LIFT = 15 * 0.6931471805599453


def need(eng, sem, value):
    if isinstance(value, int) and value <= 0:
        return
    eng.wait_ge(sem, value)


SELF_CONSTANTS = dict(
    ident=([128, 128], F32, "ident"), wqkv=([C, 3 * C], F32, "L0_attn_Wqkv"), cos=([128, 2 * C], F32, "cos"),
    sin=([128, 2 * C], F32, "sin"), identb=([128, 128], BF16, "identb"), causal=([128, JH * T], BF16, "causal"),
    headmask=([128, JH], F32, "headmask"), wo=([C, C], F32, "L0_attn_Wo"), bo=([1, C], F32, "L0_attn_bo"),
    ident16=([128, 128], F16, "ident16"))
CROSS_CONSTANTS = dict(
    ident=([128, 128], F32, "ident"), ident16=([128, 128], F16, "ident16"), headmask=([128, JH], F32, "headmask"),
    headsel=([128, H], F32, "headsel"), wq=([C, C], F32, "L0_xattn_Wq"), wk=([C, C], F32, "L0_xattn_Wk"),
    wv=([C, C], F32, "L0_xattn_Wv"), wo=([C, C], F32, "L0_xattn_Wo"), bq=([C, 1], F32, "L0_xattn_bq"),
    bk=([C, 1], F32, "L0_xattn_bk"), bv=([1, C], F32, "L0_xattn_bv"), bo=([1, C], F32, "L0_xattn_bo"),
    w1b=([128, 3, 64], F32, "L0_xattn_w1"), b1=([64, 1], F32, "L0_xattn_b1"), b2=([64, 1], F32, "L0_xattn_b2"),
    w2=([64, 64], F32, "L0_xattn_w2"), w3=([64, 1], F32, "L0_xattn_w3"), b3=([128, 1], F32, "L0_xattn_b3"))


def constant_tiles(nc, ctx, tag, constants):
    tiles = {name: ctx.enter_context(nc.sbuf_tensor(f"{tag}_{name}", shape, dt))
             for name, (shape, dt, _) in constants.items()}
    return tiles, ctx.enter_context(nc.semaphore(tag + "_loaded"))


def load_constants(sp, tiles, loaded, constants, dram):
    for name, (shape, _, source) in constants.items():
        src = dram[source]
        if name == "w1b":
            src = src.unsqueeze(0).to_broadcast(shape)
        if name == "b3":
            src = src.to_broadcast(shape)
        sp.dma_start(tiles[name][:], src).then_inc(loaded, 16)


def row_stats(nc, X, ST, b):
    return nc.vector.bn_stats(ST[:, bass.ts(b, 6)], X[:, bass.ts(b, C)])


def inverse_std(nc, tag, X, ST, MEAN, RSTD, with_stats, load_more=None):
    ctx = ExitStack()
    with ctx:
        ve = ctx.enter_context(nc.sbuf_tensor(tag + "_ve", [128, B], F32))
        root = ctx.enter_context(nc.sbuf_tensor(tag + "_root", [128, B], F32))
        y = ctx.enter_context(nc.sbuf_tensor(tag + "_y", [128, B], F32))
        t = ctx.enter_context(nc.sbuf_tensor(tag + "_t", [128, B], F32))
        loaded = [ctx.enter_context(nc.semaphore(f"{tag}_loaded{g}")) for g in range(4)]
        gathered = ctx.enter_context(nc.semaphore(tag + "_gathered"))
        step = ctx.enter_context(nc.semaphore(tag + "_step"))
        rooted = ctx.enter_context(nc.semaphore(tag + "_rooted"))
        block = ctx.enter_context(nc.Block())
        if with_stats is not None:
            @block.sync
            def _(sp):
                for g in range(4):
                    sp.dma_start(X[:, g * 16 * C:(g + 1) * 16 * C].rearrange("t (b c) -> t b c", c=C),
                                 with_stats[g * 16:(g + 1) * 16].rearrange("b t c -> t b c")).then_inc(loaded[g], 16)
                load_more(sp)

        @block.scalar
        def _(act):
            act.wait_ge(step, 3)
            nc.scalar.activation(root[:], ve[:], ACT.Sqrt).then_inc(rooted, 1)

        @block.vector
        def _(dve):
            if with_stats is not None:
                for g in range(4):
                    dve.wait_ge(loaded[g], 16)
                    for b in range(16 * g, 16 * g + 16):
                        row_stats(nc, X, ST, b).then_inc(gathered, 1)
                dve.wait_ge(gathered, B)
            s6 = ST[:].rearrange("t (b six) -> t b six", six=6)
            mean_even, m2_even, mean_odd, m2_odd = s6[:, :, 1], s6[:, :, 2], s6[:, :, 4], s6[:, :, 5]
            nc.vector.tensor_tensor(MEAN[:], mean_even, mean_odd, ALU.add)
            nc.vector.tensor_tensor(t[:], mean_even, mean_odd, ALU.subtract)
            nc.vector.tensor_tensor(ve[:], m2_even, m2_odd, ALU.add).then_inc(step, 1)
            dve.wait_ge(step, 1)
            nc.vector.tensor_scalar(MEAN[:], MEAN[:], 0.5, None, ALU.mult)
            nc.vector.tensor_tensor(t[:], t[:], t[:], ALU.mult)
            nc.vector.tensor_scalar(ve[:], ve[:], 1.0 / C, EPS, ALU.mult, ALU.add).then_inc(step, 1)
            dve.wait_ge(step, 2)
            nc.vector.scalar_tensor_tensor(ve[:], t[:], 0.25, ve[:], ALU.mult, ALU.add).then_inc(step, 1)
            dve.wait_ge(rooted, 1)
            nc.vector.reciprocal(y[:], root[:]).then_inc(step, 1)
            dve.wait_ge(step, 4)
            nc.vector.tensor_tensor(t[:], y[:], y[:], ALU.mult).then_inc(step, 1)
            dve.wait_ge(step, 5)
            nc.vector.tensor_tensor(t[:], t[:], ve[:], ALU.mult).then_inc(step, 1)
            dve.wait_ge(step, 6)
            nc.vector.tensor_scalar(t[:], t[:], -0.5, 1.5, ALU.mult, ALU.add).then_inc(step, 1)
            dve.wait_ge(step, 7)
            nc.vector.tensor_tensor(RSTD[:], t[:], y[:], ALU.mult).then_inc(step, 1)
            dve.wait_ge(step, 8)


def self_attention(nc, psum, X, ST, MEAN, RSTD, constants, loaded):
    ctx = ExitStack()
    with ctx:
        def sb(name, shape, dt=F32):
            return ctx.enter_context(nc.sbuf_tensor("sa_" + name, shape, dt))

        def sem(name):
            return ctx.enter_context(nc.semaphore("sa_" + name))

        S, L, TR, M, N = psum[0:3], psum[3], psum[4:6], psum[6], psum[7]

        ident, identb, ident16, causal, headmask, cos, sin, wqkv, wo, bo = (
            constants[n] for n in ("ident", "identb", "ident16", "causal", "headmask", "cos", "sin", "wqkv", "wo", "bo"))
        ones_row = sb("ones_row", [1, T])
        lift = sb("lift", [128, 1])
        ones_col = sb("ones_col", [128, H])
        xn = sb("xn", [128, 2, C])
        xnT = sb("xnT", [C, T])
        rope_a = sb("rope_a", [128, 2 * C])
        rope_b = sb("rope_b", [128, 2 * C])
        qk = sb("qk", [128, 2 * C])
        vf = sb("vf", [128, C])
        vr = sb("vr", [128, C])
        VS = sb("VS", [128, 2, H, 3, DK + 1], BF16)
        QT = sb("QT", [C, 2, QUADS, T])
        KM = sb("KM", [C, 2, JH, T])
        mx = sb("mx", [128, H])
        D = sb("D", [128, QUADS, JH * T])
        E = sb("E", [128, QUADS, JH * T])
        HI = sb("HI", [128, 2, QUADS, JH * T], F16)
        LO = sb("LO", [128, 2, QUADS, JH * T], F16)
        PT = sb("PT", [128, 2, 2 * JH * T], F16)
        o3 = sb("o3", [128, H, DK + 1])
        rinv = sb("rinv", [128, H])
        on = sb("on", [128, C])
        oT = sb("oT", [C, T])

        const_set = sem("const_set")
        rows_done = sem("rows_done")
        xn_ready = sem("xn_ready")
        xnT_ps = sem("xnT_ps")
        xnT_sb = sem("xnT_sb")
        qkv_ps = sem("qkv_ps")
        rope_part = sem("rope_part")
        qk_roped = sem("qk_roped")
        v_sb = sem("v_sb")
        v_part = sem("v_part")
        qkT_ps = sem("qkT_ps")
        qT_sb = sem("qT_sb")
        km_ready = sem("km_ready")
        s_ps = sem("s_ps")
        max_ready = sem("max_ready")
        d_ready = sem("d_ready")
        e_ready = sem("e_ready")
        hi_ready = sem("hi_ready")
        lo_ready = sem("lo_ready")
        tr_ps = sem("tr_ps")
        pt_act = sem("pt_act")
        pt_dve = sem("pt_dve")
        pv_ps = sem("pv_ps")
        o_sum = sem("o_sum")
        o_rinv = sem("o_rinv")
        o_norm = sem("o_norm")
        oT_ps = sem("oT_ps")
        oT_sb = sem("oT_sb")
        proj_ps = sem("proj_ps")
        x_done = sem("x_done")

        def steps(eng, step):
            for n in range(-3, 4):
                step(n, n % 2)
            with eng.Fori(2, B // 2 - 2) as i:
                step(2 * i, 0)
                step(2 * i + 1, 1)
            for n in range(B - 4, B + 2):
                step(n, n % 2)

        def real(b):
            return not isinstance(b, int) or 0 <= b < B

        block = ctx.enter_context(nc.Block())

        ALL_LOADED = 16 * len(SELF_CONSTANTS)

        @block.gpsimd
        def _(pool):
            nc.gpsimd.memset(VS[:], 0.0).then_inc(const_set, 1)
            pool.wait_ge(const_set, 1)
            nc.gpsimd.memset(VS[:, :, :, 0, DK:DK + 1], 1.0).then_inc(const_set, 1)
            nc.gpsimd.memset(ones_row[:], 1.0).then_inc(const_set, 1)
            nc.gpsimd.memset(lift[:], LIFT).then_inc(const_set, 1)
            nc.gpsimd.memset(ones_col[:], 1.0).then_inc(const_set, 1)
            nc.gpsimd.memset(QT[:], 0.0).then_inc(const_set, 1)
            pool.wait_ge(const_set, 6)

            def v_parts(b, p):
                v3 = vf[:].rearrange("k (h d) -> k h d", d=DK)
                r3 = vr[:].rearrange("k (h d) -> k h d", d=DK)
                one = ones_col[:].unsqueeze(2).to_broadcast([128, H, DK])
                need(pool, v_sb, b + 1)
                need(pool, pv_ps, QUADS * (b - 1))
                nc.gpsimd.tensor_tensor(VS[:, p, :, 0, 0:DK], v3, one, ALU.mult).then_inc(v_part, 1)
                pool.wait_ge(v_part, 5 * b + 1)
                nc.gpsimd.tensor_tensor(r3, v3, VS[:, p, :, 0, 0:DK], ALU.subtract).then_inc(v_part, 1)
                pool.wait_ge(v_part, 5 * b + 2)
                nc.gpsimd.tensor_tensor(VS[:, p, :, 1, 0:DK], r3, one, ALU.mult).then_inc(v_part, 1)
                pool.wait_ge(v_part, 5 * b + 3)
                nc.gpsimd.tensor_tensor(r3, r3, VS[:, p, :, 1, 0:DK], ALU.subtract).then_inc(v_part, 1)
                pool.wait_ge(v_part, 5 * b + 4)
                nc.gpsimd.tensor_tensor(VS[:, p, :, 2, 0:DK], r3, one, ALU.mult).then_inc(v_part, 1)

            def lo(b, g, p):
                pool.wait_ge(hi_ready, QUADS * b + g + 1)
                need(pool, tr_ps, QUADS * (b - 2) + g + 1)
                nc.gpsimd.tensor_tensor(LO[:, p, g, :], E[:, g, :], HI[:, p, g, :], ALU.subtract).then_inc(lo_ready, 1)

            def step(n, p):
                if real(n + 1):
                    lo(n + 1, 0, 1 - p)
                    v_parts(n + 1, 1 - p)
                    for g in range(1, QUADS):
                        lo(n + 1, g, 1 - p)

            steps(pool, step)

        @block.scalar
        def _(act):
            def xnT_copy(b):
                act.wait_ge(xnT_ps, b + 1)
                need(act, qkv_ps, b)
                nc.scalar.copy(xnT[:], M[:, 3 * C:4 * C]).then_inc(xnT_sb, 1)

            def v_copy(b):
                act.wait_ge(rope_part, 3 * (b + 1))
                need(act, v_part, 5 * b)
                nc.scalar.copy(vf[:], M[:, 2 * C:3 * C]).then_inc(v_sb, 1)

            def qT_copy(b, p):
                act.wait_ge(qkT_ps, b + 1)
                for g in range(QUADS):
                    rows = slice(32 * g, 32 * g + 32)
                    last = nc.scalar.copy(QT[rows, p, g, :], M[rows, 0:T])
                last.then_inc(qT_sb, 1)

            def exps(b, g, p):
                act.wait_ge(d_ready, QUADS * b + g + 1)
                need(act, lo_ready, QUADS * (b - 1) + g + 1)
                nc.scalar.activation(E[:, g, :], D[:, g, :], ACT.Exp, bias=lift[:]).then_inc(e_ready, 1)
                need(act, tr_ps, QUADS * (b - 2) + g + 1)
                nc.scalar.activation(HI[:, p, g, :], D[:, g, :], ACT.Exp, bias=lift[:]).then_inc(hi_ready, 1)

            def pt_copy(b, g):
                act.wait_ge(tr_ps, QUADS * b + g + 1)
                need(act, pv_ps, QUADS * b + g - 1)
                nc.scalar.copy(PT[:, 0, :], TR[0][:].bitcast(F16)).then_inc(pt_act, 1)

            def oT_copy(b):
                act.wait_ge(oT_ps, b + 1)
                need(act, proj_ps, b)
                nc.scalar.copy(oT[:], L[:, 0:T]).then_inc(oT_sb, 1)

            act.wait_ge(const_set, 6)

            def step(n, p):
                q = 1 - p
                if real(n + 1):
                    qT_copy(n + 1, q)
                if real(n - 2):
                    oT_copy(n - 2)
                if real(n):
                    pt_copy(n, 0)
                if real(n + 1):
                    exps(n + 1, 0, q)
                if real(n + 2):
                    xnT_copy(n + 2)
                if real(n + 1):
                    exps(n + 1, 1, q)
                if real(n):
                    pt_copy(n, 2)
                if real(n + 1):
                    exps(n + 1, 2, q)
                if real(n + 2):
                    v_copy(n + 2)
                if real(n + 1):
                    exps(n + 1, 3, q)

            steps(act, step)

        @block.vector
        def _(dve):
            def layernorm(b, p):
                xb = X[:, bass.ts(b, C)]
                need(dve, xnT_ps, b - 1)
                nc.vector.tensor_scalar(xn[:, p, :], xb, MEAN[:, bass.ds(b, 1)], RSTD[:, bass.ds(b, 1)],
                                        ALU.subtract, ALU.mult).then_inc(xn_ready, 1)

            def rope(b):
                dve.wait_ge(qkv_ps, b + 1)
                ps = M[:, 0:2 * C].rearrange("t (i two) -> t i two", two=2)
                rb = rope_b[:].rearrange("t (i two) -> t i two", two=2)
                sn = sin[:].rearrange("t (i two) -> t i two", two=2)
                nc.vector.tensor_tensor(rope_a[:], M[:, 0:2 * C], cos[:], ALU.mult).then_inc(rope_part, 1)
                nc.vector.tensor_tensor(rb[:, :, 0], ps[:, :, 1], sn[:, :, 0], ALU.mult).then_inc(rope_part, 1)
                nc.vector.tensor_tensor(rb[:, :, 1], ps[:, :, 0], sn[:, :, 1], ALU.mult).then_inc(rope_part, 1)
                dve.wait_ge(rope_part, 3 * b + 3)
                need(dve, qkT_ps, b)
                nc.vector.tensor_tensor(qk[:], rope_a[:], rope_b[:], ALU.add).then_inc(qk_roped, 1)

            def km(b, p):
                dve.wait_ge(qT_sb, b + 1)
                nc.vector.tensor_tensor(KM[:, p], M[:, T:2 * T].unsqueeze(1).to_broadcast([C, JH, T]),
                                        headmask[:].unsqueeze(2).to_broadcast([C, JH, T]),
                                        ALU.mult).then_inc(km_ready, 1)

            def sub(b, g):
                dve.wait_ge(s_ps, QUADS * b + g + 1)
                s3 = S[g % 3][:].rearrange("q (j k) -> q j k", j=JH)
                m4 = mx[:, JH * g:JH * g + JH]
                nc.vector.tensor_reduce(m4, s3, AX.X, ALU.max).then_inc(max_ready, 1)
                dve.wait_ge(max_ready, QUADS * b + g + 1)
                need(dve, hi_ready, QUADS * (b - 1) + g + 1)
                nc.vector.tensor_tensor(D[:, g, :].rearrange("q (j k) -> q j k", j=JH), s3,
                                        m4.unsqueeze(2).to_broadcast([128, JH, T]),
                                        ALU.subtract).then_inc(d_ready, 1)

            def pt_copy(b, g):
                dve.wait_ge(tr_ps, QUADS * b + g + 1)
                need(dve, pv_ps, QUADS * b + g - 1)
                nc.vector.tensor_copy(PT[:, 1, :], TR[1][:].bitcast(F16)).then_inc(pt_dve, 1)

            def norm(b):
                dve.wait_ge(pv_ps, QUADS * (b + 1))
                nc.vector.tensor_reduce(o3[:], N[:, 0:H * 27].rearrange("q (h s e) -> q h e s", h=H, s=3), AX.X,
                                        ALU.add).then_inc(o_sum, 1)
                dve.wait_ge(o_sum, b + 1)
                nc.vector.reciprocal(rinv[:], o3[:, :, DK]).then_inc(o_rinv, 1)
                dve.wait_ge(o_rinv, b + 1)
                need(dve, oT_ps, b)
                nc.vector.tensor_tensor(on[:].rearrange("q (h d) -> q h d", d=DK), o3[:, :, 0:DK],
                                        rinv[:].unsqueeze(2).to_broadcast([128, H, DK]),
                                        ALU.mult).then_inc(o_norm, 1)

            def residual(b):
                dve.wait_ge(proj_ps, b + 1)
                xb = X[:, bass.ts(b, C)]
                nc.vector.tensor_tensor(xb, xb, L[:, T:T + C], ALU.add).then_inc(x_done, 1)

            def stats(b):
                row_stats(nc, X, ST, b).then_inc(rows_done, 1)

            dve.wait_ge(loaded, ALL_LOADED)

            def step(n, p):
                if real(n + 1):
                    km(n + 1, 1 - p)
                if real(n - 1):
                    norm(n - 1)
                if real(n + 1):
                    sub(n + 1, 0)
                if real(n - 2):
                    residual(n - 2)
                if real(n + 1):
                    need(dve, x_done, n - 1)
                    sub(n + 1, 1)
                if real(n):
                    pt_copy(n, 1)
                if real(n - 2):
                    if isinstance(n, int):
                        dve.wait_ge(x_done, n - 1)
                    stats(n - 2)
                if real(n + 1):
                    sub(n + 1, 2)
                    sub(n + 1, 3)
                if real(n + 2):
                    rope(n + 2)
                if real(n):
                    pt_copy(n, 3)
                if real(n + 3):
                    layernorm(n + 3, 1 - p)

            steps(dve, step)
            dve.wait_ge(rows_done, B)

        @block.tensor
        def _(pe):
            mm, tr = nc.tensor.matmul, nc.tensor.transpose

            def xn_transpose(b, p):
                pe.wait_ge(xn_ready, b + 1)
                need(pe, qT_sb, b)
                need(pe, km_ready, b)
                tr(M[:, 3 * C:4 * C], xn[:, p, :], ident[:]).then_inc(xnT_ps, 1)

            def qkv(b):
                pe.wait_ge(xnT_sb, b + 1)
                mm(M[:, 0:3 * C], xnT[:], wqkv[:], start=True, stop=True).then_inc(qkv_ps, 1)

            def qk_transpose(b):
                pe.wait_ge(qk_roped, b + 1)
                pe.wait_ge(v_sb, b + 1)
                tr(M[:, 0:T], qk[:, 0:C], ident[:])
                tr(M[:, T:2 * T], qk[:, C:2 * C], ident[:]).then_inc(qkT_ps, 1)

            def mask(b, g):
                need(pe, d_ready, (QUADS * b + 1, QUADS * b, QUADS * (b - 1) + 2, QUADS * (b - 1) + 3)[(g + 1) % QUADS])
                mm(S[g % 3][:], identb[:], causal[:], start=True, stop=False)

            def scores(b, g, p):
                if g == 0:
                    pe.wait_ge(qT_sb, b + 1)
                    pe.wait_ge(km_ready, b + 1)
                mm(S[g % 3][:], QT[:, p, g, :], KM[:, p, :, :].rearrange("c j k -> c (j k)"),
                   start=False, stop=True).then_inc(s_ps, 1)

            def p_transpose(b, g, p):
                pe.wait_ge(lo_ready, QUADS * b + g + 1)
                free = pt_act if g % 2 == 0 else pt_dve
                need(pe, free, 2 * b + g // 2)
                t = TR[g % 2][:].bitcast(F16)
                for part, src in enumerate((HI, LO)):
                    for j in range(JH):
                        n = part * JH + j
                        last = tr(t[:, n * T:(n + 1) * T], src[:, p, g, j * T:(j + 1) * T], ident16[:])
                last.then_inc(tr_ps, 1)

            def pv(b, g, p):
                if g == 0:
                    pe.wait_ge(v_part, 5 * b + 5)
                    need(pe, o_sum, b)
                pe.wait_ge(pt_act if g % 2 == 0 else pt_dve, 2 * b + g // 2 + 1)
                for j in range(JH):
                    h = JH * g + j
                    vs = VS[:, p, h, :, :].rearrange("k s e -> k (s e)")
                    mm(N[:, h * 27:h * 27 + 27], PT[:, g % 2, j * T:(j + 1) * T], vs, start=(h == 0), stop=False,
                       skip_group_check=True)
                    last = mm(N[:, h * 27:h * 27 + 18], PT[:, g % 2, (JH + j) * T:(JH + j + 1) * T], vs[:, 0:18],
                              start=False, stop=(h == H - 1), skip_group_check=True)
                last.then_inc(pv_ps, 1)

            def o_transpose(b):
                pe.wait_ge(o_norm, b + 1)
                need(pe, x_done, b)
                tr(L[:, 0:T], on[:], ident[:]).then_inc(oT_ps, 1)

            def project(b):
                pe.wait_ge(oT_sb, b + 1)
                mm(L[:, T:T + C], ones_row[:], bo[:], start=True, stop=False)
                mm(L[:, T:T + C], oT[:], wo[:], start=False, stop=True).then_inc(proj_ps, 1)

            pe.wait_ge(loaded, ALL_LOADED)
            pe.wait_ge(const_set, 6)

            def step(n, p):
                q = 1 - p
                now, after, then, prev = real(n), real(n + 1), real(n + 2), real(n - 1)
                if after:
                    for g in range(3):
                        mask(n + 1, g)
                    qk_transpose(n + 1)
                if prev:
                    pv(n - 1, 2, q)
                    pv(n - 1, 3, q)
                if now:
                    p_transpose(n, 0, p)
                if after:
                    scores(n + 1, 0, q)
                if real(n - 2):
                    project(n - 2)
                if after:
                    scores(n + 1, 1, q)
                if now:
                    p_transpose(n, 1, p)
                if then:
                    xn_transpose(n + 2, p)
                if after:
                    scores(n + 1, 2, q)
                if now:
                    pv(n, 0, p)
                    p_transpose(n, 2, p)
                if after:
                    mask(n + 1, 3)
                    scores(n + 1, 3, q)
                if then:
                    qkv(n + 2)
                if now:
                    pv(n, 1, p)
                    p_transpose(n, 3, p)
                if prev:
                    o_transpose(n - 1)

            steps(pe, step)


def cross_attention(nc, psum, X, ST, MEAN, RSTD, constants, loaded, dram):
    GROUP = 8
    SLOTS = 2 * GROUP
    ROUNDS = B // GROUP
    W = JH * TC
    R8 = float(DK) ** 0.5
    ctx = ExitStack()
    with ctx:
        def sb(name, shape, dt=F32):
            return ctx.enter_context(nc.sbuf_tensor("xa_" + name, shape, dt))

        def sem(name):
            return ctx.enter_context(nc.semaphore("xa_" + name))

        S, BT, BQ, TR, BO, BP = psum[0:2], psum[2], psum[3], psum[4:6], psum[6], psum[7]

        ident, ident16, headmask, headsel, wq, wk, wv, wo, bq, bk, bv, bo = (
            constants[n] for n in ("ident", "ident16", "headmask", "headsel", "wq", "wk", "wv", "wo", "bq", "bk",
                                   "bv", "bo"))
        w1b, w2, w3, b1, b2, b3 = (constants[n] for n in ("w1b", "w2", "w3", "b1", "b2", "b3"))
        w1s = sb("w1s", [128, 3, 64])
        w2p = sb("w2p", [64, 128])
        w3r = sb("w3r", [64, 128])
        ones_row = sb("ones_row", [1, T])
        ones_col = sb("ones_col", [128, H])
        lift = sb("lift", [128, 1])
        cx = sb("cx", [TC, 2, C])
        xn = sb("xn", [128, 2, C])
        xcT = sb("xcT", [C, T + TC])
        QF = sb("QF", [C, T])
        QT = sb("QT", [C, 2, QUADS, T])
        KT = sb("KT", [C, TC])
        KM = sb("KM", [C, 2, JH, TC])
        vf = sb("vf", [TC, C])
        vr = sb("vr", [TC, C])
        VT = sb("VT", [TC, H * 27], BF16)
        VS = sb("VS", [TC, SLOTS * H * 27], BF16)
        qsum = sb("qsum", [C, 2])
        ksum = sb("ksum", [C, 2])
        mx = sb("mx", [128, 2, H])
        D = sb("D", [128, SLOTS * QUADS * W])
        E1 = sb("E1", [128, QUADS * W])
        E2 = sb("E2", [128, QUADS * W])
        zsum = sb("zsum", [128, 3, H])
        FEAT = sb("FEAT", [128, 3, GROUP * H])
        h1 = sb("h1", [64, GROUP * H])
        h2 = sb("h2", [64, GROUP * H])
        lt = sb("lt", [128, GROUP * H])
        CF = sb("CF", [128, GROUP * H])
        DC = sb("DC", [128, QUADS, W])
        E = sb("E", [128, QUADS, W])
        HI = sb("HI", [128, 2, QUADS, W], F16)
        LO = sb("LO", [128, 2, QUADS, W], F16)
        PT = sb("PT", [TC, 2, 2 * JH * T], F16)
        o3 = sb("o3", [128, H, DK + 1])
        rinv = sb("rinv", [128, H])
        on = sb("on", [128, C])
        oT = sb("oT", [C, T])

        const_set = sem("const_set")
        prepared = sem("prepared")
        cx_loaded = [sem("cx_loaded0"), sem("cx_loaded1")]
        xn_ready = sem("xn_ready")
        xcT_ps = sem("xcT_ps")
        xcT_sb = sem("xcT_sb")
        qkv_ps = sem("qkv_ps")
        q_sb = sem("q_sb")
        k_sb = sem("k_sb")
        qt_ready = sem("qt_ready")
        v_sb = sem("v_sb")
        km_ready = sem("km_ready")
        v_part = sem("v_part")
        v_kept = sem("v_kept")
        feat_qk = sem("feat_qk")
        s_ps = sem("s_ps")
        max_ready = sem("max_ready")
        d_ready = sem("d_ready")
        e1_ready = sem("e1_ready")
        e2_ready = sem("e2_ready")
        z_step = sem("z_step")
        feat_ready = sem("feat_ready")
        mlp_ps = sem("mlp_ps")
        mlp_act = sem("mlp_act")
        clip_step = sem("clip_step")
        cf_ready = sem("cf_ready")
        dc_ready = sem("dc_ready")
        hi_ready = sem("hi_ready")
        lo_ready = sem("lo_ready")
        tr_ps = sem("tr_ps")
        pt_act = sem("pt_act")
        pt_dve = sem("pt_dve")
        pv_ps = sem("pv_ps")
        o_sum = sem("o_sum")
        o_rinv = sem("o_rinv")
        o_norm = sem("o_norm")
        oT_ps = sem("oT_ps")
        oT_sb = sem("oT_sb")
        proj_ps = sem("proj_ps")
        x_done = sem("x_done")
        rows_done = sem("rows_done")

        ALL_LOADED = 16 * len(CROSS_CONSTANTS)

        def real(b, on=True):
            return 0 <= b < B if isinstance(b, int) else on

        def rounds(eng, step, mlp):
            def alone(r, steps):
                for n in steps:
                    step(r, n, n % 2, (n - 1) % GROUP, True, True)

            def pairs(r, first, last, early, late):
                with eng.Fori(first, last) as j:
                    for k in range(2):
                        step(r, GROUP * r + 1 + 2 * j + k, 1 - k, 2 * j + k, early, late)

            alone(0, (-2, -1, 0, 1, 2))
            pairs(0, 1, 4, True, False)
            mlp(0)
            alone(1, (9, 10, 11, 12, 13, 14, 15, 16))
            mlp(1)
            with eng.Fori(2, ROUNDS - 1) as r:
                pairs(r, 0, 4, True, True)
                mlp(r)
            pairs(ROUNDS - 1, 0, 2, True, True)
            alone(ROUNDS - 1, (B - 3, B - 2, B - 1, B))
            mlp(ROUNDS - 1)
            pairs(ROUNDS, 0, 4, False, True)
            alone(ROUNDS, range(B + 9, B + 13))

        block = ctx.enter_context(nc.Block())

        @block.sync
        def _(sp):
            ctx_d = dram["ctx_1024"]

            def load(b, k):
                sp.dma_start(cx[:, k, :], ctx_d[bass.ds(b, 1)].rearrange("b t c -> (b t) c")).then_inc(cx_loaded[k], 16)

            load(0, 0)
            load(1, 1)
            with sp.Fori(1, B // 2) as i:
                for k in range(2):
                    sp.wait_ge(xcT_ps, 2 * i + k - 1)
                    load(2 * i + k, k)

        @block.gpsimd
        def _(pool):
            nc.gpsimd.memset(VT[:], 0.0).then_inc(const_set, 1)
            pool.wait_ge(const_set, 1)
            nc.gpsimd.memset(VT[:].rearrange("k (h s e) -> k h s e", h=H, s=3)[:, :, 0, DK:DK + 1], 1.0).then_inc(const_set, 1)
            nc.gpsimd.memset(ones_row[:], 1.0).then_inc(const_set, 1)
            nc.gpsimd.memset(lift[:], LIFT).then_inc(const_set, 1)
            nc.gpsimd.memset(ones_col[:], 1.0).then_inc(const_set, 1)
            nc.gpsimd.memset(QT[:], 0.0).then_inc(const_set, 1)
            pool.wait_ge(const_set, 6)
            pool.wait_ge(loaded, ALL_LOADED)

            def km(b, p):
                need(pool, k_sb, b + 1)
                need(pool, s_ps, QUADS * (b - 1))
                nc.gpsimd.tensor_tensor(KM[:, p], KT[:].unsqueeze(1).to_broadcast([C, JH, TC]),
                                        headmask[:].unsqueeze(2).to_broadcast([C, JH, TC]),
                                        ALU.mult).then_inc(km_ready, 1)

            def v_parts(b):
                vs = VT[:].rearrange("k (h s e) -> k h s e", h=H, s=3)
                v3 = vf[:].rearrange("k (h d) -> k h d", d=DK)
                r3 = vr[:].rearrange("k (h d) -> k h d", d=DK)
                one = ones_col[0:TC].unsqueeze(2).to_broadcast([TC, H, DK])
                need(pool, v_sb, b + 1)
                need(pool, v_kept, b)
                nc.gpsimd.tensor_tensor(vs[:, :, 0, 0:DK], v3, one, ALU.mult).then_inc(v_part, 1)
                pool.wait_ge(v_part, 5 * b + 1)
                nc.gpsimd.tensor_tensor(r3, v3, vs[:, :, 0, 0:DK], ALU.subtract).then_inc(v_part, 1)
                pool.wait_ge(v_part, 5 * b + 2)
                nc.gpsimd.tensor_tensor(vs[:, :, 1, 0:DK], r3, one, ALU.mult).then_inc(v_part, 1)
                pool.wait_ge(v_part, 5 * b + 3)
                nc.gpsimd.tensor_tensor(r3, r3, vs[:, :, 1, 0:DK], ALU.subtract).then_inc(v_part, 1)
                pool.wait_ge(v_part, 5 * b + 4)
                nc.gpsimd.tensor_tensor(vs[:, :, 2, 0:DK], r3, one, ALU.mult).then_inc(v_part, 1)

            def lo(r, b, g, p):
                pool.wait_ge(hi_ready, QUADS * b + g + 1)
                need(pool, tr_ps, QUADS * (b - 2) + g + 1)
                if g == 0:
                    need(pool, cf_ready, r)
                nc.gpsimd.tensor_tensor(LO[:, p, g, :], E[:, g, :], HI[:, p, g, :], ALU.subtract).then_inc(lo_ready, 1)

            def scaled(r, b, s, g):
                if isinstance(b, int):
                    pool.wait_ge(cf_ready, r)
                cf = CF[:, bass.ds(s * H + JH * g, JH)].unsqueeze(2).to_broadcast([128, JH, TC])
                d = D[:, bass.ds((b % SLOTS) * (QUADS * W) + g * W, W)].rearrange("q (j k) -> q j k", j=JH)
                nc.gpsimd.tensor_tensor(DC[:, g, :].rearrange("q (j k) -> q j k", j=JH), d, cf,
                                        ALU.mult).then_inc(dc_ready, 1)

            def step(r, n, p, s, early, late):
                for g in range(QUADS):
                    if real(n - 10, late):
                        lo(r, n - 10, g, p)
                    if real(n - 9, late):
                        scaled(r, n - 9, s, g)
                    if g == 1 and real(n + 1, early):
                        km(n + 1, 1 - p)
                        v_parts(n + 1)

            rounds(pool, step, lambda r: None)

        @block.scalar
        def _(act):
            act.wait_ge(const_set, 6)
            act.wait_ge(loaded, ALL_LOADED)

            def xcT_copy(b):
                act.wait_ge(xcT_ps, b + 1)
                need(act, qkv_ps, b)
                nc.scalar.copy(xcT[:], BT[:, 0:T + TC]).then_inc(xcT_sb, 1)

            def qkv_copy(b, p):
                act.wait_ge(qkv_ps, b + 1)
                need(act, feat_qk, b - 1)
                need(act, qt_ready, b)
                nc.scalar.activation(QF[:], BQ[:, 0:T], ACT.Identity, bias=bq[:],
                                     accum_out=qsum[:, p:p + 1]).then_inc(q_sb, 1)
                need(act, km_ready, b)
                nc.scalar.activation(KT[:], BQ[:, T:T + TC], ACT.Identity, bias=bk[:],
                                     accum_out=ksum[:, p:p + 1]).then_inc(k_sb, 1)
                need(act, v_part, 5 * b)
                nc.scalar.copy(vf[:], BQ[0:TC, 2 * T:2 * T + C]).then_inc(v_sb, 1)

            def exps(b, g, p):
                act.wait_ge(dc_ready, QUADS * b + g + 1)
                need(act, tr_ps, QUADS * (b - 2) + g + 1)
                nc.scalar.activation(E[:, g, :], DC[:, g, :], ACT.Exp, bias=lift[:])
                nc.scalar.activation(HI[:, p, g, :], DC[:, g, :], ACT.Exp, bias=lift[:]).then_inc(hi_ready, 1)

            def pt_copy(b, g):
                act.wait_ge(tr_ps, QUADS * b + g + 1)
                need(act, pv_ps, QUADS * b + g - 1)
                nc.scalar.copy(PT[:, 0, :], TR[0][0:TC].bitcast(F16)).then_inc(pt_act, 1)

            def exp_e(b):
                act.wait_ge(d_ready, QUADS * b + QUADS)
                need(act, z_step, 5 * b)
                d = D[:, bass.ds((b % SLOTS) * (QUADS * W), QUADS * W)]
                nc.scalar.activation(E1[:], d, ACT.Exp, scale=1.0 / R8).then_inc(e1_ready, 1)

            def square_e(b):
                act.wait_ge(e1_ready, b + 1)
                nc.scalar.activation(E2[:], E1[:], ACT.Square).then_inc(e2_ready, 1)

            def oT_copy(b):
                act.wait_ge(oT_ps, b + 1)
                need(act, proj_ps, b)
                nc.scalar.copy(oT[:], BP[:, 0:T]).then_inc(oT_sb, 1)

            def step(r, n, p, s, early, late):
                features = real(n - 1, early)
                if real(n - 13, late):
                    oT_copy(n - 13)
                if real(n - 11, late):
                    pt_copy(n - 11, 0)
                if features:
                    exp_e(n - 1)
                if real(n - 10, late):
                    exps(n - 10, 0, p)
                if real(n + 1, early):
                    xcT_copy(n + 1)
                if real(n - 10, late):
                    exps(n - 10, 1, p)
                if features:
                    square_e(n - 1)
                if real(n - 10, late):
                    exps(n - 10, 2, p)
                if real(n + 1, early):
                    qkv_copy(n + 1, 1 - p)
                if real(n - 11, late):
                    pt_copy(n - 11, 2)
                if real(n - 10, late):
                    exps(n - 10, 3, p)

            def mlp(r):
                act.wait_ge(mlp_ps, 3 * r + 1)
                nc.scalar.activation(h1[:], BT[0:64, 0:128], ACT.Gelu, bias=b1[:]).then_inc(mlp_act, 1)
                act.wait_ge(mlp_ps, 3 * r + 2)
                nc.scalar.activation(h2[:], BT[0:64, 128:256], ACT.Gelu, bias=b2[:]).then_inc(mlp_act, 1)
                act.wait_ge(clip_step, 2 * r + 2)
                need(act, dc_ready, QUADS * GROUP * r)
                nc.scalar.activation(CF[:], lt[:], ACT.Exp, scale=-1.0).then_inc(mlp_act, 1)

            rounds(act, step, mlp)

        @block.vector
        def _(dve):
            dve.wait_ge(loaded, ALL_LOADED)
            for f, scale in enumerate((1.0 / (T * TC * R8), 1.0 / (T * R8), 1.0 / T)):
                nc.vector.tensor_scalar(w1s[:, f, :], w1b[:, f, :], scale, None, ALU.mult).then_inc(prepared, 1)
            nc.vector.memset(w2p[:, 64:128], 0.0).then_inc(prepared, 1)
            nc.vector.tensor_copy(w2p[:, 0:64], w2[:]).then_inc(prepared, 1)
            nc.vector.tensor_copy(w3r[:], w3[:].to_broadcast([64, 128])).then_inc(prepared, 1)

            def layernorm(b, p):
                need(dve, xcT_ps, b - 1)
                nc.vector.tensor_scalar(xn[:, p, :], X[:, bass.ts(b, C)], MEAN[:, bass.ds(b, 1)],
                                        RSTD[:, bass.ds(b, 1)], ALU.subtract, ALU.mult).then_inc(xn_ready, 1)

            def q_quads(b, p):
                dve.wait_ge(q_sb, b + 1)
                need(dve, s_ps, QUADS * (b - 1))
                for g in range(QUADS):
                    rows = slice(32 * g, 32 * g + 32)
                    last = nc.vector.tensor_copy(QT[rows, p, g, :], QF[rows])
                last.then_inc(qt_ready, 1)

            def sub(b, p, g):
                dve.wait_ge(s_ps, QUADS * b + g + 1)
                s3 = S[g % 2][:, 0:W].rearrange("q (j k) -> q j k", j=JH)
                m4 = mx[:, p, JH * g:JH * g + JH]
                nc.vector.tensor_reduce(m4, s3, AX.X, ALU.max).then_inc(max_ready, 1)
                dve.wait_ge(max_ready, QUADS * b + g + 1)
                nc.vector.tensor_tensor(D[:, bass.ds((b % SLOTS) * (QUADS * W) + g * W, W)]
                                        .rearrange("q (j k) -> q j k", j=JH),
                                        s3, m4.unsqueeze(2).to_broadcast([128, JH, TC]),
                                        ALU.subtract).then_inc(d_ready, 1)

            def keep_v(b):
                dve.wait_ge(v_part, 5 * b + 5)
                nc.vector.tensor_scalar(VS[:, bass.ds((b % SLOTS) * (H * 27), H * 27)], VT[:], 1.0, None,
                                        ALU.mult).then_inc(v_kept, 1)

            def pt_copy(b, g):
                dve.wait_ge(tr_ps, QUADS * b + g + 1)
                need(dve, pv_ps, QUADS * b + g - 1)
                nc.vector.tensor_copy(PT[:, 1, :], TR[1][0:TC].bitcast(F16)).then_inc(pt_dve, 1)

            def norm(b):
                dve.wait_ge(pv_ps, QUADS * (b + 1))
                nc.vector.tensor_reduce(o3[:], BO[:, 0:H * 27].rearrange("q (h s e) -> q h e s", h=H, s=3), AX.X,
                                        ALU.add).then_inc(o_sum, 1)
                dve.wait_ge(o_sum, b + 1)
                nc.vector.reciprocal(rinv[:], o3[:, :, DK]).then_inc(o_rinv, 1)
                dve.wait_ge(o_rinv, b + 1)
                need(dve, oT_ps, b)
                nc.vector.tensor_tensor(on[:].rearrange("q (h d) -> q h d", d=DK), o3[:, :, 0:DK],
                                        rinv[:].unsqueeze(2).to_broadcast([128, H, DK]),
                                        ALU.mult).then_inc(o_norm, 1)

            def residual(b):
                dve.wait_ge(proj_ps, b + 1)
                xb = X[:, bass.ts(b, C)]
                nc.vector.tensor_tensor(xb, xb, BP[:, T:T + C], ALU.add).then_inc(x_done, 1)

            e4 = lambda t: t[:].rearrange("q (h k) -> q h k", k=TC)

            def sum_e(b, p, s):
                dve.wait_ge(q_sb, b + 1)
                dve.wait_ge(k_sb, b + 1)
                nc.vector.scalar_tensor_tensor(FEAT[:, 0, bass.ds(s * H, H)], headsel[:], qsum[:, p:p + 1],
                                               ksum[:, p:p + 1].to_broadcast([128, H]), ALU.mult,
                                               ALU.mult).then_inc(feat_qk, 1)
                nc.vector.tensor_scalar(FEAT[:, 1, bass.ds(s * H, H)], mx[:, p, :], 1.0, None, ALU.mult).then_inc(feat_ready, 1)
                dve.wait_ge(e1_ready, b + 1)
                nc.vector.tensor_reduce(zsum[:, 0, :], e4(E1), AX.X, ALU.add).then_inc(z_step, 1)

            def sum_e2(b, s):
                dve.wait_ge(z_step, 5 * b + 1)
                nc.vector.reciprocal(zsum[:, 1, :], zsum[:, 0, :]).then_inc(z_step, 1)
                dve.wait_ge(e2_ready, b + 1)
                nc.vector.tensor_reduce(zsum[:, 2, :], e4(E2), AX.X, ALU.add).then_inc(z_step, 1)
                dve.wait_ge(z_step, 5 * b + 3)
                nc.vector.tensor_tensor(zsum[:, 2, :], zsum[:, 2, :], zsum[:, 1, :], ALU.mult).then_inc(z_step, 1)
                dve.wait_ge(z_step, 5 * b + 4)
                nc.vector.tensor_tensor(zsum[:, 2, :], zsum[:, 2, :], zsum[:, 1, :], ALU.mult).then_inc(z_step, 1)
                dve.wait_ge(z_step, 5 * b + 5)
                nc.vector.tensor_scalar(FEAT[:, 2, bass.ds(s * H, H)], zsum[:, 2, :], -1.0 / TC, 1.0 / (TC - 1),
                                        ALU.add, ALU.mult).then_inc(feat_ready, 1)

            def step(r, n, p, s, early, late):
                scores, features = real(n, early), real(n - 1, early)
                if real(n - 12, late):
                    norm(n - 12)
                if scores:
                    sub(n, p, 0)
                if real(n - 13, late):
                    residual(n - 13)
                if scores:
                    sub(n, p, 1)
                    keep_v(n)
                if real(n - 13, late):
                    dve.wait_ge(x_done, n - 12)
                if real(n - 11, late):
                    pt_copy(n - 11, 1)
                if real(n - 13, late):
                    row_stats(nc, X, ST, n - 13).then_inc(rows_done, 1)
                if features:
                    sum_e(n - 1, 1 - p, s)
                if scores:
                    sub(n, p, 2)
                    sub(n, p, 3)
                if real(n - 11, late):
                    pt_copy(n - 11, 3)
                if real(n + 1, early):
                    q_quads(n + 1, 1 - p)
                if features:
                    sum_e2(n - 1, s)
                if real(n + 2, early):
                    layernorm(n + 2, p)

            def mlp(r):
                dve.wait_ge(mlp_ps, 3 * r + 3)
                nc.vector.tensor_scalar(lt[:], BT[:, 256:384], b3[:], LOG_T_MIN, ALU.add, ALU.max).then_inc(clip_step, 1)
                dve.wait_ge(clip_step, 2 * r + 1)
                nc.vector.tensor_scalar(lt[:], lt[:], LOG_T_MAX, None, ALU.min).then_inc(clip_step, 1)
                dve.wait_ge(mlp_act, 3 * r + 3)
                nc.vector.tensor_scalar(CF[:], CF[:], 0.5, None, ALU.mult).then_inc(cf_ready, 1)

            rounds(dve, step, mlp)
            dve.wait_ge(rows_done, B)

        @block.tensor
        def _(pe):
            mm, tr = nc.tensor.matmul, nc.tensor.transpose
            pe.wait_ge(const_set, 6)
            pe.wait_ge(loaded, ALL_LOADED)
            pe.wait_ge(prepared, 6)

            def scores(b, g, p):
                need(pe, d_ready, QUADS * b + g - 1)
                if g == 0:
                    pe.wait_ge(qt_ready, b + 1)
                    pe.wait_ge(km_ready, b + 1)
                mm(S[g % 2][:, 0:W], QT[:, p, g, :], KM[:, p, :, :].rearrange("c j k -> c (j k)"),
                   start=True, stop=True).then_inc(s_ps, 1)

            def xc_transpose(r, b, p):
                pe.wait_ge(xn_ready, b + 1)
                need(pe, xcT_sb, b)
                need(pe, clip_step, 2 * r - 1)
                tr(BT[:, 0:T], xn[:, p, :], ident[:])
                pe.wait_ge(cx_loaded[p], 8 * (b - p) + 16)
                tr(BT[:, T:T + TC], cx[:, p, :], ident[0:TC, 0:TC]).then_inc(xcT_ps, 1)

            def qkv(b):
                pe.wait_ge(xcT_sb, b + 1)
                need(pe, v_sb, b)
                mm(BQ[:, 0:T], wq[:], xcT[:, 0:T], start=True, stop=True)
                mm(BQ[:, T:T + TC], wk[:], xcT[:, T:T + TC], start=True, stop=True)
                mm(BQ[0:TC, 2 * T:2 * T + C], ones_row[:, 0:TC], bv[:], start=True, stop=False)
                mm(BQ[0:TC, 2 * T:2 * T + C], xcT[:, T:T + TC], wv[:], start=False, stop=True).then_inc(qkv_ps, 1)

            def p_transpose(b, g, p):
                pe.wait_ge(lo_ready, QUADS * b + g + 1)
                need(pe, pt_act if g % 2 == 0 else pt_dve, 2 * b + g // 2)
                t = TR[g % 2][0:TC].bitcast(F16)
                for part, src in enumerate((HI, LO)):
                    for j in range(JH):
                        n = part * JH + j
                        last = tr(t[:, n * T:(n + 1) * T], src[:, p, g, j * TC:(j + 1) * TC], ident16[:])
                last.then_inc(tr_ps, 1)

            def pv(b, g):
                pe.wait_ge(pt_act if g % 2 == 0 else pt_dve, 2 * b + g // 2 + 1)
                if g == 0:
                    pe.wait_ge(v_kept, b + 1)
                    need(pe, o_sum, b)
                slot = (b % SLOTS) * (H * 27)
                for j in range(JH):
                    h = JH * g + j
                    mm(BO[:, h * 27:h * 27 + 27], PT[:, g % 2, j * T:(j + 1) * T], VS[:, bass.ds(slot + h * 27, 27)],
                       start=(h == 0), stop=False, skip_group_check=True)
                    last = mm(BO[:, h * 27:h * 27 + 18], PT[:, g % 2, (JH + j) * T:(JH + j + 1) * T],
                              VS[:, bass.ds(slot + h * 27, 18)], start=False, stop=(h == H - 1), skip_group_check=True)
                last.then_inc(pv_ps, 1)

            def o_transpose(b):
                pe.wait_ge(o_norm, b + 1)
                need(pe, x_done, b)
                tr(BP[:, 0:T], on[:], ident[:]).then_inc(oT_ps, 1)

            def project(b):
                pe.wait_ge(oT_sb, b + 1)
                mm(BP[:, T:T + C], ones_row[:], bo[:], start=True, stop=False)
                mm(BP[:, T:T + C], oT[:], wo[:], start=False, stop=True).then_inc(proj_ps, 1)

            def step(r, n, p, s, early, late):
                now, out, late_out, then = real(n, early), real(n - 11, late), real(n - 12, late), real(n + 1, early)
                if now:
                    scores(n, 0, p)
                    scores(n, 1, p)
                if late_out:
                    pv(n - 12, 2)
                    pv(n - 12, 3)
                if out:
                    p_transpose(n - 11, 0, 1 - p)
                if real(n - 13, late):
                    project(n - 13)
                if out:
                    p_transpose(n - 11, 1, 1 - p)
                if then:
                    xc_transpose(r, n + 1, 1 - p)
                if now:
                    scores(n, 2, p)
                if out:
                    pv(n - 11, 0)
                    p_transpose(n - 11, 2, 1 - p)
                if now:
                    scores(n, 3, p)
                if then:
                    qkv(n + 1)
                if late_out:
                    o_transpose(n - 12)
                if out:
                    pv(n - 11, 1)
                    p_transpose(n - 11, 3, 1 - p)

            def mlp(r):
                pe.wait_ge(feat_ready, 2 * GROUP * r + 2 * GROUP)
                for f in range(3):
                    last = mm(BT[0:64, 0:128], w1s[:, f, :], FEAT[:, f, :], start=(f == 0), stop=(f == 2))
                last.then_inc(mlp_ps, 1)
                pe.wait_ge(mlp_act, 3 * r + 1)
                mm(BT[:, 128:256], w2p[:], h1[:], start=True, stop=True).then_inc(mlp_ps, 1)
                pe.wait_ge(mlp_act, 3 * r + 2)
                mm(BT[:, 256:384], w3r[:], h2[:], start=True, stop=True).then_inc(mlp_ps, 1)

            rounds(pe, step, mlp)


def expert_ffn(nc, psum, X, ST, MEAN, RSTD, dram, out_dram):
    E8, F, R = 8, 512, 16
    FC = F // 128
    NB = 2
    G = B // NB
    NT = NB * T
    UNITS = E8 * 2
    RING = 4
    K3 = 3 * 2 * R
    ctx = ExitStack()
    with ctx:
        def sb(name, shape, dt=F32):
            return ctx.enter_context(nc.sbuf_tensor("ff_" + name, shape, dt))

        def sem(name):
            return ctx.enter_context(nc.semaphore("ff_" + name))

        W = [[sb(f"w{n}{part}", [C, F], F32R) for part in ("hi", "lo")] for n in (1, 3)]
        A = [[sb(f"a{n}{part}", [C, E8 * R], F32R) for part in ("hi", "lo")] for n in (1, 3)]
        BB = [sb(f"b{n}", [K3, E8, F], F32R) for n in (1, 3)]
        W2 = [sb(f"w2{part}", [128, E8, FC, C], F32R) for part in ("hi", "lo")]
        pick = [sb(f"pick{part}", [E8 * R, E8, K3], F32R) for part in ("hi", "lo")]
        select = sb("select", [2 * E8, E8, 128], F32R)
        ident = sb("ident", [128, 128])
        gw = sb("gw", [C, E8])
        tri = sb("tri", [128, E8, E8])

        prep = ExitStack()
        with prep:
            def psb(name, shape, dt=F32):
                return prep.enter_context(nc.sbuf_tensor("fp_" + name, shape, dt))

            def psem(name):
                return prep.enter_context(nc.semaphore("fp_" + name))

            w32 = [psb("w1", [C, F]), psb("w3", [C, F])]
            a32 = [psb("a1", [C, E8 * R]), psb("a3", [C, E8 * R])]
            stage = psb("stage", [K3, E8, F])
            sign2 = psb("sign2", [K3, 1])
            wd = psb("wd", [128, FC, C])
            A2, B2 = psb("A2", [R, E8, F]), psb("B2", [R, E8, C])
            pick32 = psb("pick32", [E8 * R, E8, K3])
            select32 = psb("select32", [2 * E8, E8, 128])
            full = psb("full", [128, 2, F])
            loaded = psem("loaded")
            picks_loaded = [psem("picks_loaded0"), psem("picks_loaded1")]
            rest_loaded = psem("rest_loaded")
            sign_loaded = psem("sign_loaded")
            zeroed = psem("zeroed")
            staged = [psem("staged0"), psem("staged1")]
            hi_done = psem("hi_done")
            lo_done = psem("lo_done")
            copied = psem("copied")
            b_hi = psem("b_hi")
            b_lo = psem("b_lo")
            product = psem("product")
            summed = psem("summed")
            w2_hi = psem("w2_hi")
            w2_lo = psem("w2_lo")
            block = prep.enter_context(nc.Block())

            def load_b(sp, n, name):
                for row in range(0, K3, 2 * R):
                    sp.dma_start(stage[row:row + R], dram[name]).then_inc(staged[n], 16)
                    sp.dma_start(stage[row + R:row + 2 * R, 1:E8], dram[name][:, 0:E8 - 1]).then_inc(staged[n], 16)
                need(sp, copied, n)
                sp.dma_start(pick32[:], dram["pick" + ("hi", "lo")[n]]).then_inc(picks_loaded[n], 16)

            @block.sync
            def _(sp):
                sp.dma_start(sign2[:], dram["sign2"]).then_inc(sign_loaded, 16)
                sp.wait_ge(zeroed, 1)
                load_b(sp, 0, "L0_ffn_B1")
                rest = [(A2, "L0_ffn_A2"), (B2, "L0_ffn_B2"), (select32, "select"), (ident, "ident"),
                        (gw, "L0_ffn_gate_w"), (tri, "tri")]
                for tile, name in rest:
                    sp.dma_start(tile[:], dram[name]).then_inc(rest_loaded, 16)
                sp.dma_start(wd[:], dram["L0_ffn_w_down"].rearrange("(c f) d -> f c d", f=128)).then_inc(rest_loaded, 16)
                for tile, name in ((w32[0], "L0_ffn_w_gate"), (w32[1], "L0_ffn_w_up"), (a32[0], "L0_ffn_A1"),
                                   (a32[1], "L0_ffn_A3")):
                    sp.dma_start(tile[:], dram[name]).then_inc(loaded, 16)
                sp.wait_ge(b_lo, 1)
                sp.wait_ge(b_hi, 1)
                load_b(sp, 1, "L0_ffn_B3")

            REST_LOADED = 16 * 7

            @block.tensor
            def _(pe):
                pe.wait_ge(rest_loaded, REST_LOADED)
                for e in range(E8):
                    for c in range(FC):
                        last = nc.tensor.matmul(psum[e][:, c * C:(c + 1) * C], A2[:, e, c * 128:(c + 1) * 128],
                                                B2[:, e, :], start=True, stop=True)
                    last.then_inc(product, 1)

            @block.gpsimd
            def _(pool):
                nc.gpsimd.memset(stage[:, 0, :], 0.0).then_inc(zeroed, 1)
                for e in range(E8):
                    pool.wait_ge(w2_hi, e + 1)
                    nc.gpsimd.tensor_tensor(W2[1][:, e].rearrange("f c d -> f (c d)"), full[:, e % 2, :],
                                            W2[0][:, e].rearrange("f c d -> f (c d)").bitcast(F32),
                                            ALU.subtract).then_inc(w2_lo, 1)

            @block.vector
            def _(dve):
                def b_lower(n):
                    low = slice(K3 - 2 * R, K3)
                    dve.wait_ge(b_hi, n + 1)
                    nc.vector.scalar_tensor_tensor(BB[n][low], stage[low], sign2[low], BB[n][low].bitcast(F32),
                                                   ALU.mult, ALU.subtract).then_inc(b_lo, 1)
                    dve.wait_ge(picks_loaded[n], 16)
                    nc.vector.tensor_copy(pick[n][:], pick32[:]).then_inc(copied, 1)

                dve.wait_ge(sign_loaded, 16)
                b_lower(0)
                dve.wait_ge(rest_loaded, REST_LOADED)
                nc.vector.tensor_copy(select[:], select32[:])
                for e in range(E8):
                    dve.wait_ge(product, e + 1)
                    need(dve, w2_hi, e - 1)
                    need(dve, w2_lo, e - 1)
                    nc.vector.scalar_tensor_tensor(full[:, e % 2, :], psum[e][:], 2.0,
                                                   wd[:].rearrange("f c d -> f (c d)"), ALU.mult,
                                                   ALU.add).then_inc(summed, 1)
                    if e >= 4:
                        n, m = divmod(e - 4, 2)
                        x32, parts = ((w32[n], W[n]), (a32[n], A[n]))[m]
                        dve.wait_ge(hi_done, 2 * n + m + 1)
                        nc.vector.tensor_tensor(parts[1][:], x32[:], parts[0][:].bitcast(F32),
                                                ALU.subtract).then_inc(lo_done, 1)
                b_lower(1)

            @block.scalar
            def _(act):
                def b_higher(n):
                    act.wait_ge(staged[n], 96)
                    nc.scalar.activation(BB[n][:], stage[:], ACT.Copy, scale=sign2[:]).then_inc(b_hi, 1)

                act.wait_ge(sign_loaded, 16)
                b_higher(0)
                act.wait_ge(loaded, 64)
                for n in range(2):
                    for x32, parts in ((w32[n], W[n]), (a32[n], A[n])):
                        nc.scalar.copy(parts[0][:], x32[:]).then_inc(hi_done, 1)
                for e in range(E8):
                    act.wait_ge(summed, e + 1)
                    nc.scalar.copy(W2[0][:, e].rearrange("f c d -> f (c d)"), full[:, e % 2, :]).then_inc(w2_hi, 1)
                b_higher(1)

        xn = sb("xn", [128, NB, C])
        xT = sb("xT", [C, NT])
        XX = [sb("XH", [C, 2, NT], F32R), sb("XL", [C, 2, NT], F32R)]
        AA = [sb("AH", [E8 * R, 2, 2 * NT], F32R), sb("AL", [E8 * R, 2, 2 * NT], F32R)]
        STK = sb("STK", [K3, RING, 2 * NT], F32R)
        mx = sb("mx", [128, NB])
        lg = sb("lg", [128, NB, E8])
        above = sb("above", [128, NB, E8, E8])
        equal = sb("equal", [128, NB, E8, E8])
        rank = sb("rank", [128, NB, E8])
        second = sb("second", [128, NB, E8])
        mx2 = sb("mx2", [128, NB])
        wt = sb("wt", [128, NB, E8])
        th = sb("th", [128, NB, E8])
        whl = sb("whl", [128, NB, 2 * E8], F32R)
        WT = sb("WT", [2 * E8, 2, NT], F32R)
        WB = sb("WB", [128, RING, NT])
        SG = sb("SG", [128, 2, 2 * NT])
        GU = sb("GU", [128, 2, 2 * NT])
        GW = sb("GW", [128, 4, 2 * NT])
        GG = [sb("GH", [128, 4, 2 * NT], F32R), sb("GL", [128, 4, 2 * NT], F32R)]
        YS = sb("YS", [C, NT])

        xn_ready = sem("xn_ready")
        xT_ps = sem("xT_ps")
        xT_sb = sem("xT_sb")
        xh_ready = sem("xh_ready")
        xl_ready = sem("xl_ready")
        logits_ps = sem("logits_ps")
        a_ps = sem("a_ps")
        ah_done = sem("ah_done")
        al_done = sem("al_done")
        th_ready = sem("th_ready")
        wT_ps = sem("wT_ps")
        wT_ready = sem("wT_ready")
        ys_done = sem("ys_done")
        back_ps = sem("back_ps")
        x_done = sem("x_done")
        stored = sem("stored")
        route = sem("route")
        ROUTE = 13
        stk_ps = sem("stk_ps")
        stk_done = sem("stk_done")
        wb_ps = sem("wb_ps")
        wb_done = sem("wb_done")
        up_ps = sem("up_ps")
        silu_done = sem("silu_done")
        gu_done = sem("gu_done")
        gw_done = sem("gw_done")
        gh_done = sem("gh_done")
        gl_done = sem("gl_done")
        y_ps = sem("y_ps")

        H1, H3, Y, BF, BS, BW = psum[0:2], psum[2:4], psum[4], psum[5], psum[6], psum[7]

        def groups(eng, first, step, end):
            first()
            step(0, 0, True)
            step(1, 1, True)
            with eng.Fori(1, G // 2 - 1) as i:
                step(2 * i, 0, True)
                step(2 * i + 1, 1, True)
            step(G - 2, 0, True)
            step(G - 1, 1, False)
            end()

        def began(g, k):
            return k >= 0 or not isinstance(g, int) or g > 0

        def ahead(g, e, p, nxt, n):
            if e + n < E8:
                return g, e + n, p
            return (g + 1, e + n - E8, 1 - p) if nxt else None

        block = ctx.enter_context(nc.Block())

        @block.sync
        def _(sp):
            with sp.Fori(0, G) as g:
                sp.wait_ge(x_done, g + 1)
                for n in range(NB):
                    b = NB * g + n
                    sp.dma_start(out_dram[bass.ds(b, 1)].rearrange("b t c -> (b t) c"),
                                 X[:, bass.ds(b * C, C)]).then_inc(stored, 16)
            sp.wait_ge(stored, 16 * B)

        @block.gpsimd
        def _(pool):
            def step(g, p, nxt):
                for k in range(UNITS):
                    e = k // 2
                    pool.wait_ge(gu_done, UNITS * g + k + 1)
                    pool.wait_ge(wb_done, E8 * g + e + 1)
                    need(pool, gl_done, UNITS * g + k - 3)
                    halves = lambda t: t.rearrange("f (c n) -> f c n", c=2)
                    nc.gpsimd.tensor_tensor(halves(GW[:, k % 4, :]), halves(GU[:, k % 2, :]),
                                            WB[:, e % RING, :].unsqueeze(1).to_broadcast([128, 2, NT]),
                                            ALU.mult).then_inc(gw_done, 1)

            groups(pool, lambda: None, step, lambda: None)

        @block.scalar
        def _(act):
            def input_T(g, p):
                act.wait_ge(xT_ps, g + 1)
                need(act, logits_ps, g)
                nc.scalar.copy(xT[:], BF[:, 0:NT]).then_inc(xT_sb, 1)
                act.wait_ge(xT_sb, g + 1)
                need(act, xl_ready, g)
                need(act, up_ps, UNITS * (g - 2) + 2)
                nc.scalar.copy(XX[0][:, p, :], xT[:]).then_inc(xh_ready, 1)

            def a_hi(g, p):
                act.wait_ge(a_ps, g + 1)
                need(act, stk_ps, E8 * (g - 1))
                nc.scalar.copy(AA[0][:, p, :], BS[:]).then_inc(ah_done, 1)

            def gate_odds(g):
                act.wait_ge(route, ROUTE * g + 10)
                nc.scalar.activation(th[:], wt[:], ACT.Tanh, scale=0.5).then_inc(th_ready, 1)

            def weights_T(g, p):
                act.wait_ge(wT_ps, g + 1)
                need(act, wb_ps, E8 * (g - 1))
                nc.scalar.copy(WT[:, p, :], BF[0:2 * E8, 0:NT]).then_inc(wT_ready, 1)

            def weight(g, e):
                act.wait_ge(wb_ps, E8 * g + e + 1)
                need(act, gw_done, UNITS * g + 2 * (e - RING) + 2)
                nc.scalar.copy(WB[:, e % RING, :], BW[:, 0:NT]).then_inc(wb_done, 1)

            def stack(g, e):
                act.wait_ge(stk_ps, E8 * g + e + 1)
                need(act, up_ps, UNITS * g + 2 * (e - RING) + 2)
                nc.scalar.copy(STK[:, e % RING, :], BS[0:K3, :]).then_inc(stk_done, 1)

            def silu(g, k):
                act.wait_ge(up_ps, UNITS * g + k + 1)
                need(act, gu_done, UNITS * g + k - 1)
                nc.scalar.activation(SG[:, k % 2, :], H1[k % 2][:], ACT.Silu).then_inc(silu_done, 1)

            def g_hi(g, k):
                if began(g, k):
                    act.wait_ge(gw_done, UNITS * g + k + 1)
                    need(act, y_ps, UNITS * g + k - 3)
                    nc.scalar.copy(GG[0][:, k % 4, :], GW[:, k % 4, :]).then_inc(gh_done, 1)

            def y_copy(g):
                act.wait_ge(y_ps, UNITS * (g + 1))
                need(act, back_ps, g)
                nc.scalar.copy(YS[:], Y[:, 0:NT]).then_inc(ys_done, 1)

            def step(g, p, nxt):
                for e in range(E8):
                    silu(g, 2 * e)
                    g_hi(g, 2 * e - 2)
                    if nxt and e == 5:
                        stack(g, 6)
                    if nxt and e == 7:
                        weights_T(g + 1, 1 - p)
                    silu(g, 2 * e + 1)
                    if nxt and e == 4:
                        a_hi(g + 1, 1 - p)
                    g_hi(g, 2 * e - 1)
                    if e == 1 and began(g, -1):
                        y_copy(g - 1)
                    later, following = ahead(g, e, p, nxt, 2), ahead(g, e, p, nxt, 1)
                    if later and not (nxt and e == 4):
                        stack(later[0], later[1])
                    if following:
                        weight(following[0], following[1])
                    if nxt and e == 1:
                        input_T(g + 1, 1 - p)
                    if nxt and e == 5:
                        gate_odds(g + 1)

            def first():
                input_T(0, 0)
                a_hi(0, 0)
                gate_odds(0)
                weights_T(0, 0)
                stack(0, 0)
                weight(0, 0)
                stack(0, 1)

            def end():
                g_hi(G, -2)
                g_hi(G, -1)
                y_copy(G - 1)

            groups(act, first, step, end)

        @block.vector
        def _(dve):
            def normalise(g):
                need(dve, xT_ps, g)
                for n in range(NB):
                    b = g * NB + n
                    last = nc.vector.tensor_scalar(xn[:, n, :], X[:, bass.ds(b * C, C)], MEAN[:, bass.ds(b, 1)],
                                                   RSTD[:, bass.ds(b, 1)], ALU.subtract, ALU.mult)
                last.then_inc(xn_ready, 1)

            def x_lo(g, p):
                dve.wait_ge(xh_ready, g + 1)
                nc.vector.tensor_tensor(XX[1][:, p, :], xT[:], XX[0][:, p, :].bitcast(F32), ALU.subtract).then_inc(xl_ready, 1)

            def a_lo(g, p):
                dve.wait_ge(ah_done, g + 1)
                nc.vector.tensor_tensor(AA[1][:, p, :], BS[:], AA[0][:, p, :].bitcast(F32), ALU.subtract).then_inc(al_done, 1)

            def route_a(g):
                at = ROUTE * g
                dve.wait_ge(logits_ps, g + 1)
                l3 = BF[:, 0:NB * E8].rearrange("n (b e) -> n b e", e=E8)
                nc.vector.tensor_reduce(mx[:], l3, AX.X, ALU.max).then_inc(route, 1)
                dve.wait_ge(route, at + 1)
                nc.vector.tensor_tensor(lg[:], l3, mx[:].unsqueeze(2).to_broadcast([128, NB, E8]),
                                        ALU.subtract).then_inc(route, 1)
                dve.wait_ge(route, at + 2)
                for n in range(NB):
                    own = lg[:, n, :].unsqueeze(2).to_broadcast([128, E8, E8])
                    other = lg[:, n, :].unsqueeze(1).to_broadcast([128, E8, E8])
                    nc.vector.tensor_tensor(above[:, n], other, own, ALU.is_gt)
                    last = nc.vector.tensor_tensor(equal[:, n], other, own, ALU.is_equal)
                last.then_inc(route, 1)

            def route_b(g):
                at = ROUTE * g
                dve.wait_ge(route, at + 3)
                eq = equal[:].rearrange("n b e j -> n b (e j)")
                nc.vector.tensor_tensor(eq, eq, tri[:].rearrange("n e j -> n (e j)").unsqueeze(1)
                                        .to_broadcast([128, NB, E8 * E8]), ALU.mult).then_inc(route, 1)
                dve.wait_ge(route, at + 4)
                nc.vector.tensor_tensor(above[:], above[:], equal[:], ALU.add).then_inc(route, 1)
                dve.wait_ge(route, at + 5)
                nc.vector.tensor_reduce(rank[:], above[:], AX.X, ALU.add).then_inc(route, 1)

            def route_c(g):
                at = ROUTE * g
                dve.wait_ge(route, at + 6)
                nc.vector.scalar_tensor_tensor(second[:], rank[:], 1.0, lg[:], ALU.is_equal, ALU.mult).then_inc(route, 1)
                dve.wait_ge(route, at + 7)
                nc.vector.tensor_reduce(mx2[:], second[:], AX.X, ALU.add).then_inc(route, 1)
                dve.wait_ge(route, at + 8)
                nc.vector.tensor_scalar(second[:], lg[:], 2.0, None, ALU.mult).then_inc(route, 1)
                dve.wait_ge(route, at + 9)
                nc.vector.tensor_tensor(wt[:], second[:], mx2[:].unsqueeze(2).to_broadcast([128, NB, E8]),
                                        ALU.subtract).then_inc(route, 1)

            def route_d(g):
                at = ROUTE * g
                dve.wait_ge(th_ready, g + 1)
                nc.vector.tensor_scalar(th[:], th[:], 0.5, 0.5, ALU.mult, ALU.add).then_inc(route, 1)
                dve.wait_ge(route, at + 11)
                need(dve, wT_ps, g)
                nc.vector.scalar_tensor_tensor(wt[:], rank[:], 2.0, th[:], ALU.is_lt, ALU.mult)
                nc.vector.scalar_tensor_tensor(whl[:, :, 0:E8], rank[:], 2.0, th[:], ALU.is_lt, ALU.mult).then_inc(route, 1)
                dve.wait_ge(route, at + 12)
                nc.vector.tensor_tensor(whl[:, :, E8:2 * E8], wt[:], whl[:, :, 0:E8].bitcast(F32),
                                        ALU.subtract).then_inc(route, 1)

            def gated(g, k):
                dve.wait_ge(silu_done, UNITS * g + k + 1)
                need(dve, gw_done, UNITS * g + k - 1)
                nc.vector.tensor_tensor(GU[:, k % 2, :], SG[:, k % 2, :], H3[k % 2][:], ALU.mult).then_inc(gu_done, 1)

            def g_lo(g, k):
                if began(g, k):
                    dve.wait_ge(gh_done, UNITS * g + k + 1)
                    nc.vector.tensor_tensor(GG[1][:, k % 4, :], GW[:, k % 4, :], GG[0][:, k % 4, :].bitcast(F32),
                                            ALU.subtract).then_inc(gl_done, 1)

            def residual(g):
                dve.wait_ge(back_ps, g + 1)
                xg = X[:, bass.ds(g * (NB * C), NB * C)]
                nc.vector.tensor_tensor(xg, xg, BF[:, 0:NB * C], ALU.add).then_inc(x_done, 1)

            def step(g, p, nxt):
                for e in range(E8):
                    gated(g, 2 * e)
                    g_lo(g, 2 * e - 2)
                    if nxt and e == 4:
                        route_a(g + 1)
                    if nxt and e == 5:
                        route_c(g + 1)
                    if nxt and e == 6:
                        route_d(g + 1)
                    gated(g, 2 * e + 1)
                    if nxt and e == 4:
                        a_lo(g + 1, 1 - p)
                    g_lo(g, 2 * e - 1)
                    if nxt and e == 0:
                        normalise(g + 1)
                    if nxt and e == 2:
                        x_lo(g + 1, 1 - p)
                    if e == 2 and began(g, -1):
                        residual(g - 1)
                    if nxt and e == 4:
                        route_b(g + 1)

            def first():
                normalise(0)
                x_lo(0, 0)
                a_lo(0, 0)
                route_a(0)
                route_b(0)
                route_c(0)
                route_d(0)

            def end():
                g_lo(G, -2)
                g_lo(G, -1)
                residual(G - 1)
                dve.wait_ge(x_done, G)

            groups(dve, first, step, end)

        @block.tensor
        def _(pe):
            mm, tr = nc.tensor.matmul, nc.tensor.transpose

            def three(out, w, x, start, stop, **kw):
                mm(out, w[0], x[0], start=start, stop=False, **kw)
                mm(out, w[0], x[1], start=False, stop=False, **kw)
                return mm(out, w[1], x[0], start=False, stop=stop, **kw)

            def input_T(g):
                pe.wait_ge(xn_ready, g + 1)
                need(pe, wT_ready, g)
                for n in range(NB):
                    last = tr(BF[:, n * T:(n + 1) * T], xn[:, n, :], ident[:])
                last.then_inc(xT_ps, 1)

            def logits(g):
                pe.wait_ge(xT_sb, g + 1)
                if began(g, -1):
                    need(pe, x_done, g - 1)
                for n in range(NB):
                    last = mm(BF[:, n * E8:(n + 1) * E8], xT[:, n * T:(n + 1) * T], gw[:], start=True, stop=True)
                last.then_inc(logits_ps, 1)

            def a_products(g, p):
                pe.wait_ge(xh_ready, g + 1)
                pe.wait_ge(xl_ready, g + 1)
                need(pe, stk_done, E8 * g - 2)
                for n in range(2):
                    last = three(BS[:, n * NT:(n + 1) * NT], [t[:] for t in A[n]], [t[:, p, :] for t in XX], True, True)
                last.then_inc(a_ps, 1)

            def weights_T(g):
                pe.wait_ge(route, ROUTE * g + ROUTE)
                for n in range(NB):
                    last = tr(BF[0:2 * E8, n * T:(n + 1) * T], whl[:, n, :].bitcast(F32), ident[:])
                last.then_inc(wT_ps, 1)

            def weight(g, e, p):
                pe.wait_ge(wT_ready, g + 1)
                need(pe, wb_done, E8 * g + e)
                mm(BW[:, 0:NT], select[:, e, :], WT[:, p, :], start=True, stop=True).then_inc(wb_ps, 1)

            def stack(g, e, p):
                pe.wait_ge(al_done, g + 1)
                need(pe, stk_done, E8 * g + e)
                for n in range(2):
                    cols = slice(n * NT, (n + 1) * NT)
                    mm(BS[0:K3, cols], pick[0][:, e, :], AA[0][:, p, cols], start=True, stop=False)
                    last = mm(BS[0:K3, cols], pick[1][:, e, :], AA[1][:, p, cols], start=False, stop=True)
                last.then_inc(stk_ps, 1)

            def up(g, k, p):
                e, u = divmod(k, 2)
                if k == 0:
                    pe.wait_ge(xh_ready, g + 1)
                    pe.wait_ge(xl_ready, g + 1)
                if u == 0:
                    pe.wait_ge(stk_done, E8 * g + e + 1)
                for n, (H, read) in enumerate(((H1, silu_done), (H3, gu_done))):
                    need(pe, read, UNITS * g + k - 1)
                    for c in range(2):
                        out = H[u][:, c * NT:(c + 1) * NT]
                        f = slice((2 * u + c) * 128, (2 * u + c + 1) * 128)
                        if e == 0:
                            three(out, [t[:, f] for t in W[n]], [t[:, p, :] for t in XX], c == 0, False,
                                  skip_group_check=True)
                        last = mm(out, BB[n][:, e, f], STK[:, e % RING, n * NT:(n + 1) * NT], start=False,
                                  stop=(e == E8 - 1 and c == 1), skip_group_check=True)
                last.then_inc(up_ps, 1)

            def down(g, k):
                if not began(g, k):
                    return
                e, u = divmod(k % UNITS, 2)
                out = Y[:, 0:NT]
                pe.wait_ge(gl_done, UNITS * g + k + 1)
                if k == 0:
                    need(pe, ys_done, g)
                for c in range(2):
                    chunk = 2 * u + c
                    cols = slice(c * NT, (c + 1) * NT)
                    last = three(out, [t[:, e, chunk, :] for t in W2], [t[:, k % 4, cols] for t in GG],
                                 k == 0 and c == 0, k % UNITS == UNITS - 1 and c == 1)
                last.then_inc(y_ps, 1)

            def back(g):
                pe.wait_ge(ys_done, g + 1)
                for n in range(NB):
                    last = tr(BF[:, n * T:(n + 1) * T], YS[:, n * T:(n + 1) * T], ident[:])
                last.then_inc(back_ps, 1)

            def step(g, p, nxt):
                for e in range(E8):
                    up(g, 2 * e, p)
                    down(g, 2 * e - 4)
                    if nxt and e == 1:
                        input_T(g + 1)
                    if nxt and e == 4:
                        a_products(g + 1, 1 - p)
                    if nxt and e == 5:
                        pe.wait_ge(al_done, g + 2)
                        stack(g, 6, p)
                    up(g, 2 * e + 1, p)
                    down(g, 2 * e - 3)
                    later, following = ahead(g, e, p, nxt, 2), ahead(g, e, p, nxt, 1)
                    if later and not (nxt and e == 4):
                        stack(*later)
                    if following:
                        weight(*following)
                    if e == 2 and began(g, -1):
                        if nxt:
                            pe.wait_ge(xT_sb, g + 2)
                        back(g - 1)
                    if nxt and e == 3:
                        logits(g + 1)
                    if nxt and e == 6:
                        weights_T(g + 1)

            def first():
                input_T(0)
                logits(0)
                a_products(0, 0)
                weights_T(0)
                stack(0, 0, 0)
                stack(0, 1, 0)
                weight(0, 0, 0)

            def end():
                down(G, -4)
                down(G, -3)
                down(G, -2)
                down(G, -1)
                back(G - 1)

            groups(pe, first, step, end)


def program(nc, dram, out):
    ctx = ExitStack()
    with ctx:
        X = ctx.enter_context(nc.sbuf_tensor("X", [T, B * C], F32))
        psum = [ctx.enter_context(nc.psum_tensor(f"bank{n}", [128, 512], F32)) for n in range(8)]
        ST = ctx.enter_context(nc.sbuf_tensor("ST", [T, 6 * B], F32))
        MEAN = ctx.enter_context(nc.sbuf_tensor("MEAN", [T, B], F32))
        RSTD = ctx.enter_context(nc.sbuf_tensor("RSTD", [T, B], F32))
        attentions = ExitStack()
        with attentions:
            self_const, self_loaded = constant_tiles(nc, attentions, "sc", SELF_CONSTANTS)
            cross_const, cross_loaded = constant_tiles(nc, attentions, "xc", CROSS_CONSTANTS)

            def load_more(sp):
                load_constants(sp, self_const, self_loaded, SELF_CONSTANTS, dram)
                load_constants(sp, cross_const, cross_loaded, CROSS_CONSTANTS, dram)

            inverse_std(nc, "ln1", X, ST, MEAN, RSTD, dram["x"], load_more)
            self_attention(nc, psum, X, ST, MEAN, RSTD, self_const, self_loaded)
            inverse_std(nc, "ln2", X, ST, MEAN, RSTD, None)
            cross_attention(nc, psum, X, ST, MEAN, RSTD, cross_const, cross_loaded, dram)
        inverse_std(nc, "ln3", X, ST, MEAN, RSTD, None)
        expert_ffn(nc, psum, X, ST, MEAN, RSTD, dram, out)


def kernel(**inputs):
    import numpy as np
    import concourse.bacc as bacc
    from concourse import mybir as mb
    from concourse.bass_utils import run_bass_kernel_spmd

    nc = bacc.Bacc("TRN2", target_bir_lowering=False, num_devices=1)
    arrays = {k: np.ascontiguousarray(v) for k, v in inputs.items()}
    for name, order in (("L0_xattn_Wq", (1, 0)), ("L0_xattn_Wk", (1, 0)), ("L0_xattn_Wv", (1, 0)),
                        ("L0_xattn_Wo", (1, 0)), ("L0_xattn_w1", (1, 0)), ("L0_xattn_w2", (1, 0)),
                        ("L0_xattn_w3", (1, 0)), ("L0_ffn_gate_w", (1, 0)), ("L0_ffn_w_gate", (1, 0)),
                        ("L0_ffn_w_up", (1, 0)), ("L0_ffn_w_down", (1, 0)), ("L0_ffn_A1", (2, 0, 1)),
                        ("L0_ffn_A3", (2, 0, 1)), ("L0_ffn_A2", (1, 0, 2)), ("L0_ffn_B1", (2, 0, 1)),
                        ("L0_ffn_B3", (2, 0, 1)), ("L0_ffn_B2", (2, 0, 1))):
        arrays[name] = np.ascontiguousarray(arrays[name].transpose(order))
    for name in ("L0_ffn_A1", "L0_ffn_A3"):
        arrays[name] = arrays[name].reshape(C, -1)
    for name in [n for n, a in arrays.items() if a.ndim == 1]:
        as_column = name in ("L0_xattn_bq", "L0_xattn_bk", "L0_xattn_b1", "L0_xattn_b2")
        arrays[name] = arrays[name].reshape(-1, 1) if as_column else arrays[name].reshape(1, -1)
    eye = np.eye(128, dtype=np.float32)
    bf16, f16 = mb.dt.np(mb.dt.bfloat16), np.float16
    inv_freq = 1.0 / 10000.0 ** (np.arange(DK // 2, dtype=np.float32) / (DK // 2))
    angle = np.arange(T, dtype=np.float32)[:, None] * inv_freq.astype(np.float32)[None]
    per_head = lambda a: np.tile(np.repeat(a, 2, axis=1), (1, H))
    sign = np.tile(np.array([-1.0, 1.0]), C // 2)
    scale = DK ** -0.5
    cos, sin = per_head(np.cos(angle)), per_head(np.sin(angle)) * sign
    experts, rank = 8, 16
    pick = np.zeros((2, experts * rank, experts, 3, 2, rank), np.float32)
    for e in range(experts):
        for r in range(rank):
            for part, third in ((0, 0), (1, 1), (0, 2)):
                pick[part, rank * e + r, e, third, 0, r] = 1.0
                if e:
                    pick[part, rank * (e - 1) + r, e, third, 1, r] = 1.0
    pick = pick.reshape(2, experts * rank, experts, 6 * rank)
    arrays.update(
        pickhi=np.ascontiguousarray(pick[0]), picklo=np.ascontiguousarray(pick[1]),
        sign2=np.tile(np.repeat(np.array([2.0, -2.0], np.float32), rank), 3)[:, None].copy(),
        ident=eye, identb=eye.astype(bf16), ident16=eye.astype(f16),
        causal=np.tile(np.where(np.tril(np.ones((T, T), bool)), 0.0, -1e30), (1, JH)).astype(bf16),
        tri=np.ascontiguousarray(np.broadcast_to(np.tril(np.ones((8, 8), np.float32), -1), (128, 8, 8))),
        select=np.repeat(np.tile(np.eye(8, dtype=np.float32), (2, 1))[:, :, None], 128, axis=2),
        headsel=(np.arange(128)[:, None] // DK == np.arange(H)[None]).astype(np.float32),
        headmask=(np.arange(128)[:, None] // DK % JH == np.arange(JH)[None]).astype(np.float32),
        cos=np.concatenate([cos * scale, cos], 1).astype(np.float32),
        sin=np.concatenate([sin * scale, sin], 1).astype(np.float32),
    )
    dram = {n: nc.dram_tensor(n, a.shape, mb.dt.from_np(a.dtype), kind="ExternalInput").ap() for n, a in arrays.items()}
    out = nc.dram_tensor("out", (B, T, C), mb.dt.float32, kind="ExternalOutput").ap()
    program(nc, dram, out)
    r = run_bass_kernel_spmd(nc, [arrays], core_ids=[0])
    return r.results[0]["out"]
```
